# Optimizing a Trainium2 kernel written in Bass

```python
import numpy as np
import jax
import jax.numpy as jnp

def _softmax(x, axis=-1):
    return jax.nn.softmax(x, axis=axis)

def _gelu(x):
    return jax.nn.gelu(x, approximate=True)

def _silu(x):
    return jax.nn.silu(x)

def _sigmoid(x):
    return jax.nn.sigmoid(x)

def _layernorm(x, axis=-1, eps=1e-05):
    m = jnp.mean(x, axis=axis, keepdims=True)
    v = jnp.var(x, axis=axis, keepdims=True)
    return (x - m) / jnp.sqrt(v + eps)

def _scatter_add(tgt, idx, src, axis=0):
    return tgt.at[idx].add(src)

def _segment_sum(src, seg, n):
    return jax.ops.segment_sum(src, seg, n)
kernel_name = 'mk_adj_resnorm_d4_adj_r2_507b81'

def setup_inputs(seed: int=0):
    np.random.seed(seed)
    _w = jnp.asarray

    def _rec_inputs():
        import jax
        import jax.numpy as jnp
        _gk = jax.random.key(seed)
        x = -0.000929 + 1 * jax.random.normal(jax.random.fold_in(_gk, 1), (8, 1024, 64), jnp.float32)
        _a = jax.random.bernoulli(jax.random.fold_in(_gk, 2), 0.00195312, (1024, 1024))
        _a = jnp.logical_or(_a, jnp.eye(1024, dtype=bool))
        _af = _a.astype(jnp.float32)
        adj = _af
        return (x, adj)
    x, adj = _rec_inputs()

    def _L0_gnn_setup():
        import jax, jax.numpy as jnp
        import numpy as np
        NEG = -1000000000.0
        key = jax.random.key(seed)
        ks = jax.random.split(key, 14)
        B, N, E, NF, NH = (8, 1024, 64, 64, 64)
        x = jax.random.normal(ks[0], (B, N, NF), dtype=jnp.float32)
        base = jax.nn.one_hot(jax.random.randint(ks[1], (N,), 0, E), E, dtype=jnp.float32)
        extra = (jax.random.uniform(ks[2], (N, E)) < 0.03).astype(jnp.float32)
        H = jnp.clip(base + extra, 0.0, 1.0)
        adj = (jax.random.uniform(ks[3], (N, N)) < 0.01).astype(jnp.float32)
        adj = jnp.clip(adj + jnp.eye(N, dtype=jnp.float32), 0.0, 1.0)
        s_in = 1.0 / np.sqrt(NF)
        s_h = 1.0 / np.sqrt(NH)
        W = jax.random.normal(ks[4], (NF, NH), dtype=jnp.float32) * s_in
        W_ind = jax.random.normal(ks[5], (NF, NH), dtype=jnp.float32) * s_in
        a_node = jax.random.normal(ks[6], (NH,), dtype=jnp.float32) * s_h
        a_gn = jax.random.normal(ks[7], (NH,), dtype=jnp.float32) * s_h
        a_ge = jax.random.normal(ks[8], (NH,), dtype=jnp.float32) * s_h
        fcW = jax.random.normal(ks[9], (NH, 2 * NH), dtype=jnp.float32) * s_h
        fcb = jnp.zeros((2 * NH,), dtype=jnp.float32)
        av = jax.random.normal(ks[10], (2 * NH,), dtype=jnp.float32) / np.sqrt(2 * NH)
        return {'x': x, 'H': H, 'adj': adj, 'nhid': NH, 'W': W, 'W_ind': W_ind, 'a_node': a_node, 'a_gn': a_gn, 'a_ge': a_ge, 'fcW': fcW, 'fcb': fcb, 'av': av}
    _L0_gnn_all = _L0_gnn_setup()
    _L0_gnn_in = {k: v for k, v in _L0_gnn_all.items() if k in ('H', 'W', 'W_ind', 'a_node', 'a_gn', 'a_ge', 'fcW', 'fcb', 'av')}
    del _L0_gnn_all

    def _L1_gnn_setup():
        import jax, jax.numpy as jnp
        import numpy as np
        NEG_INF = -1e+16

        def gat_layer(x, graph, W, b):
            h = x @ W
            s = jnp.einsum('bnd,bmd->bnm', h, h) * graph
            s = jnp.where(s == 0.0, NEG_INF, s)
            a = jax.nn.softmax(s, axis=2)
            return jnp.einsum('bnm,bmd->bnd', a, h) + b
        key = jax.random.key(seed)
        k1, k2, k3, k4, k5, k6 = jax.random.split(key, 6)
        B, N, C_IN, HID, HEADS, C_OUT = (16, 512, 64, 128, 8, 64)
        flow_x = jax.random.normal(k1, (B, N, C_IN), dtype=jnp.float32)
        graph = jax.random.randint(k2, (N, N), 0, 2).astype(jnp.float32)
        Wh = jax.random.normal(k3, (HEADS, C_IN, HID), dtype=jnp.float32)
        bh = jax.random.normal(k4, (HEADS, HID), dtype=jnp.float32)
        W_out = jax.random.normal(k5, (HID * HEADS, C_OUT), dtype=jnp.float32)
        b_out = jax.random.normal(k6, (C_OUT,), dtype=jnp.float32)
        return {'flow_x': flow_x, 'graph': graph, 'Wh': Wh, 'bh': bh, 'W_out': W_out, 'b_out': b_out}
    _L1_gnn_all = _L1_gnn_setup()
    _L1_gnn_in = {k: v for k, v in _L1_gnn_all.items() if k in ('Wh', 'bh', 'W_out', 'b_out')}
    del _L1_gnn_all

    def _L2_gnn_setup():
        import jax, jax.numpy as jnp
        import numpy as np
        B, N, C = (4, 2048, 64)
        ALPHA = 0.2
        THRESHOLD = 0.5
        NEG_INF = -9000000000000000.0
        key = jax.random.key(seed)
        k1, k2, k3 = jax.random.split(key, 3)
        inp = jax.random.normal(k1, (B, N, C), dtype=jnp.float32)
        adj = jax.random.uniform(k2, (N, N), dtype=jnp.float32)
        bound = 1.414 * float(np.sqrt(6.0 / (2 * C + 1)))
        a = jax.random.uniform(k3, (2 * C, 1), dtype=jnp.float32, minval=-bound, maxval=bound)
        return {'input': inp, 'adj': adj, 'a': a}
    _L2_gnn_all = _L2_gnn_setup()
    _L2_gnn_in = {k: v for k, v in _L2_gnn_all.items() if k in ('a',)}
    del _L2_gnn_all

    def _L3_gnn_setup():
        import jax, jax.numpy as jnp
        import numpy as np
        MAX_STEPS = 3
        key = jax.random.key(seed)
        ks = jax.random.split(key, 7)
        B, N, D = (1, 4096, 64)
        return {'causal_vars': jax.random.normal(ks[0], (B, N, D), dtype=jnp.float32), 'adj_matrix': jax.random.uniform(ks[1], (N, N), dtype=jnp.float32), 'intervention_value': jax.random.normal(ks[2], (B, D), dtype=jnp.float32), 'W1': jax.random.normal(ks[3], (D, 2 * D), dtype=jnp.float32) * (1.0 / np.sqrt(2 * D)), 'b1': jax.random.normal(ks[4], (D,), dtype=jnp.float32) * 0.01, 'W2': jax.random.normal(ks[5], (D, D), dtype=jnp.float32) * (1.0 / np.sqrt(D)), 'b2': jax.random.normal(ks[6], (D,), dtype=jnp.float32) * 0.01, 'intervention_idx': 0}
    _L3_gnn_all = _L3_gnn_setup()
    _L3_gnn_in = {k: v for k, v in _L3_gnn_all.items() if k in ('intervention_value', 'W1', 'b1', 'W2', 'b2')}
    del _L3_gnn_all
    return {'x': x, 'adj': adj, 'L0_gnn_H': _L0_gnn_in['H'], 'L0_gnn_W': _L0_gnn_in['W'], 'L0_gnn_W_ind': _L0_gnn_in['W_ind'], 'L0_gnn_a_node': _L0_gnn_in['a_node'], 'L0_gnn_a_gn': _L0_gnn_in['a_gn'], 'L0_gnn_a_ge': _L0_gnn_in['a_ge'], 'L0_gnn_fcW': _L0_gnn_in['fcW'], 'L0_gnn_fcb': _L0_gnn_in['fcb'], 'L0_gnn_av': _L0_gnn_in['av'], 'L1_gnn_Wh': _L1_gnn_in['Wh'], 'L1_gnn_bh': _L1_gnn_in['bh'], 'L1_gnn_W_out': _L1_gnn_in['W_out'], 'L1_gnn_b_out': _L1_gnn_in['b_out'], 'L2_gnn_a': _L2_gnn_in['a'], 'L3_gnn_intervention_value': _L3_gnn_in['intervention_value'], 'L3_gnn_W1': _L3_gnn_in['W1'], 'L3_gnn_b1': _L3_gnn_in['b1'], 'L3_gnn_W2': _L3_gnn_in['W2'], 'L3_gnn_b2': _L3_gnn_in['b2']}

def reference(x, adj, L0_gnn_H, L0_gnn_W, L0_gnn_W_ind, L0_gnn_a_node, L0_gnn_a_gn, L0_gnn_a_ge, L0_gnn_fcW, L0_gnn_fcb, L0_gnn_av, L1_gnn_Wh, L1_gnn_bh, L1_gnn_W_out, L1_gnn_b_out, L2_gnn_a, L3_gnn_intervention_value, L3_gnn_W1, L3_gnn_b1, L3_gnn_W2, L3_gnn_b2):
    import jax
    import jax.numpy as jnp

    def _L0_gnn_ref(x, H, adj, nhid, W, W_ind, a_node, a_gn, a_ge, fcW, fcb, av):
        import jax, jax.numpy as jnp
        import numpy as np
        NEG = -1000000000.0
        h = x @ W
        maskEN = H.T
        s = jax.nn.leaky_relu(h @ a_node, 0.2)
        logits = jnp.where(maskEN[None, :, :] > 0, s[:, None, :], NEG)
        alpha = jax.nn.softmax(logits, axis=-1)
        agg = jnp.einsum('ben,bnf->bef', alpha, h)
        beta = jax.nn.sigmoid((h @ a_gn)[:, None, :] + (agg @ a_ge)[:, :, None])
        all_he = beta[..., None] * h[:, None, :, :] + (1.0 - beta[..., None]) * agg[:, :, None, :]
        deg = jnp.maximum(adj.sum(-1), 1.0)[:, None]
        industry = jnp.einsum('nm,bmf->bnf', adj / deg, x @ W_ind)
        all_he = jax.nn.elu(all_he)
        he = jax.nn.elu(agg)

        def attn_scores(f):
            return jnp.tanh(f @ fcW + fcb) @ av
        se = attn_scores(he)
        logits2 = jnp.where(H[None, :, :] > 0, se[:, None, :], NEG)
        coefs1 = jax.nn.softmax(logits2, axis=-1)
        g = jnp.einsum('bne,benf->bnf', coefs1, all_he)
        pair = jnp.stack([industry, g], axis=2)
        coefs2 = jax.nn.softmax(attn_scores(pair), axis=-1)
        out = jnp.einsum('bnk,bnkf->bnf', coefs2, pair)
        return out

    def _L1_gnn_ref(flow_x, graph, Wh, bh, W_out, b_out):
        import jax, jax.numpy as jnp
        import numpy as np
        NEG_INF = -1e+16

        def gat_layer(x, graph, W, b):
            h = x @ W
            s = jnp.einsum('bnd,bmd->bnm', h, h) * graph
            s = jnp.where(s == 0.0, NEG_INF, s)
            a = jax.nn.softmax(s, axis=2)
            return jnp.einsum('bnm,bmd->bnd', a, h) + b
        heads = jax.vmap(lambda W, b: gat_layer(flow_x, graph, W, b))(Wh, bh)
        H, B, N, D = heads.shape
        cat = jnp.moveaxis(heads, 0, 2).reshape(B, N, H * D)
        x = jax.nn.leaky_relu(cat, negative_slope=0.01)
        out = gat_layer(x, graph, W_out, b_out)
        return jax.nn.leaky_relu(out, negative_slope=0.01)

    def _L2_gnn_ref(input, adj, a):
        import jax, jax.numpy as jnp
        import numpy as np
        B, N, C = (4, 2048, 64)
        ALPHA = 0.2
        THRESHOLD = 0.5
        NEG_INF = -9000000000000000.0
        h = input
        a1 = a[:C, 0]
        a2 = a[C:, 0]
        s1 = h @ a1
        s2 = h @ a2
        e = s1[:, :, None] + s2[:, None, :]
        e = jnp.where(e > 0, e, ALPHA * e)
        mask = adj[None, :, :] > THRESHOLD
        att = jnp.where(mask, e, NEG_INF)
        att = jax.nn.softmax(att, axis=2)
        h_prime = jnp.einsum('bij,bjc->bic', att, h)
        return jax.nn.elu(h_prime)

    def _L3_gnn_ref(causal_vars, adj_matrix, intervention_value, W1, b1, W2, b2, intervention_idx):
        import jax, jax.numpy as jnp
        import numpy as np
        MAX_STEPS = 3
        v = causal_vars.at[:, intervention_idx].set(intervention_value)
        for _ in range(MAX_STEPS):
            effects = jnp.einsum('nm,bmd->bnd', adj_matrix, v)
            h = jnp.concatenate([v, effects], axis=-1)
            h = jax.nn.relu(jnp.einsum('bnk,dk->bnd', h, W1) + b1)
            v = jnp.einsum('bnk,dk->bnd', h, W2) + b2
        return v
    x = _layernorm(x + _L0_gnn_ref(x, L0_gnn_H, adj, 64, L0_gnn_W, L0_gnn_W_ind, L0_gnn_a_node, L0_gnn_a_gn, L0_gnn_a_ge, L0_gnn_fcW, L0_gnn_fcb, L0_gnn_av), axis=-1)
    x = _layernorm(x + _L1_gnn_ref(x, adj, L1_gnn_Wh, L1_gnn_bh, L1_gnn_W_out, L1_gnn_b_out), axis=-1)
    x = _layernorm(x + _L2_gnn_ref(x, adj, L2_gnn_a), axis=-1)
    x = _layernorm(x + _L3_gnn_ref(x, adj, L3_gnn_intervention_value, L3_gnn_W1, L3_gnn_b1, L3_gnn_W2, L3_gnn_b2, 0), axis=-1)
    return x

_drawn_inputs = setup_inputs


def setup_inputs(seed=0):
    import zlib

    import numpy as np

    out = dict(_drawn_inputs(seed))
    spreads = {'L0_gnn_fcb': (0.0, 0.8)}
    factors = {'L0_gnn_a_ge': 6.575,
     'L1_gnn_b_out': 7.745,
     'L3_gnn_intervention_value': 14.57,
     'L3_gnn_b1': 8.0,
     'L3_gnn_b2': 5.414}
    for name, (base, spread) in spreads.items():
        noise = np.random.default_rng([zlib.crc32(name.encode()), seed]).standard_normal(out[name].shape)
        drawn = base * np.exp(spread * noise) if base else spread * noise
        out[name] = jnp.asarray(drawn.astype(out[name].dtype))
    for name, factor in factors.items():
        out[name] = (out[name] * factor).astype(out[name].dtype)
    return out
```

```python
import concourse.bass as bass
from concourse import mybir
from contextlib import ExitStack

F32 = mybir.dt.float32
F32R = mybir.dt.float32r
BF16 = mybir.dt.bfloat16
ALU = mybir.AluOpType
ACT = mybir.ActivationFunctionType
AX_X = mybir.AxisListType.X

B, N, F = 8, 1024, 64
HEADS, D = 8, 128
EDGES = 64
NT = N // 128
MASKED = -1e30
EPS = 1e-5




class Shared:
    pass


def wait(eng, sem, value):
    if not isinstance(value, int) or value > 0:
        eng.wait_ge(sem, value)


def sbuf(nc, ctx, stage):
    return lambda name, shape, dt=F32: ctx.enter_context(nc.sbuf_tensor(f"{stage}_{name}", shape, dt))


def psum(nc, ctx, stage):
    return lambda name, shape, dt=F32: ctx.enter_context(nc.psum_tensor(f"{stage}_{name}", shape, dt))


def semaphores(nc, ctx, stage):
    mine = []
    ctx.callback(lambda: (nc.all_engine_barrier(), nc.clear_and_free_semaphores(mine), nc.all_engine_barrier()))

    def new(name):
        mine.append(nc.alloc_semaphore(name=f"{stage}_{name}"))
        return mine[-1]
    return new


def one(ap):
    return ap.rearrange("o p n -> (o p) n")


def setup(nc, k, x, adj, adjT, H, HT):
    with ExitStack() as ctx:
        sb, sem = sbuf(nc, ctx, "setup"), semaphores(nc, ctx, "setup")
        raw = [sb(f"raw{i}", [128, NT, N]) for i in range(2)]
        raw_h = sb("raw_h", [128, NT, EDGES])
        raw_ht = sb("raw_ht", [EDGES, N])
        x_in, adj_in, adjT_in, h_in, ident_step, two_step = (sem(n) for n in (
            "x_in", "adj_in", "adjT_in", "h_in", "ident_step", "two_step"))
        block = ctx.enter_context(nc.Block())

        @block.sync
        def _(sp):
            sp.dma_start(raw[0][:, :, :], adj.rearrange("(t p) m -> p t m", p=128)).then_inc(adj_in, 16)
            sp.dma_start(raw_h[:, :, :], H.rearrange("(t p) e -> p t e", p=128)).then_inc(h_in, 16)
            sp.dma_start(raw_ht[:, :], HT).then_inc(h_in, 16)
            sp.dma_start(k.x[:, :, :], x.rearrange("b (t p) c -> p (b t) c", p=128)).then_inc(x_in, 16)
            sp.wait_ge(x_in, 16)

        @block.scalar
        def _(act):
            act.dma_start(raw[1][:, :, :], adjT.rearrange("(t p) n -> p t n", p=128)).then_inc(adjT_in, 16)
            act.wait_ge(adjT_in, 16)
            act.activation(k.adjT[:, :, :], raw[1][:, :, :], ACT.Copy)

        @block.gpsimd
        def _(pool):
            pool.memset(k.ident[:, :], 1.0).then_inc(ident_step, 1)
            pool.wait_ge(ident_step, 1)
            pool.affine_select(out=k.ident[:, :], in_=k.ident[:, :], compare_op=ALU.is_equal, fill=0.0, base=0,
                               pattern=[[-1, 128]], channel_multiplier=1).then_inc(ident_step, 1)

        @block.vector
        def _(dve):
            dve.wait_ge(h_in, 32)
            dve.tensor_scalar(k.mask_ne[:, :, :], raw_h[:, :, :], 0.0, MASKED, ALU.is_le, ALU.mult)
            dve.tensor_scalar(k.mask_en[:, :], raw_ht[:, :], 0.0, MASKED, ALU.is_le, ALU.mult)
            dve.wait_ge(ident_step, 2)
            dve.tensor_copy(k.two[0:64, :], k.ident[0:64, 0:64]).then_inc(two_step, 1)
            dve.tensor_copy(k.two[64:128, :], k.ident[64:128, 64:128]).then_inc(two_step, 1)
            dve.wait_ge(adj_in, 16)
            dve.tensor_scalar(k.mask[:, :, :], raw[0][:, :, :], 0.0, MASKED, ALU.is_equal, ALU.mult)


def layernorm(nc, k, stage, x_d):
    Q = 4
    G = B * NT // Q
    with ExitStack() as ctx:
        sb, sem = sbuf(nc, ctx, stage), semaphores(nc, ctx, stage)
        total = sb("total", [128, Q, G])
        mean = sb("mean", [128, Q, G])
        square = [sb(f"square{i}", [128, G, F]) for i in range(2)]
        spread = sb("spread", [128, Q, G])
        var = sb("var", [128, Q, G])
        std = sb("std", [128, Q, G])
        rstd = sb("rstd", [128, Q, G])
        summed, meant, centred, squared, spread_done, var_done, std_done, rstd_done, scaled, out_d = (sem(n) for n in (
            "summed", "meant", "centred", "squared", "spread_done", "var_done", "std_done", "rstd_done", "scaled",
            "out_d"))
        block = ctx.enter_context(nc.Block())

        def part(q):
            return k.x[:, G * q:G * q + G, :]

        def wide(t, q):
            return t[:, q, :].unsqueeze(2).broadcast_to([128, G, F])

        @block.sync
        def _(sp):
            per = B // Q
            for q in range(Q):
                sp.wait_ge(scaled, q + 1)
                sp.dma_start(x_d[per * q:per * q + per].rearrange("b (t p) c -> p (b t) c", p=128), part(q)).then_inc(out_d, 16)
            sp.wait_ge(out_d, 16 * Q)

        @block.scalar
        def _(act):
            for q in range(Q):
                act.wait_ge(centred, q + 1)
                if q >= 2:
                    act.wait_ge(spread_done, q - 1)
                act.activation(square[q % 2][:, :, :], part(q), ACT.Square).then_inc(squared, 1)
            act.wait_ge(var_done, 1)
            act.activation(std[:, :, :], var[:, :, :], ACT.Sqrt).then_inc(std_done, 1)

        @block.vector
        def _(dve):
            for q in range(Q):
                dve.reduce_sum(total[:, q, :], part(q), axis=AX_X).then_inc(summed, 1)
            dve.wait_ge(summed, Q)
            dve.tensor_scalar(mean[:, :, :], total[:, :, :], 1.0 / F, None, ALU.mult).then_inc(meant, 1)
            dve.wait_ge(meant, 1)
            for q in range(Q):
                dve.tensor_tensor(part(q), part(q), wide(mean, q), ALU.subtract).then_inc(centred, 1)
            for q in range(Q):
                dve.wait_ge(squared, q + 1)
                dve.reduce_sum(spread[:, q, :], square[q % 2][:, :, :], axis=AX_X).then_inc(spread_done, 1)
            dve.wait_ge(spread_done, Q)
            dve.tensor_scalar(var[:, :, :], spread[:, :, :], 1.0 / F, EPS, ALU.mult, ALU.add).then_inc(var_done, 1)
            dve.wait_ge(std_done, 1)
            dve.reciprocal(rstd[:, :, :], std[:, :, :]).then_inc(rstd_done, 1)
            dve.wait_ge(rstd_done, 1)
            for q in range(Q):
                dve.tensor_tensor(part(q), part(q), wide(rstd, q), ALU.mult).then_inc(scaled, 1)


def industry(nc, k, xT, W_ind, ind_d):
    with ExitStack() as ctx:
        sb, pb, sem = sbuf(nc, ctx, "industry"), psum(nc, ctx, "industry"), semaphores(nc, ctx, "industry")
        xT_sb = sb("xT_sb", [F, B, N])
        w = sb("w", [F, F])
        ones = sb("ones", [128, 128], F32R)
        ones_raw = sb("ones_raw", [128, 128])
        deg = sb("deg", [128, N])
        rdeg = sb("rdeg", [128, N])
        v_hi = sb("v_hi", [128, NT, B, F], F32R)
        v_lo = sb("v_lo", [128, NT, B, F], F32R)
        out = [sb(f"out{i}", [128, N]) for i in range(2)]
        v_ps = [pb(f"v_ps{i}", [128, NT, F]) for i in range(2)]
        o_ps = [pb(f"o_ps{i}", [128, N]) for i in range(2)]
        d_ps = pb("d_ps", [128, N])
        (x_in, w_in, ones_step, deg_sum, deg_step, v_filled, v_hi_done, v_lo_done, o_filled, o_scaled) = (sem(n) for n in (
            "x_in", "w_in", "ones_step", "deg_sum", "deg_step", "v_filled", "v_hi_done", "v_lo_done", "o_filled",
            "o_scaled"))
        out_d = [sem(f"out_d{i}") for i in range(2)]
        block = ctx.enter_context(nc.Block())

        @block.sync
        def _(sp):
            sp.dma_start(w[:, :], W_ind).then_inc(w_in, 16)
            sp.dma_start(xT_sb[:, :, :], xT.rearrange("b c n -> c b n")).then_inc(x_in, 16)
            for p in range(B // 2):
                sp.wait_ge(o_scaled, p + 1)
                sp.dma_start(ind_d[2 * p:2 * p + 2].rearrange("b c n -> (b c) n"), out[p % 2][:, :]).then_inc(out_d[p % 2], 16)
            for i in range(2):
                sp.wait_ge(out_d[i], 16 * (B // 4))

        @block.tensor
        def _(pe):
            pe.wait_ge(ones_step, 2)
            for c in range(2):
                for t in range(NT):
                    last = pe.matmul(d_ps[:, 512 * c:512 * c + 512], ones[:, :], k.adjT[:, t, 512 * c:512 * c + 512],
                                     start=(t == 0), stop=(t == NT - 1))
            last.then_inc(deg_sum, 1)
            pe.wait_ge(w_in, 16)
            pe.wait_ge(x_in, 16)
            for b in range(B):
                if b >= 2:
                    pe.wait_ge(v_lo_done, b - 1)
                for t in range(NT):
                    last = pe.matmul(v_ps[b % 2][:, t, :], xT_sb[:, b, 128 * t:128 * t + 128], w[:, :], start=True, stop=True)
                last.then_inc(v_filled, 1)
            for p in range(B // 2):
                pe.wait_ge(v_lo_done, 2 * p + 2)
                if p >= 2:
                    pe.wait_ge(o_scaled, p - 1)
                for t in range(NT):
                    for n, v in enumerate((v_hi, v_lo)):
                        for c in range(2):
                            last = pe.matmul(o_ps[p % 2][:, 512 * c:512 * c + 512],
                                             v[:, t, 2 * p:2 * p + 2, :].rearrange("p b c -> p (b c)"),
                                             k.adjT[:, t, 512 * c:512 * c + 512], start=(t == 0 and n == 0),
                                             stop=(t == NT - 1 and n == 1))
                last.then_inc(o_filled, 1)

        @block.scalar
        def _(act):
            for b in range(B):
                act.wait_ge(v_filled, b + 1)
                act.activation(v_hi[:, :, b, :], v_ps[b % 2][:, :, :], ACT.Copy).then_inc(v_hi_done, 1)

        @block.vector
        def _(dve):
            dve.memset(ones_raw[:, :], 1.0).then_inc(ones_step, 1)
            dve.wait_ge(ones_step, 1)
            dve.tensor_copy(ones[:, :], ones_raw[:, :]).then_inc(ones_step, 1)
            dve.wait_ge(deg_sum, 1)
            dve.tensor_scalar(deg[:, :], d_ps[:, :], 1.0, None, ALU.max).then_inc(deg_step, 1)
            dve.wait_ge(deg_step, 1)
            dve.reciprocal(rdeg[:, :], deg[:, :]).then_inc(deg_step, 1)
            for b in range(B):
                dve.wait_ge(v_hi_done, b + 1)
                dve.tensor_tensor(v_lo[:, :, b, :], v_ps[b % 2][:, :, :], v_hi[:, :, b, :].bitcast(F32),
                                  ALU.subtract).then_inc(v_lo_done, 1)
            dve.wait_ge(deg_step, 2)
            for p in range(B // 2):
                dve.wait_ge(o_filled, p + 1)
                if p >= 2:
                    dve.wait_ge(out_d[p % 2], 16 * (p // 2))
                dve.tensor_tensor(out[p % 2][:, :], o_ps[p % 2][:, :], rdeg[:, :], ALU.mult).then_inc(o_scaled, 1)


def hyperedges(nc, k, xT, w, d):
    L = 4
    with ExitStack() as ctx:
        sb, pb, sem = sbuf(nc, ctx, "hyperedges"), psum(nc, ctx, "hyperedges"), semaphores(nc, ctx, "hyperedges")
        W2 = sb("W2", [F, 2, F])
        vecs = sb("vecs", [F, 3])
        a_node_b = sb("a_node_b", [F, EDGES])
        a_gn_b = sb("a_gn_b", [F, EDGES])
        fcW = sb("fcW", [F, 128])
        fcb = sb("fcb", [128, 1])
        av = sb("av", [128, 1])
        av_b = sb("av_b", [128, 128])

        def lanes(name, shape, dt=F32):
            return [sb(f"{name}{i}", shape, dt) for i in range(L)]

        xT_sb = lanes("xT_sb", [F, N])
        hT2 = lanes("hT2", [128, N])
        rows = lanes("rows", [128, NT, F])
        s_e = lanes("s_e", [EDGES, N])
        p_e = lanes("p_e", [EDGES, N])
        alpha = lanes("alpha", [EDGES, N])
        nmax = lanes("nmax", [EDGES, 1])
        den = lanes("den", [EDGES, 1])
        rden = lanes("rden", [EDGES, 1])
        agg2 = lanes("agg2", [EDGES, 2, F])
        aggT = lanes("aggT", [128, EDGES])
        agg = lanes("agg", [128, 3, EDGES // 2])
        low = lanes("low", [F, EDGES])
        elow = lanes("elow", [F, EDGES])
        he = lanes("he", [F, EDGES])
        tu = lanes("tu", [128, EDGES])
        qh = lanes("qh", [EDGES, 1])
        alphaT = coef = lanes("coef", [128, NT, EDGES])
        top = lanes("top", [128, NT])
        weight = lanes("weight", [128, NT])
        rweight = lanes("rweight", [128, NT])
        beta_st = lanes("beta_st", [128, N], F32R)
        coef_st = lanes("coef_st", [128, N], F32R)
        Z = [pb(f"Z{i}", [128, N]) for i in range(L)]
        names = ("w_in wide hT rows_f hT_sb rows_sb s_f s_sb s_leaky s_top p_f p_sb alpha_done rden_done alphaT_f "
                 "alphaT_sb agg_f agg_done aggT_f aggT_sb low_done elow_done he_part he_done u_f tu_done q_done se_f "
                 "th_done lg_done top_done lg_less coef_exp weight_done rweight_done coef_done beta_done beta_hi beta_lo "
                 "coefT_f coef_hi coef_lo agg_parts out_d").split()
        S = dict((n, sem(n)) for n in names)
        x_in = [sem(f"x_in{l}") for l in range(L)]
        block = ctx.enter_context(nc.Block())
        lane_of = [(g * L + l, l) for g in range(B // L) for l in range(L)]

        def groups():
            for g in range(B // L):
                yield [(g * L + l, l) for l in range(L)]

        @block.sync
        def _(sp):
            def col(v):
                return v.rearrange("(p o) -> p o", o=1)
            for half in range(2):
                sp.dma_start(W2[:, half, :], w["W"]).then_inc(S["w_in"], 16)
            for n, name in enumerate(("a_node", "a_gn", "a_ge")):
                sp.dma_start(vecs[:, n:n + 1], col(w[name])).then_inc(S["w_in"], 16)
            sp.dma_start(fcW[:, :], w["fcW"]).then_inc(S["w_in"], 16)
            sp.dma_start(fcb[:, :], col(w["fcb"])).then_inc(S["w_in"], 16)
            sp.dma_start(av[:, :], col(w["av"])).then_inc(S["w_in"], 16)
            for bs in groups():
                for b, l in bs:
                    if b >= L:
                        sp.wait_ge(S["rows_f"], b - L + 1)
                    sp.dma_start(xT_sb[l][:, :], xT[b]).then_inc(x_in[l], 16)
                for b, l in bs:
                    sp.wait_ge(S["agg_parts"], b + 1)
                    sp.dma_start(d["agg"][b], agg[l][:, :, :]).then_inc(S["out_d"], 16)
                    sp.wait_ge(S["hT_sb"], b + 1)
                    sp.dma_start(d["hT"][b], hT2[l][:, :]).then_inc(S["out_d"], 16)
                    sp.wait_ge(S["beta_lo"], b + 1)
                    sp.dma_start(d["beta"][b], beta_st[l][:, :].bitcast(F32)).then_inc(S["out_d"], 16)
                    sp.wait_ge(S["coef_lo"], b + 1)
                    sp.dma_start(d["coef"][b], coef_st[l][:, :].bitcast(F32)).then_inc(S["out_d"], 16)
            sp.wait_ge(S["out_d"], 64 * B)

        @block.tensor
        def _(pe):
            pe.wait_ge(S["w_in"], 16 * 8)
            pe.wait_ge(S["wide"], 3)
            for bs in groups():
                for b, l in bs:
                    pe.wait_ge(x_in[l], 16 * (b // L + 1))
                    wait(pe, S["coef_lo"], b - L + 1)
                    for c in range(2):
                        last = pe.matmul(Z[l][:, 512 * c:512 * c + 512], W2[:, :, :].rearrange("p a c -> p (a c)"),
                                         xT_sb[l][:, 512 * c:512 * c + 512], start=True, stop=True)
                    last.then_inc(S["hT"], 1)
                for b, l in bs:
                    pe.wait_ge(S["hT_sb"], b + 1)
                    for t in range(NT):
                        last = pe.matmul(Z[l][:, F * t:F * t + F], xT_sb[l][:, 128 * t:128 * t + 128], W2[:, 0, :],
                                         start=True, stop=True)
                    last.then_inc(S["rows_f"], 1)
                for b, l in bs:
                    pe.wait_ge(S["rows_sb"], b + 1)
                    for c in range(2):
                        last = pe.matmul(Z[l][0:EDGES, 512 * c:512 * c + 512], a_node_b[:, :],
                                         hT2[l][0:F, 512 * c:512 * c + 512], start=True, stop=True)
                    last.then_inc(S["s_f"], 1)
                for b, l in bs:
                    pe.wait_ge(S["s_sb"], b + 1)
                    for c in range(2):
                        last = pe.matmul(Z[l][0:EDGES, 512 * c:512 * c + 512], a_gn_b[:, :],
                                         hT2[l][0:F, 512 * c:512 * c + 512], start=True, stop=True)
                    last.then_inc(S["p_f"], 1)
                for b, l in bs:
                    pe.wait_ge(S["p_sb"], b + 1)
                    pe.wait_ge(S["alpha_done"], b + 1)
                    for t in range(NT):
                        last = pe.transpose(Z[l][:, EDGES * t:EDGES * t + EDGES], alpha[l][:, 128 * t:128 * t + 128],
                                            k.ident[0:64, 0:64])
                    last.then_inc(S["alphaT_f"], 1)
                for b, l in bs:
                    pe.wait_ge(S["alphaT_sb"], b + 1)
                    for t in range(NT):
                        last = pe.matmul(Z[l][0:EDGES, 0:F], alphaT[l][:, t, :], rows[l][:, t, :], start=(t == 0),
                                         stop=(t == NT - 1))
                    last.then_inc(S["agg_f"], 1)
                for b, l in bs:
                    pe.wait_ge(S["agg_done"], b + 1)
                    pe.transpose(Z[l][:, 0:EDGES], agg2[l][:, :, :].rearrange("p a c -> p (a c)"),
                                 k.ident[0:64, 0:64]).then_inc(S["aggT_f"], 1)
                for b, l in bs:
                    pe.wait_ge(S["he_done"], b + 1)
                    pe.matmul(Z[l][:, 0:EDGES], fcW[:, :], he[l][:, :], start=True, stop=True)
                    pe.matmul(Z[l][0:EDGES, 512:513], aggT[l][0:F, :], vecs[:, 2:3], start=True, stop=True).then_inc(S["u_f"], 1)
                for b, l in bs:
                    pe.wait_ge(S["tu_done"], b + 1)
                    pe.wait_ge(S["q_done"], b + 1)
                    pe.matmul(Z[l][:, 0:EDGES], av_b[:, :], tu[l][:, :], start=True, stop=True).then_inc(S["se_f"], 1)
                for b, l in bs:
                    pe.wait_ge(S["coef_done"], b + 1)
                    for t in range(NT):
                        last = pe.transpose(Z[l][0:EDGES, 128 * t:128 * t + 128], coef[l][:, t, :], k.ident[:, :])
                    last.then_inc(S["coefT_f"], 1)

        @block.scalar
        def _(act):
            for bs in groups():
                for b, l in bs:
                    act.wait_ge(S["rows_f"], b + 1)
                    act.activation(rows[l][:, :, :].rearrange("p t c -> p (t c)"), Z[l][:, 0:512], ACT.Copy).then_inc(S["rows_sb"], 1)
                for b, l in bs:
                    act.wait_ge(S["s_f"], b + 1)
                    act.activation(s_e[l][:, :], Z[l][0:EDGES, :], ACT.Copy).then_inc(S["s_sb"], 1)
                for b, l in bs:
                    act.wait_ge(S["p_f"], b + 1)
                    act.activation(p_e[l][:, :], Z[l][0:EDGES, :], ACT.Copy).then_inc(S["p_sb"], 1)
                for b, l in bs:
                    act.wait_ge(S["s_top"], b + 1)
                    act.activation(alpha[l][:, :], alpha[l][:, :], ACT.Exp, bias=nmax[l][:, 0:1], scale=-1.0,
                                   accum_out=den[l][:, 0:1]).then_inc(S["alpha_done"], 1)
                for b, l in bs:
                    act.wait_ge(S["low_done"], b + 1)
                    act.activation(elow[l][:, :], low[l][:, :], ACT.Exp).then_inc(S["elow_done"], 1)
                for b, l in bs:
                    act.wait_ge(S["u_f"], b + 1)
                    act.activation(tu[l][:, :], Z[l][:, 0:EDGES], ACT.Tanh, bias=fcb[:, 0:1]).then_inc(S["tu_done"], 1)
                    act.activation(qh[l][:, :], Z[l][0:EDGES, 512:513], ACT.Copy, scale=0.5).then_inc(S["q_done"], 1)
                for b, l in bs:
                    act.wait_ge(S["q_done"], b + 1)
                    act.activation(p_e[l][:, :], p_e[l][:, :], ACT.Tanh, bias=qh[l][:, 0:1], scale=0.5).then_inc(S["th_done"], 1)
                for b, l in bs:
                    act.wait_ge(S["lg_less"], b + 1)
                    act.activation(coef[l][:, :, :], coef[l][:, :, :], ACT.Exp).then_inc(S["coef_exp"], 1)
                for b, l in bs:
                    act.wait_ge(S["beta_done"], b + 1)
                    act.activation(beta_st[l][0:64, :], p_e[l][:, :], ACT.Copy).then_inc(S["beta_hi"], 1)
                for b, l in bs:
                    act.wait_ge(S["coefT_f"], b + 1)
                    act.activation(coef_st[l][0:64, :], Z[l][0:EDGES, :], ACT.Copy).then_inc(S["coef_hi"], 1)

        @block.vector
        def _(dve):
            dve.wait_ge(S["w_in"], 16 * 8)
            dve.tensor_copy(a_node_b[:, :], vecs[:, 0:1].broadcast_to([F, EDGES])).then_inc(S["wide"], 1)
            dve.tensor_copy(a_gn_b[:, :], vecs[:, 1:2].broadcast_to([F, EDGES])).then_inc(S["wide"], 1)
            dve.tensor_copy(av_b[:, :], av[:, 0:1].broadcast_to([128, 128])).then_inc(S["wide"], 1)
            for bs in groups():
                for b, l in bs:
                    dve.wait_ge(S["hT"], b + 1)
                    wait(dve, S["out_d"], 64 * (b // L) * L)
                    dve.tensor_copy(hT2[l][:, :], Z[l][:, :]).then_inc(S["hT_sb"], 1)
                for b, l in bs:
                    dve.wait_ge(S["s_sb"], b + 1)
                    dve.scalar_tensor_tensor(out=s_e[l][:, :], in0=s_e[l][:, :], scalar=0.2, in1=s_e[l][:, :], op0=ALU.mult,
                                             op1=ALU.max).then_inc(S["s_leaky"], 1)
                for b, l in bs:
                    dve.wait_ge(S["s_leaky"], b + 1)
                    dve.tensor_tensor_reduce(alpha[l][:, :], s_e[l][:, :], k.mask_en[:, :], -1.0, 3.0e38, ALU.add, ALU.min,
                                             nmax[l][:, 0:1]).then_inc(S["s_top"], 1)
                for b, l in bs:
                    dve.wait_ge(S["alpha_done"], b + 1)
                    dve.reciprocal(rden[l][:, :], den[l][:, :]).then_inc(S["rden_done"], 1)
                for b, l in bs:
                    dve.wait_ge(S["alphaT_f"], b + 1)
                    dve.tensor_copy(alphaT[l][:, :, :].rearrange("p t e -> p (t e)"), Z[l][:, 0:512]).then_inc(S["alphaT_sb"], 1)
                for b, l in bs:
                    dve.wait_ge(S["agg_f"], b + 1)
                    dve.wait_ge(S["rden_done"], b + 1)
                    dve.tensor_scalar(agg2[l][:, :, :], Z[l][0:EDGES, 0:F].unsqueeze(1).broadcast_to([EDGES, 2, F]),
                                      rden[l][:, 0:1], None, ALU.mult).then_inc(S["agg_done"], 1)
                for b, l in bs:
                    dve.wait_ge(S["aggT_f"], b + 1)
                    dve.tensor_copy(aggT[l][:, :], Z[l][:, 0:EDGES]).then_inc(S["aggT_sb"], 1)
                for b, l in bs:
                    dve.wait_ge(S["aggT_sb"], b + 1)
                    for half in range(2):
                        p = slice(64 * half, 64 * half + 64)
                        mine = aggT[l][p, :].rearrange("p (i two) -> p i two", two=2)[:, :, half]
                        dve.tensor_copy(agg[l][p, 0, :], mine)
                        dve.tensor_scalar(agg[l][p, 1, :], mine, -1.0, None, ALU.mult)
                        last = dve.tensor_scalar(agg[l][p, 2, :], mine, 1.0, None, ALU.add)
                    last.then_inc(S["agg_parts"], 1)
                    dve.tensor_scalar(low[l][:, :], aggT[l][0:F, :], 0.0, None, ALU.min).then_inc(S["low_done"], 1)
                for b, l in bs:
                    dve.wait_ge(S["elow_done"], b + 1)
                    dve.scalar_tensor_tensor(out=low[l][:, :], in0=aggT[l][0:F, :], scalar=0.0, in1=elow[l][:, :], op0=ALU.max,
                                             op1=ALU.add).then_inc(S["he_part"], 1)
                for b, l in bs:
                    dve.wait_ge(S["he_part"], b + 1)
                    dve.tensor_scalar(he[l][:, :], low[l][:, :], -1.0, None, ALU.add).then_inc(S["he_done"], 1)
                for b, l in bs:
                    dve.wait_ge(S["se_f"], b + 1)
                    dve.tensor_tensor(coef[l][:, :, :], Z[l][:, 0:EDGES].unsqueeze(1).broadcast_to([128, NT, EDGES]),
                                      k.mask_ne[:, :, :], ALU.add).then_inc(S["lg_done"], 1)
                for b, l in bs:
                    dve.wait_ge(S["lg_done"], b + 1)
                    dve.tensor_reduce(top[l][:, :], coef[l][:, :, :], AX_X, ALU.max).then_inc(S["top_done"], 1)
                for b, l in bs:
                    dve.wait_ge(S["top_done"], b + 1)
                    dve.tensor_tensor(coef[l][:, :, :], coef[l][:, :, :],
                                      top[l][:, :].unsqueeze(2).broadcast_to([128, NT, EDGES]), ALU.subtract).then_inc(S["lg_less"], 1)
                for b, l in bs:
                    dve.wait_ge(S["th_done"], b + 1)
                    dve.tensor_scalar(p_e[l][:, :], p_e[l][:, :], 0.5, 0.5, ALU.mult, ALU.add).then_inc(S["beta_done"], 1)
                for b, l in bs:
                    dve.wait_ge(S["coef_exp"], b + 1)
                    dve.reduce_sum(weight[l][:, :], coef[l][:, :, :], axis=AX_X).then_inc(S["weight_done"], 1)
                for b, l in bs:
                    dve.wait_ge(S["weight_done"], b + 1)
                    dve.reciprocal(rweight[l][:, :], weight[l][:, :]).then_inc(S["rweight_done"], 1)
                for b, l in bs:
                    dve.wait_ge(S["rweight_done"], b + 1)
                    dve.tensor_tensor(coef[l][:, :, :], coef[l][:, :, :],
                                      rweight[l][:, :].unsqueeze(2).broadcast_to([128, NT, EDGES]), ALU.mult).then_inc(S["coef_done"], 1)
                for b, l in bs:
                    dve.wait_ge(S["beta_hi"], b + 1)
                    dve.tensor_tensor(beta_st[l][64:128, :], p_e[l][:, :], beta_st[l][0:64, :].bitcast(F32),
                                      ALU.subtract).then_inc(S["beta_lo"], 1)
                for b, l in bs:
                    dve.wait_ge(S["coef_hi"], b + 1)
                    dve.tensor_tensor(coef_st[l][64:128, :], Z[l][0:EDGES, :], coef_st[l][0:64, :].bitcast(F32),
                                      ALU.subtract).then_inc(S["coef_lo"], 1)


def messages(nc, k, d):
    PAIRS = EDGES // 2
    STEPS = 2 * PAIRS
    ITERS = B // 2
    ALL = B * PAIRS
    with ExitStack() as ctx:
        sb, pb, sem = sbuf(nc, ctx, "messages"), psum(nc, ctx, "messages"), semaphores(nc, ctx, "messages")
        sel = sb("sel", [128, PAIRS, 2, 64], F32R)
        hT = [sb(f"hT{i}", [128, N]) for i in range(2)]
        beta = [sb(f"beta{i}", [128, N], F32R) for i in range(2)]
        coef = [sb(f"coef{i}", [128, N], F32R) for i in range(2)]
        agg = [sb(f"agg{i}", [128, 3, PAIRS]) for i in range(2)]
        y = [sb(f"y{i}", [128, N]) for i in range(4)]
        e = [sb(f"e{i}", [128, N]) for i in range(2)]
        part = [sb(f"part{i}", [128, N]) for i in range(2)]
        g_sb = [sb(f"g_sb{i}", [F, N]) for i in range(2)]
        beta_ps = [pb(f"beta_ps{i}", [128, N]) for i in range(2)]
        coef_ps = pb("coef_ps", [128, N])
        g_ps = pb("g_ps", [F, N])
        op_in = [sem(f"op_in{i}") for i in range(2)]
        (sel_done, beta_f, coef_f, y_done, low_done, e_done, t_done, part_done, g_added, g_out) = (sem(n) for n in (
            "sel_done", "beta_f", "coef_f", "y_done", "low_done", "e_done", "t_done", "part_done", "g_added", "g_out"))
        out_d = [sem(f"out_d{i}") for i in range(2)]
        block = ctx.enter_context(nc.Block())

        def exists(i, n):
            return not isinstance(i, int) or 0 <= i < n

        def run(eng, step):
            for s in range(STEPS):
                step(0, s)
            with eng.Fori(1, ITERS - 1) as it:
                for s in range(STEPS):
                    step(it, s)
            for s in range(STEPS):
                step(ITERS - 1, s)
            for s in range(4):
                step(ITERS, s)

        @block.sync
        def _(sp):
            def load(b, par, first):
                if not first:
                    sp.wait_ge(part_done, PAIRS * (b - 1))
                for name, t in (("hT", hT[par][:, :]), ("beta", beta[par][:, :].bitcast(F32)),
                                ("coef", coef[par][:, :].bitcast(F32)), ("agg", agg[par][:, :, :].rearrange("p a i -> p (a i)"))):
                    sp.dma_start(t, one(d[name][bass.ds(b, 1)] if name != "agg" else
                                        d[name][bass.ds(b, 1)].rearrange("o p a i -> o p (a i)"))).then_inc(op_in[par], 16)

            load(0, 0, True)
            load(1, 1, True)
            with sp.Fori(1, ITERS) as it:
                load(2 * it, 0, False)
                sp.wait_ge(g_out, 2 * it - 1)
                sp.dma_start(one(d["g"][bass.ds(2 * it - 2, 1)]), g_sb[0][:, :]).then_inc(out_d[0], 16)
                load(2 * it + 1, 1, False)
                sp.wait_ge(g_out, 2 * it)
                sp.dma_start(one(d["g"][bass.ds(2 * it - 1, 1)]), g_sb[1][:, :]).then_inc(out_d[1], 16)
            for par in range(2):
                sp.wait_ge(g_out, B - 1 + par)
                sp.dma_start(d["g"][B - 2 + par], g_sb[par][:, :]).then_inc(out_d[par], 16)
            for par in range(2):
                sp.wait_ge(out_d[par], 16 * (ITERS + par))

        @block.tensor
        def _(pe):
            pe.wait_ge(sel_done, 4)

            def fill_beta(n, s):
                par, i = (s // PAIRS) % 2, s % PAIRS
                wait(pe, y_done, n - 1)
                for c in range(2):
                    last = pe.matmul(beta_ps[s % 2][:, 512 * c:512 * c + 512], sel[:, i, :, :].rearrange("p a c -> p (a c)"),
                                     beta[par][:, 512 * c:512 * c + 512], start=True, stop=True)
                last.then_inc(beta_f, 1)

            pe.wait_ge(op_in[0], 64)
            fill_beta(0, 0)

            def step(it, s):
                n = STEPS * it + s
                par, i = s // PAIRS, s % PAIRS
                if exists(n + 1, ALL):
                    if i == PAIRS - 1:
                        nxt = 1 - par
                        if not (isinstance(it, int) and it == ITERS - 1 and par == 1):
                            pe.wait_ge(op_in[nxt], 64 * (it + par) + 64)
                if exists(n + 1, ALL):
                    fill_beta(n + 1, s + 1)
                if exists(n - 1, ALL):
                    wait(pe, part_done, n - 1)
                    i1, par1 = (s - 1) % PAIRS, ((s - 1) // PAIRS) % 2
                    for c in range(2):
                        last = pe.matmul(coef_ps[:, 512 * c:512 * c + 512], sel[:, i1, :, :].rearrange("p a c -> p (a c)"),
                                         coef[par1][:, 512 * c:512 * c + 512], start=True, stop=True)
                    last.then_inc(coef_f, 1)
                if exists(n - 2, ALL):
                    j = (s - 2) % PAIRS
                    wait(pe, part_done, n - 1)
                    if j == 0:
                        wait(pe, g_out, 2 * it + (s - 2) // PAIRS)
                    for c in range(2):
                        last = pe.matmul(g_ps[:, 512 * c:512 * c + 512], k.two[:, :], part[s % 2][:, 512 * c:512 * c + 512],
                                         start=(j == 0), stop=(j == PAIRS - 1))
                    last.then_inc(g_added, 1)

            run(pe, step)

        @block.scalar
        def _(act):
            act.sem_inc(out_d[1], 16)

            def step(it, s):
                n = STEPS * it + s
                par, i = s // PAIRS, s % PAIRS
                if exists(n, ALL):
                    a = agg[par]
                    act.wait_ge(y_done, n + 1)
                    wait(act, t_done, n - 1)
                    act.activation(e[s % 2][:, :], y[s % 4][:, :], ACT.Relu, bias=a[:, 1, i:i + 1], scale=-1.0).then_inc(low_done, 1)
                    act.wait_ge(low_done, n + 1)
                    act.activation(e[s % 2][:, :], e[s % 2][:, :], ACT.Exp, scale=-1.0).then_inc(e_done, 1)
                if i == 2:
                    b = 2 * it + (s - 3) // PAIRS
                    if exists(b, B):
                        p = (par + 1) % 2
                        wait(act, out_d[p], 16 * it)
                        act.wait_ge(g_added, PAIRS * (b + 1))
                        act.activation(g_sb[p][:, :], g_ps[:, :], ACT.Copy, bias=-1.0).then_inc(g_out, 1)

            run(act, step)

        @block.vector
        def _(dve):
            for half in range(2):
                for p in (slice(0, 64), slice(64, 128)):
                    mine = k.two[p, :].rearrange("p (i two) -> p i two", two=2)[:, :, half]
                    dve.tensor_copy(sel[p, :, half, :], mine.unsqueeze(2).broadcast_to([64, PAIRS, 64])).then_inc(sel_done, 1)

            def step(it, s):
                n = STEPS * it + s
                par, i = s // PAIRS, s % PAIRS
                if exists(n, ALL):
                    if i == 0:
                        dve.wait_ge(op_in[par], 64 * it + 64)
                    wait(dve, part_done, n - 3)
                    dve.wait_ge(beta_f, n + 1)
                    dve.scalar_tensor_tensor(out=y[s % 4][:, :], in0=hT[par][:, :], scalar=agg[par][:, 0, i:i + 1],
                                             in1=beta_ps[s % 2][:, :], op0=ALU.subtract, op1=ALU.mult).then_inc(y_done, 1)
                if exists(n - 1, ALL):
                    yq = y[(s - 1) % 4]
                    a = agg[((s - 1) // PAIRS) % 2]
                    j = (s - 1) % PAIRS
                    dve.wait_ge(e_done, n)
                    dve.scalar_tensor_tensor(out=yq[:, :], in0=yq[:, :], scalar=a[:, 2, j:j + 1], in1=e[(s - 1) % 2][:, :],
                                             op0=ALU.add, op1=ALU.max).then_inc(t_done, 1)
                if exists(n - 2, ALL):
                    wait(dve, g_added, n - 3)
                    dve.wait_ge(coef_f, n - 1)
                    dve.wait_ge(t_done, n - 1)
                    dve.tensor_tensor(part[s % 2][:, :], y[(s - 2) % 4][:, :], coef_ps[:, :], ALU.mult).then_inc(part_done, 1)

            run(dve, step)


def mix(nc, k, w, d):
    with ExitStack() as ctx:
        sb, pb, sem = sbuf(nc, ctx, "mix"), psum(nc, ctx, "mix"), semaphores(nc, ctx, "mix")
        fcW = sb("fcW", [F, 128])
        fcb = sb("fcb", [128, 1])
        av = sb("av", [128, 1])
        av_b = sb("av_b", [128, 2, F])
        g = [sb(f"g{i}", [F, N]) for i in range(2)]
        ind = [sb(f"ind{i}", [F, N]) for i in range(2)]
        tg = [sb(f"tg{i}", [128, N]) for i in range(2)]
        ti = [sb(f"ti{i}", [128, N]) for i in range(2)]
        c = [sb(f"c{i}", [F, N]) for i in range(2)]
        o = [sb(f"o{i}", [F, N]) for i in range(2)]
        g_ps, i_ps, d_ps = pb("g_ps", [128, N]), pb("i_ps", [128, N]), pb("d_ps", [F, N])
        r_ps = pb("r_ps", [128, NT, F])
        (w_in, wide, u_f, tg_done, ti_done, d_f, c_done, diff_done, mixed, o_done, r_f, r_done) = (sem(n) for n in (
            "w_in", "wide", "u_f", "tg_done", "ti_done", "d_f", "c_done", "diff_done", "mixed", "o_done", "r_f",
            "r_done"))
        in_ = [sem(f"in{i}") for i in range(2)]
        block = ctx.enter_context(nc.Block())

        @block.sync
        def _(sp):
            sp.dma_start(fcW[:, :], w["fcW"]).then_inc(w_in, 16)
            sp.dma_start(fcb[:, :], w["fcb"].rearrange("(p o) -> p o", o=1)).then_inc(w_in, 16)
            sp.dma_start(av[:, :], w["av"].rearrange("(p o) -> p o", o=1)).then_inc(w_in, 16)
            for b in range(B):
                wait(sp, o_done, b - 1)
                sp.dma_start(g[b % 2][:, :], d["g"][b]).then_inc(in_[b % 2], 16)
                sp.dma_start(ind[b % 2][:, :], d["ind"][b]).then_inc(in_[b % 2], 16)

        @block.tensor
        def _(pe):
            pe.wait_ge(w_in, 48)
            pe.wait_ge(wide, 2)
            for n in range(B + 2):
                b = n
                if b < B:
                    pe.wait_ge(in_[b % 2], 32 * (b // 2 + 1))
                    wait(pe, tg_done, b)
                    wait(pe, ti_done, b)
                    for src, ps in ((g, g_ps), (ind, i_ps)):
                        for ch in range(2):
                            s = slice(512 * ch, 512 * ch + 512)
                            last = pe.matmul(ps[:, s], fcW[:, :], src[b % 2][:, s], start=True, stop=True)
                        last.then_inc(u_f, 1)
                b = n - 1
                if 0 <= b < B:
                    pe.wait_ge(ti_done, b + 1)
                    wait(pe, c_done, b)
                    for ch in range(2):
                        s = slice(512 * ch, 512 * ch + 512)
                        pe.matmul(d_ps[:, s], av_b[:, 0, :], ti[b % 2][:, s], start=True, stop=False)
                        last = pe.matmul(d_ps[:, s], av_b[:, 1, :], tg[b % 2][:, s], start=False, stop=True)
                    last.then_inc(d_f, 1)
                b = n - 2
                if 0 <= b < B:
                    pe.wait_ge(o_done, b + 1)
                    wait(pe, r_done, b)
                    for t in range(NT):
                        last = pe.transpose(r_ps[:, t, :], o[b % 2][:, 128 * t:128 * t + 128], k.ident[0:64, 0:64])
                    last.then_inc(r_f, 1)

        @block.scalar
        def _(act):
            act.wait_ge(w_in, 48)
            for n in range(B + 1):
                b = n
                if b < B:
                    wait(act, d_f, b - 1)
                    act.wait_ge(u_f, 2 * b + 1)
                    act.activation(tg[b % 2][:, :], g_ps[:, :], ACT.Tanh, bias=fcb[:, 0:1]).then_inc(tg_done, 1)
                    act.wait_ge(u_f, 2 * b + 2)
                    act.activation(ti[b % 2][:, :], i_ps[:, :], ACT.Tanh, bias=fcb[:, 0:1]).then_inc(ti_done, 1)
                b = n - 1
                if 0 <= b < B:
                    act.wait_ge(d_f, b + 1)
                    wait(act, mixed, b - 1)
                    act.activation(c[b % 2][:, :], d_ps[:, :], ACT.Tanh, scale=0.5).then_inc(c_done, 1)

        @block.vector
        def _(dve):
            dve.wait_ge(w_in, 48)
            dve.tensor_copy(av_b[:, 0, :], av[:, 0:1].broadcast_to([128, F])).then_inc(wide, 1)
            dve.tensor_scalar(av_b[:, 1, :], av[:, 0:1].broadcast_to([128, F]), -1.0, None, ALU.mult).then_inc(wide, 1)
            for n in range(B + 1):
                b = n
                if b < B:
                    p = b % 2
                    dve.wait_ge(in_[b % 2], 32 * (b // 2 + 1))
                    wait(dve, r_f, b - 1)
                    dve.tensor_tensor(o[p][:, :], ind[p][:, :], g[p][:, :], ALU.subtract).then_inc(diff_done, 1)
                    dve.wait_ge(diff_done, b + 1)
                    dve.wait_ge(c_done, b + 1)
                    dve.scalar_tensor_tensor(out=c[p][:, :], in0=c[p][:, :], scalar=1.0, in1=o[p][:, :], op0=ALU.add,
                                             op1=ALU.mult).then_inc(mixed, 1)
                    dve.wait_ge(mixed, b + 1)
                    dve.scalar_tensor_tensor(out=o[p][:, :], in0=c[p][:, :], scalar=0.5, in1=g[p][:, :], op0=ALU.mult,
                                             op1=ALU.add).then_inc(o_done, 1)
                b = n - 1
                if 0 <= b < B:
                    dve.wait_ge(r_f, b + 1)
                    xb = k.x[:, NT * b:NT * b + NT, :]
                    dve.tensor_tensor(xb, r_ps[:, :, :], xb, ALU.add).then_inc(r_done, 1)


def split_heads(nc, k, Wh, xs_d, ws_d):
    G = B * 2
    with ExitStack() as ctx:
        sb, pb, sem = sbuf(nc, ctx, "split_heads"), psum(nc, ctx, "split_heads"), semaphores(nc, ctx, "split_heads")
        x_stack = sb("x_stack", [128, B, N], F32R)
        x_twice = [sb(f"x_twice{i}", [128, 4, 2, F]) for i in range(4)]
        w_in = sb("w_in", [128, HEADS, D])
        w_stack = sb("w_stack", [128, HEADS, 2, D], F32R)
        xT = [pb(f"xT{i}", [128, 512]) for i in range(4)]
        w_got, x_doubled, x_turned, x_hi, x_lo, w_hi, w_lo, out_d = (sem(n) for n in (
            "w_got", "x_doubled", "x_turned", "x_hi", "x_lo", "w_hi", "w_lo", "out_d"))
        block = ctx.enter_context(nc.Block())

        @block.sync
        def _(sp):
            for half in range(2):
                sp.dma_start(w_in[64 * half:64 * half + 64, :, :], Wh.rearrange("h c d -> c h d")).then_inc(w_got, 16)
            for b in range(B):
                sp.wait_ge(x_lo, 2 * b + 2)
                sp.dma_start(xs_d[b], x_stack[:, b, :].bitcast(F32)).then_inc(out_d, 16)
            sp.wait_ge(w_lo, 1)
            sp.dma_start(ws_d.rearrange("h p c d -> p h c d"), w_stack[:, :, :, :].bitcast(F32)).then_inc(out_d, 16)
            sp.wait_ge(out_d, 16 * (B + 1))

        @block.tensor
        def _(pe):
            for g in range(G):
                pe.wait_ge(x_doubled, g + 1)
                if g >= 4:
                    pe.wait_ge(x_lo, g - 3)
                for i in range(4):
                    last = pe.transpose(xT[g % 4][:, 128 * i:128 * i + 128],
                                        x_twice[g % 4][:, i, :, :].rearrange("p a c -> p (a c)"), k.ident[:, :])
                last.then_inc(x_turned, 1)

        @block.gpsimd
        def _(pool):
            for g in range(G):
                if g >= 4:
                    pool.wait_ge(x_turned, g - 3)
                pool.tensor_copy(x_twice[g % 4][:, :, :, :],
                                 k.x[:, 4 * g:4 * g + 4, :].unsqueeze(2).broadcast_to([128, 4, 2, F])).then_inc(x_doubled, 1)

        @block.scalar
        def _(act):
            for g in range(G):
                act.wait_ge(x_turned, g + 1)
                act.activation(x_stack[:, g // 2, 512 * (g % 2):512 * (g % 2) + 512], xT[g % 4][:, :], ACT.Copy).then_inc(x_hi, 1)
            act.wait_ge(w_got, 32)
            act.activation(w_stack[:, :, 0, :], w_in[:, :, :], ACT.Copy).then_inc(w_hi, 1)

        @block.vector
        def _(dve):
            for g in range(G):
                dve.wait_ge(x_hi, g + 1)
                part = x_stack[64:128, g // 2, 512 * (g % 2):512 * (g % 2) + 512]
                dve.tensor_tensor(part, xT[g % 4][64:128, :], part.bitcast(F32), ALU.subtract).then_inc(x_lo, 1)
            dve.wait_ge(w_hi, 1)
            dve.tensor_tensor(w_stack[:, :, 1, :], w_in[:, :, :], w_stack[:, :, 0, :].bitcast(F32), ALU.subtract).then_inc(w_lo, 1)


def heads(nc, k, xs_d, ws_d, bh, Wout):
    U = B * HEADS
    ITERS = U // 2
    J_ALL, C_ALL = U * 16, U * 2
    with ExitStack() as ctx:
        sb, pb, sem = sbuf(nc, ctx, "heads"), psum(nc, ctx, "heads"), semaphores(nc, ctx, "heads")
        x_st = [sb(f"x_st{i}", [128, N], F32R) for i in range(2)]
        w_st = [sb(f"w_st{i}", [128, 2, D], F32R) for i in range(2)]
        bias = [sb(f"bias{i}", [128, 1]) for i in range(2)]
        w_out = [sb(f"w_out{i}", [128, F]) for i in range(2)]
        hT = [[sb(f"hT{i}{p}", [128, N], F32R) for p in "hl"] for i in range(2)]
        hR = [[sb(f"hR{i}{p}", [128, NT, D], F32R) for p in "hl"] for i in range(2)]
        neg = [sb(f"neg{i}", [128, N]) for i in range(2)]
        nmax = sb("nmax", [128, 2, 1])
        P = [sb(f"P{i}", [128, 4, N]) for i in range(2)]
        den = [sb(f"den{i}", [128, 4]) for i in range(2)]
        rden = [sb(f"rden{i}", [128, 4]) for i in range(2)]
        PTh = [sb(f"PTh{i}", [128, 512], F32R) for i in range(4)]
        PTl = [sb(f"PTl{i}", [128, 512], F32R) for i in range(4)]
        rB = sb("rB", [128, 512])
        pos = sb("pos", [128, 512])
        att = sb("att", [128, 512])
        cat = [sb(f"cat{i}", [128, 512]) for i in range(2)]
        S_ps = [pb(f"S_ps{i}", [128, N]) for i in range(2)]
        T_ps = [pb(f"T_ps{i}", [128, 512]) for i in range(2)]
        O_ps = [pb(f"O_ps{i}", [128, 512]) for i in range(2)]
        wx_in = [sem(f"wx_in{i}") for i in range(2)]
        bo_in = [sem(f"bo_in{i}") for i in range(2)]
        (s_filled, s_taken, h_hi, exp_done, turned, pt_hi, pt_lo, av_done, r_ready, rb_turned, rb_done, att_done,
         cat_done, h2_done, acc_done, zeroed, max_turn, cat_turn, att_read, pool_step) = (sem(n) for n in (
            "s_filled", "s_taken", "h_hi", "exp_done", "turned", "pt_hi", "pt_lo", "av_done", "r_ready", "rb_turned",
            "rb_done", "att_done", "cat_done", "h2_done", "acc_done", "zeroed", "max_turn", "cat_turn",
            "att_read", "pool_step"))
        block = ctx.enter_context(nc.Block())

        S_POS = [0, 1, 2, 3, 4, 5, 7, 9]
        HT_POS, HR_POS = 6, 8
        T_BANK = {6: 0, 7: 1, 0: 1, 1: 0, 2: 1, 3: 0, 4: 1, 5: 0}

        def item(it, hp, pos):
            return 20 * it + (10 * hp + pos + 2)

        def s_pos(it, hp, i):
            return i if isinstance(it, int) and it == ITERS - 1 and hp == 1 else S_POS[i]

        def exists(i, n):
            return not isinstance(i, int) or 0 <= i < n

        def run(eng, slot):
            for s in range(16):
                slot(0, s, False)
            with eng.Fori(1, ITERS - 1) as it:
                for s in range(16):
                    slot(it, s, False)
            for s in range(16):
                slot(ITERS - 1, s, False)
            for s in range(8):
                slot(ITERS, s, True)

        @block.sync
        def _(sp):
            def wx(u, b, h, par, it):
                wait(sp, s_filled, 10 * u - 18)
                sp.dma_start(w_st[par][:, :, :].bitcast(F32), ws_d[bass.ds(h, 1)].rearrange("o p c d -> (o p) c d")).then_inc(wx_in[par], 16)
                sp.dma_start(x_st[par][:, :].bitcast(F32), xs_d[bass.ds(b, 1)].rearrange("o p n -> (o p) n")).then_inc(wx_in[par], 16)

            def bo(u, h, par):
                wait(sp, h2_done, 2 * u - 2)
                sp.dma_start(bias[par][:, :], bh[bass.ds(h, 1), :].rearrange("o d -> d o")).then_inc(bo_in[par], 16)
                sp.dma_start(w_out[par][:, :], Wout[bass.ds(h, 1)].rearrange("o d f -> (o d) f")).then_inc(bo_in[par], 16)

            wx(0, 0, 0, 0, 0)
            wx(1, 0, 1, 1, 0)
            bo(0, 0, 0)
            bo(1, 1, 1)
            with sp.Fori(1, ITERS) as it:
                wx(2 * it, it // 4, (2 * it) % 8, 0, it)
                bo(2 * it, (2 * it) % 8, 0)
                wx(2 * it + 1, it // 4, (2 * it + 1) % 8, 1, it)
                bo(2 * it + 1, (2 * it + 1) % 8, 1)

        @block.tensor
        def _(pe):
            def project(it, hp, nxt_it, par, r_t, r_r):
                pe.wait_ge(wx_in[par], 32 * nxt_it + 32)
                wait(pe, s_taken, r_t - 1)
                ps = S_ps[0]
                for c in range(2):
                    pe.matmul(ps[:, 512 * c:512 * c + 512], w_st[par][:, 0, :], x_st[par][:, 512 * c:512 * c + 512],
                              start=True, stop=False)
                for c in range(2):
                    last = pe.matmul(ps[:, 512 * c:512 * c + 512], w_st[par][:, 1, :], x_st[par][:, 512 * c:512 * c + 512],
                                     start=False, stop=True)
                last.then_inc(s_filled, 1)

            def project_rows(par, r_r, ps):
                wait(pe, s_taken, r_r - 1)
                for t in range(NT):
                    for c in range(2):
                        last = pe.matmul(ps[:, 128 * t:128 * t + 128], x_st[par][:, 128 * t:128 * t + 128], w_st[par][:, c, :],
                                         start=(c == 0), stop=(c == 1))
                last.then_inc(s_filled, 1)

            project(0, 0, 0, 0, 0, 1)
            project_rows(0, 1, S_ps[1])

            def slot(it, s, tail):
                hp, i = s // 8, s % 8
                if not tail:
                    r = item(it, hp, s_pos(it, hp, i))
                    wait(pe, s_taken, r - 1)
                    if i == 0:
                        wait(pe, s_taken, r - 3 if not (isinstance(it, int) and it == 0 and hp == 0) else 1)
                    ps = S_ps[s_pos(it, hp, i) % 2]
                    hh, hl = hT[hp]
                    tile = slice(128 * i, 128 * i + 128)
                    for c in range(2):
                        ch = slice(512 * c, 512 * c + 512)
                        pe.matmul(ps[:, ch], hh[:, tile], hh[:, ch], start=True, stop=False)
                        pe.matmul(ps[:, ch], hh[:, tile], hl[:, ch], start=False, stop=False)
                    for c in range(2):
                        ch = slice(512 * c, 512 * c + 512)
                        last = pe.matmul(ps[:, ch], hl[:, tile], hh[:, ch], start=False, stop=True)
                    last.then_inc(s_filled, 1)
                    if not (isinstance(it, int) and it == ITERS - 1 and hp == 1):
                        if i == 5:
                            project(it, hp, it + hp, 1 - hp, item(it, hp, HT_POS), 0)
                        if i == 6:
                            project_rows(1 - hp, item(it, hp, HR_POS), S_ps[0])
                for a in range(2):
                    J = 32 * it + (2 * s - 10 + a)
                    j = (2 * s - 10 + a) % 8
                    if exists(J, J_ALL):
                        C4 = 16 * it + 4 * ((2 * s - 10 + a) // 8)
                        if j == 0:
                            wait(pe, exp_done, C4 + 4)
                        if j == 7:
                            wait(pe, acc_done, 4 * it + (s - 8) // 4)
                        elif j == 1:
                            wait(pe, rb_done, 4 * it + (s - 5) // 4)
                        elif j == 0:
                            wait(pe, pt_lo, J)
                        else:
                            wait(pe, pt_lo, J if j == 6 else J - 1)
                        for q in range(4):
                            last = pe.transpose(T_ps[T_BANK[j]][:, 128 * q:128 * q + 128],
                                                P[(j_chunk(s, a)) % 2][:, q, 128 * j:128 * j + 128], k.ident[:, :])
                        last.then_inc(turned, 1)
                    V = 32 * it + (2 * s - 12 + a)
                    v = (2 * s - 12 + a) % 8
                    if exists(V, J_ALL):
                        cpar = ((2 * s - 12 + a) // 8) % 2
                        hpar = ((2 * s - 12 + a) // 16) % 2
                        wait(pe, pt_lo, V + 1)
                        if v == 0:
                            wait(pe, att_done, 4 * it + ((2 * s - 12 + a) // 8 - 1))
                        o = O_ps[cpar]
                        rh, rl = hR[hpar]
                        pe.matmul(o[:, :], rh[:, v, :], PTh[v % 4][:, :], start=(v == 0), stop=False)
                        pe.matmul(o[:, :], rh[:, v, :], PTl[v % 4][:, :], start=False, stop=False)
                        pe.matmul(o[:, :], rl[:, v, :], PTh[v % 4][:, :], start=False, stop=(v == 7)).then_inc(av_done, 1)
                if s % 4 == 0:
                    C = 4 * it + (s - 8) // 4
                    if exists(C, C_ALL):
                        wait(pe, r_ready, C + 1)
                        wait(pe, pt_lo, 8 * C + 7)
                        rd = rden[((s - 8) // 4) % 2]
                        for q in range(4):
                            last = pe.transpose(T_ps[0][:, 128 * q:128 * q + 128], rd[:, q:q + 1].broadcast_to([128, 128]),
                                                k.ident[:, :])
                        last.then_inc(rb_turned, 1)
                if s % 4 == 3:
                    C = 4 * it + (s - 11) // 4
                    if exists(C, C_ALL):
                        wait(pe, cat_done, C + 1)
                        wait(pe, pt_lo, min(8 * C + 13, J_ALL) if isinstance(C, int) else 8 * C + 13)
                        hpar = ((s - 11) // 8) % 2
                        pe.matmul(T_ps[1][0:F, :], w_out[hpar][:, :], cat[((s - 11) // 4) % 2][:, :], start=True,
                                  stop=True).then_inc(h2_done, 1)

            def j_chunk(s, a):
                return (2 * s - 10 + a) // 8

            run(pe, slot)

        @block.scalar
        def _(act):
            def take_hi(r, dst, bank):
                act.wait_ge(s_filled, r + 1)
                act.activation(dst, S_ps[bank][:, :], ACT.Copy).then_inc(h_hi, 1)

            take_hi(0, hT[0][0][:, :], 0)
            take_hi(1, hR[0][0][:, :, :].rearrange("p t d -> p (t d)"), 1)

            def slot(it, s, tail):
                hp, i = s // 8, s % 8
                for a in range(2):
                    J = 32 * it + (2 * s - 10 + a)
                    j = (2 * s - 10 + a) % 8
                    if exists(J, J_ALL):
                        act.wait_ge(turned, J + 1)
                        wait(act, av_done, J - 3)
                        act.activation(PTh[j % 4][:, :], T_ps[T_BANK[j]][:, :], ACT.Copy).then_inc(pt_hi, 1)
                if not tail:
                    r = item(it, hp, s_pos(it, hp, i))
                    c = s // 4
                    act.wait_ge(s_taken, r + 1)
                    if i % 4 == 0:
                        wait(act, turned, 32 * it + 8 * (c - 1))
                    act.activation(P[c % 2][:, i % 4, :], neg[i % 2][:, :], ACT.Exp, bias=nmax[:, i % 2, :], scale=-1.0,
                                   accum_out=den[c % 2][:, i % 4:i % 4 + 1]).then_inc(exp_done, 1)
                    if not (isinstance(it, int) and it == ITERS - 1 and hp == 1):
                        if i == 5:
                            take_hi(item(it, hp, HT_POS), hT[1 - hp][0][:, :], 0)
                        if i == 6:
                            take_hi(item(it, hp, HR_POS), hR[1 - hp][0][:, :, :].rearrange("p t d -> p (t d)"), 0)
                if s % 4 == 0:
                    C = 4 * it + (s - 8) // 4
                    if exists(C, C_ALL):
                        wait(act, rb_turned, C + 1)
                        wait(act, att_done, C)
                        act.activation(rB[:, :], T_ps[0][:, :], ACT.Copy).then_inc(rb_done, 1)

            run(act, slot)

        @block.gpsimd
        def _(pool):
            def slot(it, s, tail):
                if s % 4 == 2:
                    C = 4 * it + (s - 10) // 4
                    if exists(C, C_ALL):
                        par = ((s - 10) // 8) % 2
                        c = cat[((s - 10) // 4) % 2]
                        pool.wait_ge(bo_in[par], 32 * (it + (s - 10) // 16) + 32)
                        wait(pool, h2_done, C - 1)
                        wait(pool, att_done, C + 1)
                        pool.sem_inc(cat_turn, 1)
                        pool.tensor_scalar(pos[:, :], att[:, :], bias[par][:, 0:1], 0.0, ALU.add, ALU.max).then_inc(pool_step, 1)
                        pool.tensor_scalar(c[:, :], att[:, :], bias[par][:, 0:1], 0.01, ALU.add, ALU.mult).then_inc(att_read, 1)
                        wait(pool, pool_step, 2 * C + 1)
                        pool.sem_inc(cat_turn, 1)
                        pool.tensor_scalar(pos[:, :], pos[:, :], 0.99, 1.0, ALU.mult, ALU.mult).then_inc(pool_step, 1)
                        wait(pool, pool_step, 2 * C + 2)
                        pool.tensor_tensor(c[:, :], c[:, :], pos[:, :], ALU.add).then_inc(cat_done, 1)

            run(pool, slot)

        @block.vector
        def _(dve):
            def take_lo(r, hi_count, dst, hi, bank):
                dve.wait_ge(h_hi, hi_count)
                dve.tensor_tensor(dst, S_ps[bank][:, :], hi.bitcast(F32), ALU.subtract).then_inc(s_taken, 1)

            def rows(t):
                return t[:, :, :].rearrange("p t d -> p (t d)")

            dve.memset(k.acc[:, :], 0.0).then_inc(zeroed, 1)
            take_lo(0, 1, hT[0][1][:, :], hT[0][0][:, :], 0)
            take_lo(1, 2, rows(hR[0][1]), rows(hR[0][0]), 1)
            dve.wait_ge(zeroed, 1)

            def slot(it, s, tail):
                hp, i = s // 8, s % 8
                if not tail:
                    r = item(it, hp, s_pos(it, hp, i))
                    wait(dve, exp_done, 16 * it + (s - 1))
                    dve.wait_ge(s_filled, r + 1)
                    dve.sem_inc(max_turn, 1)
                    dve.tensor_tensor_reduce(neg[i % 2][:, :], S_ps[s_pos(it, hp, i) % 2][:, :], k.mask[:, i, :], -1.0, 3.0e38,
                                             ALU.add, ALU.min, nmax[:, i % 2, :]).then_inc(s_taken, 1)
                    if not (isinstance(it, int) and it == ITERS - 1 and hp == 1):
                        if i == 5:
                            take_lo(item(it, hp, HT_POS), 4 * it + 2 * hp + 3, hT[1 - hp][1][:, :], hT[1 - hp][0][:, :], 0)
                        if i == 6:
                            take_lo(item(it, hp, HR_POS), 4 * it + 2 * hp + 4, rows(hR[1 - hp][1]), rows(hR[1 - hp][0]), 0)
                for a in range(2):
                    J = 32 * it + (2 * s - 10 + a)
                    j = (2 * s - 10 + a) % 8
                    if exists(J, J_ALL):
                        dve.wait_ge(pt_hi, J + 1)
                        dve.tensor_tensor(PTl[j % 4][:, :], T_ps[T_BANK[j]][:, :], PTh[j % 4][:, :].bitcast(F32),
                                          ALU.subtract).then_inc(pt_lo, 1)
                if s % 4 == 1:
                    C = 4 * it + (s - 5) // 4
                    if exists(C, C_ALL):
                        wait(dve, exp_done, 4 * C + 4)
                        wait(dve, rb_turned, C - 1)
                        dve.reciprocal(rden[((s - 5) // 4) % 2][:, :], den[((s - 5) // 4) % 2][:, :]).then_inc(r_ready, 1)
                    C = 4 * it + (s - 9) // 4
                    if exists(C, C_ALL):
                        wait(dve, av_done, 8 * C + 8)
                        wait(dve, rb_done, C + 1)
                        wait(dve, att_read, C)
                        dve.tensor_tensor(att[:, :], O_ps[((s - 9) // 4) % 2][:, :], rB[:, :], ALU.mult).then_inc(att_done, 1)
                if s % 4 == 3:
                    C = 4 * it + (s - 11) // 4
                    if exists(C, C_ALL):
                        u2 = (s - 11) // 8
                        at = ((2 * it + u2) // 8) * N + 512 * (((s - 11) // 4) % 2)
                        if isinstance(at, int):
                            dst = k.acc[:, at:at + 512]
                        else:
                            dst = k.acc[:, bass.ds(at, 512)]
                        wait(dve, h2_done, C + 1)
                        dve.tensor_tensor(dst, T_ps[1][0:F, :], dst, ALU.add).then_inc(acc_done, 1)

            run(dve, slot)


def split_output(nc, k, d):
    with ExitStack() as ctx:
        sb, pb, sem = sbuf(nc, ctx, "split_output"), psum(nc, ctx, "split_output"), semaphores(nc, ctx, "split_output")
        hi_lo = [sb(f"hi_lo{i}", [128, N], F32R) for i in range(2)]
        lo_hi = [sb(f"lo_hi{i}", [128, N], F32R) for i in range(2)]
        rows = [sb(f"rows{i}", [128, NT, F]) for i in range(2)]
        r_ps = [pb(f"r_ps{i}", [128, NT, F]) for i in range(2)]
        hi_done, lo_done, turned, rows_done = (sem(n) for n in ("hi_done", "lo_done", "turned", "rows_done"))
        out_d = [sem(f"out_d{i}") for i in range(2)]
        block = ctx.enter_context(nc.Block())

        @block.sync
        def _(sp):
            for b in range(B):
                p = b % 2
                sp.wait_ge(rows_done, b + 1)
                sp.dma_start(d["rows"][b], rows[p][:, :, :]).then_inc(out_d[p], 16)
                sp.wait_ge(lo_done, b + 1)
                sp.dma_start(d["hi_lo"][b], hi_lo[p][:, :].bitcast(F32)).then_inc(out_d[p], 16)
                sp.dma_start(d["lo_hi"][b], lo_hi[p][:, :].bitcast(F32)).then_inc(out_d[p], 16)
            for p in range(2):
                sp.wait_ge(out_d[p], 48 * (B // 2))

        @block.tensor
        def _(pe):
            for b in range(B):
                wait(pe, rows_done, b - 1)
                for t in range(NT):
                    last = pe.transpose(r_ps[b % 2][:, t, :], k.acc[:, N * b + 128 * t:N * b + 128 * t + 128], k.ident[0:64, 0:64])
                last.then_inc(turned, 1)

        @block.scalar
        def _(act):
            for b in range(B):
                p = b % 2
                mine = k.acc[:, N * b:N * b + N]
                wait(act, out_d[p], 48 * (b // 2))
                act.activation(hi_lo[p][0:64, :], mine, ACT.Copy).then_inc(hi_done, 1)
                act.activation(lo_hi[p][64:128, :], mine, ACT.Copy).then_inc(hi_done, 1)

        @block.vector
        def _(dve):
            for b in range(B):
                p = b % 2
                mine = k.acc[:, N * b:N * b + N]
                wait(dve, out_d[p], 48 * (b // 2))
                dve.wait_ge(turned, b + 1)
                dve.tensor_copy(rows[p][:, :, :], r_ps[p][:, :, :]).then_inc(rows_done, 1)
                dve.wait_ge(hi_done, 2 * b + 2)
                hi = hi_lo[p][0:64, :].bitcast(F32)
                dve.tensor_tensor(hi_lo[p][64:128, :], mine, hi, ALU.subtract)
                dve.tensor_tensor(lo_hi[p][0:64, :], mine, hi, ALU.subtract).then_inc(lo_done, 1)


def split_scores(nc, k, a, d):
    with ExitStack() as ctx:
        sb, pb, sem = sbuf(nc, ctx, "split_scores"), psum(nc, ctx, "split_scores"), semaphores(nc, ctx, "split_scores")
        a1 = sb("a1", [F, 1])
        a2 = sb("a2", [F, 1])
        a2_b = sb("a2_b", [F, 128])
        xT = [sb(f"xT{i}", [F, N]) for i in range(2)]
        s2 = [sb(f"s2{i}", [128, N]) for i in range(2)]
        s1 = [sb(f"s1{i}", [128, NT]) for i in range(2)]
        t_ps = pb("t_ps", [F, N])
        s2_ps = [pb(f"s2_ps{i}", [128, N]) for i in range(2)]
        s1_ps = [pb(f"s1_ps{i}", [128, NT]) for i in range(2)]
        a_in, wide, turned, xT_done, s_f, s_done = (sem(n) for n in ("a_in", "wide", "turned", "xT_done", "s_f", "s_done"))
        out_d = [sem(f"out_d{i}") for i in range(2)]
        block = ctx.enter_context(nc.Block())

        @block.sync
        def _(sp):
            sp.dma_start(a1[:, :], a[0:F, :]).then_inc(a_in, 16)
            sp.dma_start(a2[:, :], a[F:2 * F, :]).then_inc(a_in, 16)
            for b in range(B):
                sp.wait_ge(s_done, 2 * b + 2)
                sp.dma_start(d["s2"][b], s2[b % 2][:, :]).then_inc(out_d[b % 2], 16)
                sp.dma_start(d["s1"][b], s1[b % 2][:, :]).then_inc(out_d[b % 2], 16)
            for p in range(2):
                sp.wait_ge(out_d[p], 32 * (B // 2))

        @block.tensor
        def _(pe):
            pe.wait_ge(wide, 1)
            for n in range(B + 1):
                if n < B:
                    wait(pe, xT_done, n)
                    for t in range(NT):
                        last = pe.transpose(t_ps[:, 128 * t:128 * t + 128], k.x[:, NT * n + t, :], k.ident[:, :])
                    last.then_inc(turned, 1)
                b = n - 1
                if b >= 0:
                    pe.wait_ge(xT_done, b + 1)
                    wait(pe, s_done, 2 * (b - 1))
                    for c in range(2):
                        pe.matmul(s2_ps[b % 2][:, 512 * c:512 * c + 512], a2_b[:, :], xT[b % 2][:, 512 * c:512 * c + 512],
                                  start=True, stop=True)
                    for t in range(NT):
                        last = pe.matmul(s1_ps[b % 2][:, t:t + 1], xT[b % 2][:, 128 * t:128 * t + 128], a1[:, :],
                                         start=True, stop=True)
                    last.then_inc(s_f, 1)

        @block.scalar
        def _(act):
            for b in range(B):
                act.wait_ge(turned, b + 1)
                wait(act, s_f, b - 1)
                act.activation(xT[b % 2][:, :], t_ps[:, :], ACT.Copy).then_inc(xT_done, 1)

        @block.vector
        def _(dve):
            dve.wait_ge(a_in, 32)
            dve.tensor_copy(a2_b[:, :], a2[:, 0:1].broadcast_to([F, 128])).then_inc(wide, 1)
            for b in range(B):
                dve.wait_ge(s_f, b + 1)
                wait(dve, out_d[b % 2], 32 * (b // 2))
                dve.tensor_copy(s2[b % 2][:, :], s2_ps[b % 2][:, :]).then_inc(s_done, 1)
                dve.tensor_copy(s1[b % 2][:, :], s1_ps[b % 2][:, :]).then_inc(s_done, 1)


def attention(nc, k, stage, products, d, b_out=None):
    ITERS = B // 2
    J_ALL, C_ALL = B * 16, B * 2
    with ExitStack() as ctx:
        sb, pb, sem = sbuf(nc, ctx, stage), psum(nc, ctx, stage), semaphores(nc, ctx, stage)
        if products:
            ops = [[sb(f"{n}{i}", [128, N], F32R) for n in ("hi_lo", "lo_hi")] for i in range(2)]
            S_ps = [pb(f"S_ps{i}", [128, N]) for i in range(2)]
            bias = sb("bias", [128, F])
        else:
            s2 = [sb(f"s2_{i}", [128, N]) for i in range(2)]
            s1 = [sb(f"s1_{i}", [128, NT]) for i in range(2)]
            z = [sb(f"z{i}", [128, N]) for i in range(2)]
            leaky = [sb(f"leaky{i}", [128, N]) for i in range(2)]
        rows = [sb(f"rows{i}", [128, NT, F]) for i in range(2)]
        neg = [sb(f"neg{i}", [128, N]) for i in range(2)]
        nmax = sb("nmax", [128, 2, 1])
        P = [sb(f"P{i}", [128, 4, N]) for i in range(2)]
        den = [sb(f"den{i}", [128, 4]) for i in range(2)]
        rden = [sb(f"rden{i}", [128, 4]) for i in range(2)]
        PT = [sb(f"PT{i}", [128, 512]) for i in range(4)]
        att = [sb(f"att{i}", [F, 512]) for i in range(2)]
        o1 = [sb(f"o1{i}", [128, 4, F]) for i in range(2)]
        low = sb("low", [128, 4, F])
        elow = sb("elow", [128, 4, F])
        up = sb("up", [128, 4, F])
        T_ps = [pb(f"T_ps{i}", [128, 512]) for i in range(2)]
        O_ps = pb("O_ps", [F, 512])
        F_ps = pb("F_ps", [128, 4, F])
        op_in = [sem(f"op_in{i}") for i in range(2)]
        pt_done = [sem(f"pt_done{i}") for i in range(2)]
        (bias_in, s_filled, s_taken, z_done, leaky_done, exp_done, turned, av_done, att_done, f_turned, r_ready, o1_done,
         low_done, elow_done, out_step, out_turn, max_turn, f_turn, x_done) = (sem(n) for n in (
            "bias_in", "s_filled", "s_taken", "z_done", "leaky_done", "exp_done", "turned", "av_done", "att_done",
            "f_turned", "r_ready", "o1_done", "low_done", "elow_done", "out_step", "out_turn", "max_turn", "f_turn", "x_done"))
        block = ctx.enter_context(nc.Block())

        def exists(i, n):
            return not isinstance(i, int) or 0 <= i < n

        def run(eng, slot):
            for s in range(16):
                slot(0, s)
            with eng.Fori(1, ITERS - 1) as it:
                for s in range(16):
                    slot(it, s)
            for s in range(16):
                slot(ITERS - 1, s)
            for s in range(9):
                slot(ITERS, s)

        @block.sync
        def _(sp):
            def load(b, par):
                wait(sp, av_done, 16 * (b - 1))
                if products:
                    for n, name in enumerate(("hi_lo", "lo_hi")):
                        sp.dma_start(ops[par][n][:, :].bitcast(F32), one(d[name][bass.ds(b, 1)])).then_inc(op_in[par], 16)
                    sp.dma_start(rows[par][:, :, :].rearrange("p t c -> p (t c)"),
                                 d["rows"][bass.ds(b, 1)].rearrange("o p t c -> (o p) (t c)")).then_inc(op_in[par], 16)
                else:
                    sp.dma_start(s2[par][:, :], one(d["s2"][bass.ds(b, 1)])).then_inc(op_in[par], 16)
                    sp.dma_start(s1[par][:, :], one(d["s1"][bass.ds(b, 1)])).then_inc(op_in[par], 16)
                    sp.dma_start(rows[par][:, :, :],
                                 d["x"][bass.ds(b, 1)].rearrange("o (t p) c -> (o p) t c", p=128)).then_inc(op_in[par], 16)

            if products:
                sp.dma_start(bias[:, :], b_out.rearrange("(o f) -> o f", o=1).broadcast_to([128, F])).then_inc(bias_in, 16)
            load(0, 0)
            load(1, 1)
            with sp.Fori(1, ITERS) as it:
                load(2 * it, 0)
                load(2 * it + 1, 1)

        T_PAR = [0, 1]

        @block.tensor
        def _(pe):
            def slot(it, s):
                G = 16 * it + s
                hp, i = s // 8, s % 8
                if exists(G, 8 * B):
                    if i == 0:
                        pe.wait_ge(op_in[hp], 48 * it + 48)
                    if products:
                        wait(pe, s_taken, G - 1)
                        tile = slice(128 * i, 128 * i + 128)
                        for n in range(2):
                            for c in range(2):
                                ch = slice(512 * c, 512 * c + 512)
                                last = pe.matmul(S_ps[i % 2][:, ch], ops[hp][0][:, tile], ops[hp][n][:, ch], start=(n == 0),
                                                 stop=(n == 1))
                        last.then_inc(s_filled, 1)
                for a in range(2):
                    J = 32 * it + (2 * s - 10 + a)
                    j = (2 * s - 10 + a) % 8
                    if exists(J, J_ALL):
                        if j == 0:
                            wait(pe, exp_done, 16 * it + 4 * ((2 * s - 10 + a) // 8) + 4)
                        wait(pe, pt_done[a], 16 * it + (2 * s - 10) // 2)
                        for q in range(4):
                            last = pe.transpose(T_ps[a][:, 128 * q:128 * q + 128],
                                                P[((2 * s - 10 + a) // 8) % 2][:, q, 128 * j:128 * j + 128], k.ident[:, :])
                        last.then_inc(turned, 1)
                    V = 32 * it + (2 * s - 12 + a)
                    v = (2 * s - 12 + a) % 8
                    if exists(V, J_ALL):
                        hpar = ((2 * s - 12 + a) // 16) % 2
                        wait(pe, pt_done[a], 16 * it + (2 * s - 12) // 2 + 1)
                        if v == 0:
                            wait(pe, att_done, 4 * it + (2 * s - 12) // 8)
                        pe.matmul(O_ps[:, :], rows[hpar][:, v, :], PT[v % 4][:, :], start=(v == 0),
                                  stop=(v == 7)).then_inc(av_done, 1)
                if s % 4 == 2:
                    C = 4 * it + (s - 10) // 4
                    if exists(C, C_ALL):
                        wait(pe, att_done, C + 1)
                        wait(pe, o1_done, C)
                        pe.sem_inc(f_turn, 1)
                        for q in range(4):
                            last = pe.transpose(F_ps[:, q, :], att[((s - 10) // 4) % 2][:, 128 * q:128 * q + 128],
                                                k.ident[0:64, 0:64])
                        last.then_inc(f_turned, 1)

            run(pe, slot)

        @block.scalar
        def _(act):
            def take(it, s, a):
                J = 32 * it + (2 * s - 10 + a)
                if exists(J, J_ALL):
                    act.wait_ge(turned, J + 1)
                    wait(act, av_done, J - 3)
                    act.activation(PT[(2 * s - 10 + a) % 4][:, :], T_ps[a][:, :], ACT.Copy).then_inc(pt_done[a], 1)

            def scores(it, s):
                G = 16 * it + s
                hp, i = (s // 8) % 2, s % 8
                if exists(G, 8 * B):
                    if i == 0:
                        act.wait_ge(op_in[hp], 48 * (it + s // 16) + 48)
                    wait(act, leaky_done, G - 1)
                    act.activation(z[i % 2][:, :], s2[hp][:, :], ACT.Identity, bias=s1[hp][:, i:i + 1]).then_inc(z_done, 1)

            if not products:
                scores(0, 0)

            def slot(it, s):
                G = 16 * it + s
                hp, i = s // 8, s % 8
                if s % 4 == 2:
                    C = 4 * it + (s - 10) // 4
                    if exists(C, C_ALL):
                        act.wait_ge(av_done, 8 * C + 8)
                        wait(act, f_turned, C - 1)
                        act.activation(att[((s - 10) // 4) % 2][:, :], O_ps[:, :], ACT.Copy).then_inc(att_done, 1)
                take(it, s, 0)
                if not products:
                    scores(it, s + 1)
                if exists(G, 8 * B):
                    act.wait_ge(s_taken, G + 1)
                    if i % 4 == 0:
                        wait(act, turned, 32 * it + 8 * (s // 4 - 1))
                    act.activation(P[(s // 4) % 2][:, i % 4, :], neg[i % 2][:, :], ACT.Exp, bias=nmax[:, i % 2, :], scale=-1.0,
                                   accum_out=den[(s // 4) % 2][:, i % 4:i % 4 + 1]).then_inc(exp_done, 1)
                if s % 4 == 0 and not products:
                    C = 4 * it + (s - 12) // 4
                    if exists(C, C_ALL):
                        act.wait_ge(low_done, C + 1)
                        act.activation(elow[:, :, :], low[:, :, :], ACT.Exp).then_inc(elow_done, 1)

            run(act, slot)

        @block.gpsimd
        def _(pool):
            if products:
                pool.wait_ge(bias_in, 16)

            def slot(it, s):
                if s % 4 == 3:
                    C = 4 * it + (s - 11) // 4
                    if exists(C, C_ALL):
                        o = o1[((s - 11) // 4) % 2]
                        xs = k.x[:, bass.ds(4 * C, 4), :]
                        pool.wait_ge(o1_done, C + 1)
                        if products:
                            pool.sem_inc(out_turn, 1)
                            pool.tensor_tensor(low[:, :, :], o[:, :, :], bias[:, :].unsqueeze(1).broadcast_to([128, 4, F]),
                                               ALU.add).then_inc(out_step, 1)
                            pool.wait_ge(out_step, 3 * C + 1)
                            pool.sem_inc(out_turn, 1)
                            pool.tensor_scalar(up[:, :, :], low[:, :, :], 0.0, 0.99, ALU.max, ALU.mult)
                            pool.tensor_scalar(elow[:, :, :], low[:, :, :], 0.01, 1.0, ALU.mult, ALU.mult).then_inc(out_step, 1)
                            pool.wait_ge(out_step, 3 * C + 2)
                        else:
                            wait(pool, elow_done, C)
                            pool.sem_inc(out_turn, 1)
                            pool.tensor_scalar(low[:, :, :], o[:, :, :], 0.0, 0.0, ALU.min, ALU.add).then_inc(low_done, 1)
                            pool.tensor_scalar(up[:, :, :], o[:, :, :], 0.0, -1.0, ALU.max, ALU.add).then_inc(out_step, 1)
                            pool.wait_ge(out_step, 2 * C + 1)
                            pool.wait_ge(elow_done, C + 1)
                        pool.sem_inc(out_turn, 1)
                        pool.tensor_tensor(up[:, :, :], up[:, :, :], elow[:, :, :], ALU.add).then_inc(out_step, 1)
                        pool.wait_ge(out_step, (3 if products else 2) * (C + 1))
                        pool.sem_inc(out_turn, 1)
                        pool.tensor_tensor(xs, xs, up[:, :, :], ALU.add).then_inc(x_done, 1)
                        pool.wait_ge(x_done, C + 1)

            run(pool, slot)

        @block.vector
        def _(dve):
            def slot(it, s):
                G = 16 * it + s
                i = s % 8
                if exists(G, 8 * B):
                    if not products:
                        dve.wait_ge(z_done, G + 1)
                        wait(dve, s_taken, G - 1)
                        dve.scalar_tensor_tensor(out=leaky[i % 2][:, :], in0=z[i % 2][:, :], scalar=0.2, in1=z[i % 2][:, :],
                                                 op0=ALU.mult, op1=ALU.max).then_inc(leaky_done, 1)
                for a in ([1] if products else [1]):
                    J = 32 * it + (2 * s - 10 + a)
                    if exists(J, J_ALL) and not products:
                        dve.wait_ge(turned, J + 1)
                        wait(dve, av_done, J - 3)
                        dve.tensor_copy(PT[(2 * s - 10 + a) % 4][:, :], T_ps[a][:, :]).then_inc(pt_done[a], 1)
                if exists(G, 8 * B):
                    wait(dve, exp_done, G - 1)
                    dve.wait_ge(s_filled if products else leaky_done, G + 1)
                    dve.sem_inc(max_turn, 1)
                    dve.tensor_tensor_reduce(neg[i % 2][:, :], S_ps[i % 2][:, :] if products else leaky[i % 2][:, :],
                                             k.mask[:, i, :], -1.0, 3.0e38, ALU.add, ALU.min, nmax[:, i % 2, :]).then_inc(s_taken, 1)
                J = 32 * it + (2 * s - 10 + 1)
                if exists(J, J_ALL) and products:
                    dve.wait_ge(turned, J + 1)
                    wait(dve, av_done, J - 3)
                    dve.tensor_copy(PT[(2 * s - 10 + 1) % 4][:, :], T_ps[1][:, :]).then_inc(pt_done[1], 1)
                if s % 4 == 1:
                    C = 4 * it + (s - 5) // 4
                    if exists(C, C_ALL):
                        wait(dve, exp_done, 4 * C + 4)
                        wait(dve, o1_done, C - 1)
                        dve.reciprocal(rden[((s - 5) // 4) % 2][:, :], den[((s - 5) // 4) % 2][:, :]).then_inc(r_ready, 1)
                if s % 4 == 3:
                    C = 4 * it + (s - 11) // 4
                    if exists(C, C_ALL):
                        q = ((s - 11) // 4) % 2
                        dve.wait_ge(f_turned, C + 1)
                        dve.wait_ge(r_ready, C + 1)
                        wait(dve, x_done, C - 1)
                        dve.tensor_tensor(o1[q][:, :, :], F_ps[:, :, :], rden[q][:, :].unsqueeze(2).broadcast_to([128, 4, F]),
                                          ALU.mult).then_inc(o1_done, 1)

            run(dve, slot)


def causal(nc, k, w):
    PAIRS = B // 2
    STEPS = 3
    R = STEPS * PAIRS
    with ExitStack() as ctx:
        sb, pb, sem = sbuf(nc, ctx, "causal"), psum(nc, ctx, "causal"), semaphores(nc, ctx, "causal")
        w1v, w1e, w2 = (sb(n, [128, 128]) for n in ("w1v", "w1e", "w2"))
        b1 = sb("b1", [128, 1])
        b2 = sb("b2", [128, 1])
        b2_b = sb("b2_b", [128, 128])
        given = sb("given", [1, F])
        v = sb("v", [128, NT, B, F])
        v_hi = sb("v_hi", [128, NT, B, F], F32R)
        v_lo = sb("v_lo", [128, NT, B, F], F32R)
        vT = [sb(f"vT{p}", [128, N]) for p in range(PAIRS)]
        eff = [sb(f"eff{i}", [128, N]) for i in range(2)]
        h = [sb(f"h{i}", [128, N]) for i in range(2)]
        e_ps = [pb(f"e_ps{i}", [128, N]) for i in range(2)]
        h_ps = pb("h_ps", [128, N])
        v_ps = pb("v_ps", [128, N])
        (zeroed, w_in, given_in, v_copied, given_set, v_hi_done, v_lo_done, vT_turned, vT_taken, e_f, e_done, h_f, h_done, vT_f,
         vT_done, v_f, v_done, x_done) = (sem(n) for n in (
            "zeroed", "w_in", "given_in", "v_copied", "given_set", "v_hi_done", "v_lo_done", "vT_turned", "vT_taken", "e_f",
            "e_done", "h_f", "h_done", "vT_f", "vT_done", "v_f", "v_done", "x_done"))
        block = ctx.enter_context(nc.Block())

        def of_pair(t, p):
            return t[:, :, 2 * p:2 * p + 2, :]

        @block.sync
        def _(sp):
            sp.dma_start(given[:, :], w["intervention"]).then_inc(given_in, 16)
            for half in range(2):
                s = slice(64 * half, 64 * half + 64)
                sp.dma_start(b1[s, :], w["b1"].rearrange("(p o) -> p o", o=1)).then_inc(w_in, 16)
                sp.dma_start(b2[s, :], w["b2"].rearrange("(p o) -> p o", o=1)).then_inc(w_in, 16)
                sp.dma_start(b2_b[:, s], w["b2"].rearrange("(o f) -> o f", o=1).broadcast_to([128, F])).then_inc(w_in, 16)
            sp.wait_ge(zeroed, 3)
            for half in range(2):
                s = slice(64 * half, 64 * half + 64)
                sp.dma_start(w1v[s, s], w["W1T"][0:F, :]).then_inc(w_in, 16)
                sp.dma_start(w1e[s, s], w["W1T"][F:2 * F, :]).then_inc(w_in, 16)
                sp.dma_start(w2[s, s], w["W2T"]).then_inc(w_in, 16)

        @block.gpsimd
        def _(pool):
            for t in (w1v, w1e, w2):
                pool.memset(t[:, :], 0.0).then_inc(zeroed, 1)
            for p in range(PAIRS):
                q = R - PAIRS + p
                pool.wait_ge(v_done, q + 1)
                for b in (2 * p, 2 * p + 1):
                    xb = k.x[:, NT * b:NT * b + NT, :]
                    pool.tensor_tensor(xb, xb, v[:, :, b, :], ALU.add).then_inc(x_done, 1)

        @block.tensor
        def _(pe):
            for p in range(PAIRS):
                pe.wait_ge(given_set, 1)
                for t in range(NT):
                    last = pe.transpose((e_ps[p % 2] if p < 2 else (h_ps, v_ps)[p % 2])[:, 128 * t:128 * t + 128],
                                        of_pair(v, p)[:, t].rearrange("p b c -> p (b c)"), k.ident[:, :])
                last.then_inc(vT_turned, 1)
            pe.wait_ge(w_in, 16 * 12)
            pe.wait_ge(vT_taken, PAIRS)
            for n in range(R + 2):
                if n < R:
                    p = n % PAIRS
                    pe.wait_ge(v_hi_done, n + 1)
                    pe.wait_ge(v_lo_done, n + 1)
                    wait(pe, e_done, n - 1)
                    for t in range(NT):
                        for m, part in enumerate((v_hi, v_lo)):
                            for c in range(2):
                                last = pe.matmul(e_ps[n % 2][:, 512 * c:512 * c + 512],
                                                 of_pair(part, p)[:, t].rearrange("p b c -> p (b c)"),
                                                 k.adjT[:, t, 512 * c:512 * c + 512], start=(t == 0 and m == 0),
                                                 stop=(t == NT - 1 and m == 1))
                    last.then_inc(e_f, 1)
                q = n - 1
                if 0 <= q < R:
                    pe.wait_ge(e_done, q + 1)
                    wait(pe, h_done, q)
                    wait(pe, vT_done, q - PAIRS + 1)
                    for m in range(2):
                        for c in range(2):
                            ch = slice(512 * c, 512 * c + 512)
                            last = pe.matmul(h_ps[:, ch], (w1v, w1e)[m][:, :], (vT[q % PAIRS], eff[q % 2])[m][:, ch],
                                             start=(m == 0), stop=(m == 1))
                    last.then_inc(h_f, 1)
                q = n - 2
                if 0 <= q < R:
                    pe.wait_ge(h_done, q + 1)
                    wait(pe, v_done, q)
                    if q < R - PAIRS:
                        for c in range(2):
                            ch = slice(512 * c, 512 * c + 512)
                            last = pe.matmul(v_ps[:, ch], w2[:, :], h[q % 2][:, ch], start=True, stop=True)
                        last.then_inc(vT_f, 1)
                        pe.wait_ge(vT_done, q + 1)
                    for t in range(NT):
                        last = pe.matmul(v_ps[:, 128 * t:128 * t + 128], h[q % 2][:, 128 * t:128 * t + 128], w2[:, :],
                                         start=True, stop=True)
                    last.then_inc(v_f, 1)

        @block.scalar
        def _(act):
            act.wait_ge(given_set, 1)
            for p in range(PAIRS):
                act.activation(of_pair(v_hi, p), of_pair(v, p), ACT.Copy).then_inc(v_hi_done, 1)
            act.wait_ge(w_in, 16 * 12)
            for n in range(R + 2):
                if n < R:
                    act.wait_ge(e_f, n + 1)
                    wait(act, h_f, n - 1)
                    act.activation(eff[n % 2][:, :], e_ps[n % 2][:, :], ACT.Copy).then_inc(e_done, 1)
                q = n - 1
                if 0 <= q < R:
                    act.wait_ge(h_f, q + 1)
                    wait(act, v_f, q - 1)
                    act.activation(h[q % 2][:, :], h_ps[:, :], ACT.Relu, bias=b1[:, 0:1]).then_inc(h_done, 1)
                q = n - 2
                if 0 <= q < R - PAIRS:
                    act.wait_ge(vT_f, q + 1)
                    act.activation(vT[q % PAIRS][:, :], v_ps[:, :], ACT.Identity, bias=b2[:, 0:1]).then_inc(vT_done, 1)
                    act.wait_ge(v_done, q + 1)
                    act.activation(of_pair(v_hi, q % PAIRS), of_pair(v, q % PAIRS), ACT.Copy).then_inc(v_hi_done, 1)

        @block.vector
        def _(dve):
            dve.tensor_copy(v[:, :, :, :].rearrange("p t b c -> p b t c"),
                            k.x[:, :, :].rearrange("p (b t) c -> p b t c", b=B)).then_inc(v_copied, 1)
            dve.wait_ge(v_copied, 1)
            dve.wait_ge(given_in, 16)
            dve.tensor_copy(v[0:1, 0, :, :], given[:, :].unsqueeze(1).broadcast_to([1, B, F])).then_inc(given_set, 1)
            for p in range(PAIRS):
                dve.wait_ge(v_hi_done, p + 1)
                dve.wait_ge(given_set, 1)
                dve.tensor_tensor(of_pair(v_lo, p), of_pair(v, p), of_pair(v_hi, p).bitcast(F32), ALU.subtract).then_inc(v_lo_done, 1)
            for p in range(PAIRS):
                dve.wait_ge(vT_turned, p + 1)
                dve.tensor_copy(vT[p][:, :], (e_ps[p % 2] if p < 2 else (h_ps, v_ps)[p % 2])[:, :]).then_inc(vT_taken, 1)
            dve.wait_ge(w_in, 16 * 12)
            for q in range(R):
                dve.wait_ge(v_f, q + 1)
                dve.tensor_tensor(of_pair(v, q % PAIRS), v_ps[:, :].rearrange("p (t b c) -> p t b c", t=NT, b=2),
                                  b2_b[:, :].rearrange("p (b c) -> p b c", b=2).unsqueeze(1).broadcast_to([128, NT, 2, F]),
                                  ALU.add).then_inc(v_done, 1)
                if q < R - PAIRS:
                    dve.wait_ge(v_hi_done, PAIRS + q + 1)
                    dve.tensor_tensor(of_pair(v_lo, q % PAIRS), of_pair(v, q % PAIRS), of_pair(v_hi, q % PAIRS).bitcast(F32),
                                      ALU.subtract).then_inc(v_lo_done, 1)


def program(nc, a, out):
    with ExitStack() as ctx:
        sb = sbuf(nc, ctx, "program")
        k = Shared()
        k.ident = sb("ident", [128, 128])
        k.x = sb("x", [128, B * NT, F])
        k.mask = sb("mask", [128, NT, N], BF16)
        k.adjT = sb("adjT", [128, NT, N], F32R)

        def scratch(name, shape):
            return nc.dram_tensor(name, shape, F32, kind="Internal").ap()

        d = {"hT": scratch("hT_d", [B, 128, N]), "beta": scratch("beta_d", [B, 128, N]), "coef": scratch("coef_d", [B, 128, N]),
             "agg": scratch("agg_d", [B, 128, 3, EDGES // 2]), "g": scratch("g_d", [B, F, N]), "ind": scratch("ind_d", [B, F, N])}
        w = {"W": a["L0_gnn_W"], "a_node": a["L0_gnn_a_node"], "a_gn": a["L0_gnn_a_gn"], "a_ge": a["L0_gnn_a_ge"],
             "fcW": a["L0_gnn_fcW"], "fcb": a["L0_gnn_fcb"], "av": a["L0_gnn_av"]}
        with ExitStack() as hyper:
            sb = sbuf(nc, hyper, "hypergraph")
            k.two = sb("two", [128, 64])
            k.mask_ne = sb("mask_ne", [128, NT, EDGES], BF16)
            k.mask_en = sb("mask_en", [EDGES, N], BF16)
            setup(nc, k, a["x"], a["adj"], a["adjT"], a["L0_gnn_H"], a["HT"])
            industry(nc, k, a["xT"], a["L0_gnn_W_ind"], d["ind"])
            hyperedges(nc, k, a["xT"], w, d)
            messages(nc, k, d)
            mix(nc, k, w, d)
        x_d = scratch("x_d", [B, N, F])
        layernorm(nc, k, "norm0", x_d)

        with ExitStack() as graph:
            k.acc = graph.enter_context(nc.sbuf_tensor("acc", [F, B * N], F32))
            xs_d = scratch("xs_d", [B, 128, N])
            ws_d = scratch("ws_d", [HEADS, 128, 2, D])
            d["rows"], d["hi_lo"], d["lo_hi"] = scratch("rows_d", [B, 128, NT, F]), scratch("hi_lo_d", [B, 128, N]), scratch("lo_hi_d", [B, 128, N])
            split_heads(nc, k, a["L1_gnn_Wh"], xs_d, ws_d)
            heads(nc, k, xs_d, ws_d, a["L1_gnn_bh"], a["L1_gnn_W_out"].rearrange("(h d) f -> h d f", h=HEADS))
            split_output(nc, k, d)
            attention(nc, k, "output_layer", True, d, a["L1_gnn_b_out"])
        layernorm(nc, k, "norm1", x_d)

        d["x"], d["s2"], d["s1"] = x_d, scratch("s2_d", [B, 128, N]), scratch("s1_d", [B, 128, NT])
        split_scores(nc, k, a["L2_gnn_a"], d)
        attention(nc, k, "threshold_layer", False, d)
        layernorm(nc, k, "norm2", x_d)

        causal(nc, k, {"intervention": a["L3_gnn_intervention_value"], "W1T": a["W1T"], "W2T": a["W2T"],
                       "b1": a["L3_gnn_b1"], "b2": a["L3_gnn_b2"]})
        layernorm(nc, k, "norm3", out)


_INS = ['x', 'adj', 'L0_gnn_H', 'L0_gnn_W', 'L0_gnn_W_ind', 'L0_gnn_a_node', 'L0_gnn_a_gn', 'L0_gnn_a_ge', 'L0_gnn_fcW', 'L0_gnn_fcb',
        'L0_gnn_av', 'L1_gnn_Wh', 'L1_gnn_bh', 'L1_gnn_W_out', 'L1_gnn_b_out', 'L2_gnn_a', 'L3_gnn_intervention_value',
        'L3_gnn_W1', 'L3_gnn_b1', 'L3_gnn_W2', 'L3_gnn_b2']


def kernel(**inputs):
    import numpy as _np
    import concourse.bacc as _bacc
    from concourse import mybir as _mybir
    from concourse.bass_utils import run_bass_kernel_spmd as _run

    given = {name: _np.asarray(inputs[name]) for name in _INS}
    given["xT"] = given["x"].transpose(0, 2, 1)
    given["adjT"] = given["adj"].T
    given["HT"] = given["L0_gnn_H"].T
    given["W1T"] = given.pop("L3_gnn_W1").T
    given["W2T"] = given.pop("L3_gnn_W2").T
    nc = _bacc.Bacc("TRN2", target_bir_lowering=False, num_devices=1)
    arrays, args = {}, {}
    for name, v in given.items():
        v = _np.ascontiguousarray(v)
        arrays[f"in_{name}_dram"] = v
        args[name] = nc.dram_tensor(f"in_{name}_dram", v.shape, _mybir.dt.from_np(v.dtype), kind="ExternalInput").ap()
    out = nc.dram_tensor("out_0_dram", (B, N, F), _mybir.dt.float32, kind="ExternalOutput").ap()
    program(nc, args, out)
    r = _run(nc, [arrays], core_ids=[0])
    return r.results[0]["out_0_dram"]
```

```python
import concourse.bass as bass
from concourse import mybir
from contextlib import ExitStack

F32 = mybir.dt.float32
F32R = mybir.dt.float32r
BF16 = mybir.dt.bfloat16
ALU = mybir.AluOpType
ACT = mybir.ActivationFunctionType
AX_X = mybir.AxisListType.X

B, N, F = 8, 1024, 64
HEADS, D = 8, 128
EDGES = 64
NT = N // 128
MASKED = -1e30
EPS = 1e-5
LEAK = 0.01
LEAK_UP = 1.0 - LEAK




class Shared:
    pass


def wait(eng, sem, value):
    if not isinstance(value, int) or value > 0:
        eng.wait_ge(sem, value)


def sbuf(nc, ctx, stage):
    return lambda name, shape, dt=F32: ctx.enter_context(nc.sbuf_tensor(f"{stage}_{name}", shape, dt))


def psum(nc, ctx, stage):
    return lambda name, shape, dt=F32: ctx.enter_context(nc.psum_tensor(f"{stage}_{name}", shape, dt))


def semaphores(nc, ctx, stage):
    mine = []
    ctx.callback(lambda: (nc.all_engine_barrier(), nc.clear_and_free_semaphores(mine), nc.all_engine_barrier()))

    def new(name):
        mine.append(nc.alloc_semaphore(name=f"{stage}_{name}"))
        return mine[-1]
    return new


def one(ap):
    return ap.rearrange("o p n -> (o p) n")


def setup(nc, k, x, adj, adjT, H, HT):
    with ExitStack() as ctx:
        sb, sem = sbuf(nc, ctx, "setup"), semaphores(nc, ctx, "setup")
        raw = [sb(f"raw{i}", [128, NT, N]) for i in range(2)]
        raw_h = sb("raw_h", [128, NT, EDGES])
        raw_ht = sb("raw_ht", [EDGES, N])
        x_in, adj_in, adjT_in, h_in, ident_step, two_step = (sem(n) for n in (
            "x_in", "adj_in", "adjT_in", "h_in", "ident_step", "two_step"))
        block = ctx.enter_context(nc.Block())

        @block.sync
        def _(sp):
            sp.dma_start(raw[0][:, :, :], adj.rearrange("(t p) m -> p t m", p=128)).then_inc(adj_in, 16)
            sp.dma_start(raw_h[:, :, :], H.rearrange("(t p) e -> p t e", p=128)).then_inc(h_in, 16)
            sp.dma_start(raw_ht[:, :], HT).then_inc(h_in, 16)
            sp.dma_start(k.x[:, :, :], x.rearrange("b (t p) c -> p (b t) c", p=128)).then_inc(x_in, 16)
            sp.wait_ge(x_in, 16)

        @block.scalar
        def _(act):
            act.dma_start(raw[1][:, :, :], adjT.rearrange("(t p) n -> p t n", p=128)).then_inc(adjT_in, 16)
            act.wait_ge(adjT_in, 16)
            act.activation(k.adjT[:, :, :], raw[1][:, :, :], ACT.Copy)

        @block.gpsimd
        def _(pool):
            pool.memset(k.ident[:, :], 1.0).then_inc(ident_step, 1)
            pool.wait_ge(ident_step, 1)
            pool.affine_select(out=k.ident[:, :], in_=k.ident[:, :], compare_op=ALU.is_equal, fill=0.0, base=0,
                               pattern=[[-1, 128]], channel_multiplier=1).then_inc(ident_step, 1)

        @block.vector
        def _(dve):
            dve.wait_ge(h_in, 32)
            dve.tensor_scalar(k.mask_ne[:, :, :], raw_h[:, :, :], 0.0, MASKED, ALU.is_le, ALU.mult)
            dve.tensor_scalar(k.mask_en[:, :], raw_ht[:, :], 0.0, MASKED, ALU.is_le, ALU.mult)
            dve.wait_ge(ident_step, 2)
            dve.tensor_copy(k.two[0:64, :], k.ident[0:64, 0:64]).then_inc(two_step, 1)
            dve.tensor_copy(k.two[64:128, :], k.ident[64:128, 64:128]).then_inc(two_step, 1)
            dve.wait_ge(adj_in, 16)
            dve.tensor_scalar(k.mask[:, :, :], raw[0][:, :, :], 0.0, MASKED, ALU.is_equal, ALU.mult)


def layernorm(nc, k, stage, x_d):
    Q = 4
    G = B * NT // Q
    with ExitStack() as ctx:
        sb, sem = sbuf(nc, ctx, stage), semaphores(nc, ctx, stage)
        total = sb("total", [128, Q, G])
        mean = sb("mean", [128, Q, G])
        square = [sb(f"square{i}", [128, G, F]) for i in range(2)]
        spread = sb("spread", [128, Q, G])
        var = sb("var", [128, Q, G])
        std = sb("std", [128, Q, G])
        rstd = sb("rstd", [128, Q, G])
        summed, meant, centred, squared, spread_done, var_done, std_done, rstd_done, scaled, out_d = (sem(n) for n in (
            "summed", "meant", "centred", "squared", "spread_done", "var_done", "std_done", "rstd_done", "scaled",
            "out_d"))
        block = ctx.enter_context(nc.Block())

        def part(q):
            return k.x[:, G * q:G * q + G, :]

        def wide(t, q):
            return t[:, q, :].unsqueeze(2).broadcast_to([128, G, F])

        @block.sync
        def _(sp):
            per = B // Q
            for q in range(Q):
                sp.wait_ge(scaled, q + 1)
                sp.dma_start(x_d[per * q:per * q + per].rearrange("b (t p) c -> p (b t) c", p=128), part(q)).then_inc(out_d, 16)
            sp.wait_ge(out_d, 16 * Q)

        @block.scalar
        def _(act):
            for q in range(Q):
                act.wait_ge(centred, q + 1)
                if q >= 2:
                    act.wait_ge(spread_done, q - 1)
                act.activation(square[q % 2][:, :, :], part(q), ACT.Square).then_inc(squared, 1)
            act.wait_ge(var_done, 1)
            act.activation(std[:, :, :], var[:, :, :], ACT.Sqrt).then_inc(std_done, 1)

        @block.vector
        def _(dve):
            for q in range(Q):
                dve.reduce_sum(total[:, q, :], part(q), axis=AX_X).then_inc(summed, 1)
            dve.wait_ge(summed, Q)
            dve.tensor_scalar(mean[:, :, :], total[:, :, :], 1.0 / F, None, ALU.mult).then_inc(meant, 1)
            dve.wait_ge(meant, 1)
            for q in range(Q):
                dve.tensor_tensor(part(q), part(q), wide(mean, q), ALU.subtract).then_inc(centred, 1)
            for q in range(Q):
                dve.wait_ge(squared, q + 1)
                dve.reduce_sum(spread[:, q, :], square[q % 2][:, :, :], axis=AX_X).then_inc(spread_done, 1)
            dve.wait_ge(spread_done, Q)
            dve.tensor_scalar(var[:, :, :], spread[:, :, :], 1.0 / F, EPS, ALU.mult, ALU.add).then_inc(var_done, 1)
            dve.wait_ge(std_done, 1)
            dve.reciprocal(rstd[:, :, :], std[:, :, :]).then_inc(rstd_done, 1)
            dve.wait_ge(rstd_done, 1)
            for q in range(Q):
                dve.tensor_tensor(part(q), part(q), wide(rstd, q), ALU.mult).then_inc(scaled, 1)


def industry(nc, k, xT, W_ind, ind_d):
    with ExitStack() as ctx:
        sb, pb, sem = sbuf(nc, ctx, "industry"), psum(nc, ctx, "industry"), semaphores(nc, ctx, "industry")
        xT_sb = sb("xT_sb", [F, B, N])
        w = sb("w", [F, F])
        ones = sb("ones", [128, 128], F32R)
        ones_raw = sb("ones_raw", [128, 128])
        deg = sb("deg", [128, N])
        rdeg = sb("rdeg", [128, N])
        v_hi = sb("v_hi", [128, NT, B, F], F32R)
        v_lo = sb("v_lo", [128, NT, B, F], F32R)
        out = [sb(f"out{i}", [128, N]) for i in range(2)]
        v_ps = [pb(f"v_ps{i}", [128, NT, F]) for i in range(2)]
        o_ps = [pb(f"o_ps{i}", [128, N]) for i in range(2)]
        d_ps = pb("d_ps", [128, N])
        (x_in, w_in, ones_step, deg_sum, deg_step, v_filled, v_hi_done, v_lo_done, o_filled, o_scaled) = (sem(n) for n in (
            "x_in", "w_in", "ones_step", "deg_sum", "deg_step", "v_filled", "v_hi_done", "v_lo_done", "o_filled",
            "o_scaled"))
        out_d = [sem(f"out_d{i}") for i in range(2)]
        block = ctx.enter_context(nc.Block())

        @block.sync
        def _(sp):
            sp.dma_start(w[:, :], W_ind).then_inc(w_in, 16)
            sp.dma_start(xT_sb[:, :, :], xT.rearrange("b c n -> c b n")).then_inc(x_in, 16)
            for p in range(B // 2):
                sp.wait_ge(o_scaled, p + 1)
                sp.dma_start(ind_d[2 * p:2 * p + 2].rearrange("b c n -> (b c) n"), out[p % 2][:, :]).then_inc(out_d[p % 2], 16)
            for i in range(2):
                sp.wait_ge(out_d[i], 16 * (B // 4))

        @block.tensor
        def _(pe):
            pe.wait_ge(ones_step, 2)
            for c in range(2):
                for t in range(NT):
                    last = pe.matmul(d_ps[:, 512 * c:512 * c + 512], ones[:, :], k.adjT[:, t, 512 * c:512 * c + 512],
                                     start=(t == 0), stop=(t == NT - 1))
            last.then_inc(deg_sum, 1)
            pe.wait_ge(w_in, 16)
            pe.wait_ge(x_in, 16)
            for b in range(B):
                if b >= 2:
                    pe.wait_ge(v_lo_done, b - 1)
                for t in range(NT):
                    last = pe.matmul(v_ps[b % 2][:, t, :], xT_sb[:, b, 128 * t:128 * t + 128], w[:, :], start=True, stop=True)
                last.then_inc(v_filled, 1)
            for p in range(B // 2):
                pe.wait_ge(v_lo_done, 2 * p + 2)
                if p >= 2:
                    pe.wait_ge(o_scaled, p - 1)
                for t in range(NT):
                    for n, v in enumerate((v_hi, v_lo)):
                        for c in range(2):
                            last = pe.matmul(o_ps[p % 2][:, 512 * c:512 * c + 512],
                                             v[:, t, 2 * p:2 * p + 2, :].rearrange("p b c -> p (b c)"),
                                             k.adjT[:, t, 512 * c:512 * c + 512], start=(t == 0 and n == 0),
                                             stop=(t == NT - 1 and n == 1))
                last.then_inc(o_filled, 1)

        @block.scalar
        def _(act):
            for b in range(B):
                act.wait_ge(v_filled, b + 1)
                act.activation(v_hi[:, :, b, :], v_ps[b % 2][:, :, :], ACT.Copy).then_inc(v_hi_done, 1)

        @block.vector
        def _(dve):
            dve.memset(ones_raw[:, :], 1.0).then_inc(ones_step, 1)
            dve.wait_ge(ones_step, 1)
            dve.tensor_copy(ones[:, :], ones_raw[:, :]).then_inc(ones_step, 1)
            dve.wait_ge(deg_sum, 1)
            dve.tensor_scalar(deg[:, :], d_ps[:, :], 1.0, None, ALU.max).then_inc(deg_step, 1)
            dve.wait_ge(deg_step, 1)
            dve.reciprocal(rdeg[:, :], deg[:, :]).then_inc(deg_step, 1)
            for b in range(B):
                dve.wait_ge(v_hi_done, b + 1)
                dve.tensor_tensor(v_lo[:, :, b, :], v_ps[b % 2][:, :, :], v_hi[:, :, b, :].bitcast(F32),
                                  ALU.subtract).then_inc(v_lo_done, 1)
            dve.wait_ge(deg_step, 2)
            for p in range(B // 2):
                dve.wait_ge(o_filled, p + 1)
                if p >= 2:
                    dve.wait_ge(out_d[p % 2], 16 * (p // 2))
                dve.tensor_tensor(out[p % 2][:, :], o_ps[p % 2][:, :], rdeg[:, :], ALU.mult).then_inc(o_scaled, 1)


def hyperedges(nc, k, xT, w, d):
    L = 4
    with ExitStack() as ctx:
        sb, pb, sem = sbuf(nc, ctx, "hyperedges"), psum(nc, ctx, "hyperedges"), semaphores(nc, ctx, "hyperedges")
        W2 = sb("W2", [F, 2, F])
        vecs = sb("vecs", [F, 3])
        a_node_b = sb("a_node_b", [F, EDGES])
        a_gn_b = sb("a_gn_b", [F, EDGES])
        fcW = sb("fcW", [F, 128])
        fcb = sb("fcb", [128, 1])
        av = sb("av", [128, 1])
        av_b = sb("av_b", [128, 128])

        def lanes(name, shape, dt=F32):
            return [sb(f"{name}{i}", shape, dt) for i in range(L)]

        xT_sb = lanes("xT_sb", [F, N])
        hT2 = lanes("hT2", [128, N])
        rows = lanes("rows", [128, NT, F])
        s_e = lanes("s_e", [EDGES, N])
        p_e = lanes("p_e", [EDGES, N])
        alpha = lanes("alpha", [EDGES, N])
        nmax = lanes("nmax", [EDGES, 1])
        den = lanes("den", [EDGES, 1])
        rden = lanes("rden", [EDGES, 1])
        agg2 = lanes("agg2", [EDGES, 2, F])
        aggT = lanes("aggT", [128, EDGES])
        agg = lanes("agg", [128, 3, EDGES // 2])
        low = lanes("low", [F, EDGES])
        elow = lanes("elow", [F, EDGES])
        he = lanes("he", [F, EDGES])
        tu = lanes("tu", [128, EDGES])
        qh = lanes("qh", [EDGES, 1])
        alphaT = coef = lanes("coef", [128, NT, EDGES])
        top = lanes("top", [128, NT])
        weight = lanes("weight", [128, NT])
        rweight = lanes("rweight", [128, NT])
        beta_st = lanes("beta_st", [128, N], F32R)
        coef_st = lanes("coef_st", [128, N], F32R)
        Z = [pb(f"Z{i}", [128, N]) for i in range(L)]
        names = ("w_in wide hT rows_f hT_sb rows_sb s_f s_sb s_leaky s_top p_f p_sb alpha_done rden_done alphaT_f "
                 "alphaT_sb agg_f agg_done aggT_f aggT_sb low_done elow_done he_part he_done u_f tu_done q_done se_f "
                 "th_done lg_done top_done lg_less coef_exp weight_done rweight_done coef_done beta_done beta_hi beta_lo "
                 "coefT_f coef_hi coef_lo agg_parts out_d").split()
        S = dict((n, sem(n)) for n in names)
        x_in = [sem(f"x_in{l}") for l in range(L)]
        block = ctx.enter_context(nc.Block())
        lane_of = [(g * L + l, l) for g in range(B // L) for l in range(L)]

        def groups():
            for g in range(B // L):
                yield [(g * L + l, l) for l in range(L)]

        @block.sync
        def _(sp):
            def col(v):
                return v.rearrange("(p o) -> p o", o=1)
            for half in range(2):
                sp.dma_start(W2[:, half, :], w["W"]).then_inc(S["w_in"], 16)
            for n, name in enumerate(("a_node", "a_gn", "a_ge")):
                sp.dma_start(vecs[:, n:n + 1], col(w[name])).then_inc(S["w_in"], 16)
            sp.dma_start(fcW[:, :], w["fcW"]).then_inc(S["w_in"], 16)
            sp.dma_start(fcb[:, :], col(w["fcb"])).then_inc(S["w_in"], 16)
            sp.dma_start(av[:, :], col(w["av"])).then_inc(S["w_in"], 16)
            for bs in groups():
                for b, l in bs:
                    if b >= L:
                        sp.wait_ge(S["rows_f"], b - L + 1)
                    sp.dma_start(xT_sb[l][:, :], xT[b]).then_inc(x_in[l], 16)
                for b, l in bs:
                    sp.wait_ge(S["agg_parts"], b + 1)
                    sp.dma_start(d["agg"][b], agg[l][:, :, :]).then_inc(S["out_d"], 16)
                    sp.wait_ge(S["hT_sb"], b + 1)
                    sp.dma_start(d["hT"][b], hT2[l][:, :]).then_inc(S["out_d"], 16)
                    sp.wait_ge(S["beta_lo"], b + 1)
                    sp.dma_start(d["beta"][b], beta_st[l][:, :].bitcast(F32)).then_inc(S["out_d"], 16)
                    sp.wait_ge(S["coef_lo"], b + 1)
                    sp.dma_start(d["coef"][b], coef_st[l][:, :].bitcast(F32)).then_inc(S["out_d"], 16)
            sp.wait_ge(S["out_d"], 64 * B)

        @block.tensor
        def _(pe):
            pe.wait_ge(S["w_in"], 16 * 8)
            pe.wait_ge(S["wide"], 3)
            for bs in groups():
                for b, l in bs:
                    pe.wait_ge(x_in[l], 16 * (b // L + 1))
                    wait(pe, S["coef_lo"], b - L + 1)
                    for c in range(2):
                        last = pe.matmul(Z[l][:, 512 * c:512 * c + 512], W2[:, :, :].rearrange("p a c -> p (a c)"),
                                         xT_sb[l][:, 512 * c:512 * c + 512], start=True, stop=True)
                    last.then_inc(S["hT"], 1)
                for b, l in bs:
                    pe.wait_ge(S["hT_sb"], b + 1)
                    for t in range(NT):
                        last = pe.matmul(Z[l][:, F * t:F * t + F], xT_sb[l][:, 128 * t:128 * t + 128], W2[:, 0, :],
                                         start=True, stop=True)
                    last.then_inc(S["rows_f"], 1)
                for b, l in bs:
                    pe.wait_ge(S["rows_sb"], b + 1)
                    for c in range(2):
                        last = pe.matmul(Z[l][0:EDGES, 512 * c:512 * c + 512], a_node_b[:, :],
                                         hT2[l][0:F, 512 * c:512 * c + 512], start=True, stop=True)
                    last.then_inc(S["s_f"], 1)
                for b, l in bs:
                    pe.wait_ge(S["s_sb"], b + 1)
                    for c in range(2):
                        last = pe.matmul(Z[l][0:EDGES, 512 * c:512 * c + 512], a_gn_b[:, :],
                                         hT2[l][0:F, 512 * c:512 * c + 512], start=True, stop=True)
                    last.then_inc(S["p_f"], 1)
                for b, l in bs:
                    pe.wait_ge(S["p_sb"], b + 1)
                    pe.wait_ge(S["alpha_done"], b + 1)
                    for t in range(NT):
                        last = pe.transpose(Z[l][:, EDGES * t:EDGES * t + EDGES], alpha[l][:, 128 * t:128 * t + 128],
                                            k.ident[0:64, 0:64])
                    last.then_inc(S["alphaT_f"], 1)
                for b, l in bs:
                    pe.wait_ge(S["alphaT_sb"], b + 1)
                    for t in range(NT):
                        last = pe.matmul(Z[l][0:EDGES, 0:F], alphaT[l][:, t, :], rows[l][:, t, :], start=(t == 0),
                                         stop=(t == NT - 1))
                    last.then_inc(S["agg_f"], 1)
                for b, l in bs:
                    pe.wait_ge(S["agg_done"], b + 1)
                    pe.transpose(Z[l][:, 0:EDGES], agg2[l][:, :, :].rearrange("p a c -> p (a c)"),
                                 k.ident[0:64, 0:64]).then_inc(S["aggT_f"], 1)
                for b, l in bs:
                    pe.wait_ge(S["he_done"], b + 1)
                    pe.matmul(Z[l][:, 0:EDGES], fcW[:, :], he[l][:, :], start=True, stop=True)
                    pe.matmul(Z[l][0:EDGES, 512:513], aggT[l][0:F, :], vecs[:, 2:3], start=True, stop=True).then_inc(S["u_f"], 1)
                for b, l in bs:
                    pe.wait_ge(S["tu_done"], b + 1)
                    pe.wait_ge(S["q_done"], b + 1)
                    pe.matmul(Z[l][:, 0:EDGES], av_b[:, :], tu[l][:, :], start=True, stop=True).then_inc(S["se_f"], 1)
                for b, l in bs:
                    pe.wait_ge(S["coef_done"], b + 1)
                    for t in range(NT):
                        last = pe.transpose(Z[l][0:EDGES, 128 * t:128 * t + 128], coef[l][:, t, :], k.ident[:, :])
                    last.then_inc(S["coefT_f"], 1)

        @block.scalar
        def _(act):
            for bs in groups():
                for b, l in bs:
                    act.wait_ge(S["rows_f"], b + 1)
                    act.activation(rows[l][:, :, :].rearrange("p t c -> p (t c)"), Z[l][:, 0:512], ACT.Copy).then_inc(S["rows_sb"], 1)
                for b, l in bs:
                    act.wait_ge(S["s_f"], b + 1)
                    act.activation(s_e[l][:, :], Z[l][0:EDGES, :], ACT.Copy).then_inc(S["s_sb"], 1)
                for b, l in bs:
                    act.wait_ge(S["p_f"], b + 1)
                    act.activation(p_e[l][:, :], Z[l][0:EDGES, :], ACT.Copy).then_inc(S["p_sb"], 1)
                for b, l in bs:
                    act.wait_ge(S["s_top"], b + 1)
                    act.activation(alpha[l][:, :], alpha[l][:, :], ACT.Exp, bias=nmax[l][:, 0:1], scale=-1.0,
                                   accum_out=den[l][:, 0:1]).then_inc(S["alpha_done"], 1)
                for b, l in bs:
                    act.wait_ge(S["low_done"], b + 1)
                    act.activation(elow[l][:, :], low[l][:, :], ACT.Exp).then_inc(S["elow_done"], 1)
                for b, l in bs:
                    act.wait_ge(S["u_f"], b + 1)
                    act.activation(tu[l][:, :], Z[l][:, 0:EDGES], ACT.Tanh, bias=fcb[:, 0:1]).then_inc(S["tu_done"], 1)
                    act.activation(qh[l][:, :], Z[l][0:EDGES, 512:513], ACT.Copy, scale=0.5).then_inc(S["q_done"], 1)
                for b, l in bs:
                    act.wait_ge(S["q_done"], b + 1)
                    act.activation(p_e[l][:, :], p_e[l][:, :], ACT.Tanh, bias=qh[l][:, 0:1], scale=0.5).then_inc(S["th_done"], 1)
                for b, l in bs:
                    act.wait_ge(S["lg_less"], b + 1)
                    act.activation(coef[l][:, :, :], coef[l][:, :, :], ACT.Exp).then_inc(S["coef_exp"], 1)
                for b, l in bs:
                    act.wait_ge(S["beta_done"], b + 1)
                    act.activation(beta_st[l][0:64, :], p_e[l][:, :], ACT.Copy).then_inc(S["beta_hi"], 1)
                for b, l in bs:
                    act.wait_ge(S["coefT_f"], b + 1)
                    act.activation(coef_st[l][0:64, :], Z[l][0:EDGES, :], ACT.Copy).then_inc(S["coef_hi"], 1)

        @block.vector
        def _(dve):
            dve.wait_ge(S["w_in"], 16 * 8)
            dve.tensor_copy(a_node_b[:, :], vecs[:, 0:1].broadcast_to([F, EDGES])).then_inc(S["wide"], 1)
            dve.tensor_copy(a_gn_b[:, :], vecs[:, 1:2].broadcast_to([F, EDGES])).then_inc(S["wide"], 1)
            dve.tensor_copy(av_b[:, :], av[:, 0:1].broadcast_to([128, 128])).then_inc(S["wide"], 1)
            for bs in groups():
                for b, l in bs:
                    dve.wait_ge(S["hT"], b + 1)
                    wait(dve, S["out_d"], 64 * (b // L) * L)
                    dve.tensor_copy(hT2[l][:, :], Z[l][:, :]).then_inc(S["hT_sb"], 1)
                for b, l in bs:
                    dve.wait_ge(S["s_sb"], b + 1)
                    dve.scalar_tensor_tensor(out=s_e[l][:, :], in0=s_e[l][:, :], scalar=0.2, in1=s_e[l][:, :], op0=ALU.mult,
                                             op1=ALU.max).then_inc(S["s_leaky"], 1)
                for b, l in bs:
                    dve.wait_ge(S["s_leaky"], b + 1)
                    dve.tensor_tensor_reduce(alpha[l][:, :], s_e[l][:, :], k.mask_en[:, :], -1.0, 3.0e38, ALU.add, ALU.min,
                                             nmax[l][:, 0:1]).then_inc(S["s_top"], 1)
                for b, l in bs:
                    dve.wait_ge(S["alpha_done"], b + 1)
                    dve.reciprocal(rden[l][:, :], den[l][:, :]).then_inc(S["rden_done"], 1)
                for b, l in bs:
                    dve.wait_ge(S["alphaT_f"], b + 1)
                    dve.tensor_copy(alphaT[l][:, :, :].rearrange("p t e -> p (t e)"), Z[l][:, 0:512]).then_inc(S["alphaT_sb"], 1)
                for b, l in bs:
                    dve.wait_ge(S["agg_f"], b + 1)
                    dve.wait_ge(S["rden_done"], b + 1)
                    dve.tensor_scalar(agg2[l][:, :, :], Z[l][0:EDGES, 0:F].unsqueeze(1).broadcast_to([EDGES, 2, F]),
                                      rden[l][:, 0:1], None, ALU.mult).then_inc(S["agg_done"], 1)
                for b, l in bs:
                    dve.wait_ge(S["aggT_f"], b + 1)
                    dve.tensor_copy(aggT[l][:, :], Z[l][:, 0:EDGES]).then_inc(S["aggT_sb"], 1)
                for b, l in bs:
                    dve.wait_ge(S["aggT_sb"], b + 1)
                    for half in range(2):
                        p = slice(64 * half, 64 * half + 64)
                        mine = aggT[l][p, :].rearrange("p (i two) -> p i two", two=2)[:, :, half]
                        dve.tensor_copy(agg[l][p, 0, :], mine)
                        dve.tensor_scalar(agg[l][p, 1, :], mine, -1.0, None, ALU.mult)
                        last = dve.tensor_scalar(agg[l][p, 2, :], mine, 1.0, None, ALU.add)
                    last.then_inc(S["agg_parts"], 1)
                    dve.tensor_scalar(low[l][:, :], aggT[l][0:F, :], 0.0, None, ALU.min).then_inc(S["low_done"], 1)
                for b, l in bs:
                    dve.wait_ge(S["elow_done"], b + 1)
                    dve.scalar_tensor_tensor(out=low[l][:, :], in0=aggT[l][0:F, :], scalar=0.0, in1=elow[l][:, :], op0=ALU.max,
                                             op1=ALU.add).then_inc(S["he_part"], 1)
                for b, l in bs:
                    dve.wait_ge(S["he_part"], b + 1)
                    dve.tensor_scalar(he[l][:, :], low[l][:, :], -1.0, None, ALU.add).then_inc(S["he_done"], 1)
                for b, l in bs:
                    dve.wait_ge(S["se_f"], b + 1)
                    dve.tensor_tensor(coef[l][:, :, :], Z[l][:, 0:EDGES].unsqueeze(1).broadcast_to([128, NT, EDGES]),
                                      k.mask_ne[:, :, :], ALU.add).then_inc(S["lg_done"], 1)
                for b, l in bs:
                    dve.wait_ge(S["lg_done"], b + 1)
                    dve.tensor_reduce(top[l][:, :], coef[l][:, :, :], AX_X, ALU.max).then_inc(S["top_done"], 1)
                for b, l in bs:
                    dve.wait_ge(S["top_done"], b + 1)
                    dve.tensor_tensor(coef[l][:, :, :], coef[l][:, :, :],
                                      top[l][:, :].unsqueeze(2).broadcast_to([128, NT, EDGES]), ALU.subtract).then_inc(S["lg_less"], 1)
                for b, l in bs:
                    dve.wait_ge(S["th_done"], b + 1)
                    dve.tensor_scalar(p_e[l][:, :], p_e[l][:, :], 0.5, 0.5, ALU.mult, ALU.add).then_inc(S["beta_done"], 1)
                for b, l in bs:
                    dve.wait_ge(S["coef_exp"], b + 1)
                    dve.reduce_sum(weight[l][:, :], coef[l][:, :, :], axis=AX_X).then_inc(S["weight_done"], 1)
                for b, l in bs:
                    dve.wait_ge(S["weight_done"], b + 1)
                    dve.reciprocal(rweight[l][:, :], weight[l][:, :]).then_inc(S["rweight_done"], 1)
                for b, l in bs:
                    dve.wait_ge(S["rweight_done"], b + 1)
                    dve.tensor_tensor(coef[l][:, :, :], coef[l][:, :, :],
                                      rweight[l][:, :].unsqueeze(2).broadcast_to([128, NT, EDGES]), ALU.mult).then_inc(S["coef_done"], 1)
                for b, l in bs:
                    dve.wait_ge(S["beta_hi"], b + 1)
                    dve.tensor_tensor(beta_st[l][64:128, :], p_e[l][:, :], beta_st[l][0:64, :].bitcast(F32),
                                      ALU.subtract).then_inc(S["beta_lo"], 1)
                for b, l in bs:
                    dve.wait_ge(S["coef_hi"], b + 1)
                    dve.tensor_tensor(coef_st[l][64:128, :], Z[l][0:EDGES, :], coef_st[l][0:64, :].bitcast(F32),
                                      ALU.subtract).then_inc(S["coef_lo"], 1)


def messages(nc, k, d):
    PAIRS = EDGES // 2
    STEPS = 2 * PAIRS
    ITERS = B // 2
    ALL = B * PAIRS
    with ExitStack() as ctx:
        sb, pb, sem = sbuf(nc, ctx, "messages"), psum(nc, ctx, "messages"), semaphores(nc, ctx, "messages")
        sel = sb("sel", [128, PAIRS, 2, 64], F32R)
        hT = [sb(f"hT{i}", [128, N]) for i in range(2)]
        beta = [sb(f"beta{i}", [128, N], F32R) for i in range(2)]
        coef = [sb(f"coef{i}", [128, N], F32R) for i in range(2)]
        agg = [sb(f"agg{i}", [128, 3, PAIRS]) for i in range(2)]
        y = [sb(f"y{i}", [128, N]) for i in range(4)]
        e = [sb(f"e{i}", [128, N]) for i in range(2)]
        part = [sb(f"part{i}", [128, N]) for i in range(2)]
        g_sb = [sb(f"g_sb{i}", [F, N]) for i in range(2)]
        beta_ps = [pb(f"beta_ps{i}", [128, N]) for i in range(2)]
        coef_ps = pb("coef_ps", [128, N])
        g_ps = pb("g_ps", [F, N])
        op_in = [sem(f"op_in{i}") for i in range(2)]
        (sel_done, beta_f, coef_f, y_done, low_done, e_done, t_done, part_done, g_added, g_out) = (sem(n) for n in (
            "sel_done", "beta_f", "coef_f", "y_done", "low_done", "e_done", "t_done", "part_done", "g_added", "g_out"))
        out_d = [sem(f"out_d{i}") for i in range(2)]
        block = ctx.enter_context(nc.Block())

        def exists(i, n):
            return not isinstance(i, int) or 0 <= i < n

        def run(eng, step):
            for s in range(STEPS):
                step(0, s)
            with eng.Fori(1, ITERS - 1) as it:
                for s in range(STEPS):
                    step(it, s)
            for s in range(STEPS):
                step(ITERS - 1, s)
            for s in range(4):
                step(ITERS, s)

        @block.sync
        def _(sp):
            def load(b, par, first):
                if not first:
                    sp.wait_ge(part_done, PAIRS * (b - 1))
                for name, t in (("hT", hT[par][:, :]), ("beta", beta[par][:, :].bitcast(F32)),
                                ("coef", coef[par][:, :].bitcast(F32)), ("agg", agg[par][:, :, :].rearrange("p a i -> p (a i)"))):
                    sp.dma_start(t, one(d[name][bass.ds(b, 1)] if name != "agg" else
                                        d[name][bass.ds(b, 1)].rearrange("o p a i -> o p (a i)"))).then_inc(op_in[par], 16)

            load(0, 0, True)
            load(1, 1, True)
            with sp.Fori(1, ITERS) as it:
                load(2 * it, 0, False)
                sp.wait_ge(g_out, 2 * it - 1)
                sp.dma_start(one(d["g"][bass.ds(2 * it - 2, 1)]), g_sb[0][:, :]).then_inc(out_d[0], 16)
                load(2 * it + 1, 1, False)
                sp.wait_ge(g_out, 2 * it)
                sp.dma_start(one(d["g"][bass.ds(2 * it - 1, 1)]), g_sb[1][:, :]).then_inc(out_d[1], 16)
            for par in range(2):
                sp.wait_ge(g_out, B - 1 + par)
                sp.dma_start(d["g"][B - 2 + par], g_sb[par][:, :]).then_inc(out_d[par], 16)
            for par in range(2):
                sp.wait_ge(out_d[par], 16 * (ITERS + par))

        @block.tensor
        def _(pe):
            pe.wait_ge(sel_done, 4)

            def fill_beta(n, s):
                par, i = (s // PAIRS) % 2, s % PAIRS
                wait(pe, y_done, n - 1)
                for c in range(2):
                    last = pe.matmul(beta_ps[s % 2][:, 512 * c:512 * c + 512], sel[:, i, :, :].rearrange("p a c -> p (a c)"),
                                     beta[par][:, 512 * c:512 * c + 512], start=True, stop=True)
                last.then_inc(beta_f, 1)

            pe.wait_ge(op_in[0], 64)
            fill_beta(0, 0)

            def step(it, s):
                n = STEPS * it + s
                par, i = s // PAIRS, s % PAIRS
                if exists(n + 1, ALL):
                    if i == PAIRS - 1:
                        nxt = 1 - par
                        if not (isinstance(it, int) and it == ITERS - 1 and par == 1):
                            pe.wait_ge(op_in[nxt], 64 * (it + par) + 64)
                if exists(n + 1, ALL):
                    fill_beta(n + 1, s + 1)
                if exists(n - 1, ALL):
                    wait(pe, part_done, n - 1)
                    i1, par1 = (s - 1) % PAIRS, ((s - 1) // PAIRS) % 2
                    for c in range(2):
                        last = pe.matmul(coef_ps[:, 512 * c:512 * c + 512], sel[:, i1, :, :].rearrange("p a c -> p (a c)"),
                                         coef[par1][:, 512 * c:512 * c + 512], start=True, stop=True)
                    last.then_inc(coef_f, 1)
                if exists(n - 2, ALL):
                    j = (s - 2) % PAIRS
                    wait(pe, part_done, n - 1)
                    if j == 0:
                        wait(pe, g_out, 2 * it + (s - 2) // PAIRS)
                    for c in range(2):
                        last = pe.matmul(g_ps[:, 512 * c:512 * c + 512], k.two[:, :], part[s % 2][:, 512 * c:512 * c + 512],
                                         start=(j == 0), stop=(j == PAIRS - 1))
                    last.then_inc(g_added, 1)

            run(pe, step)

        @block.scalar
        def _(act):
            act.sem_inc(out_d[1], 16)

            def step(it, s):
                n = STEPS * it + s
                par, i = s // PAIRS, s % PAIRS
                if exists(n, ALL):
                    a = agg[par]
                    act.wait_ge(y_done, n + 1)
                    wait(act, t_done, n - 1)
                    act.activation(e[s % 2][:, :], y[s % 4][:, :], ACT.Relu, bias=a[:, 1, i:i + 1], scale=-1.0).then_inc(low_done, 1)
                    act.wait_ge(low_done, n + 1)
                    act.activation(e[s % 2][:, :], e[s % 2][:, :], ACT.Exp, scale=-1.0).then_inc(e_done, 1)
                if i == 2:
                    b = 2 * it + (s - 3) // PAIRS
                    if exists(b, B):
                        p = (par + 1) % 2
                        wait(act, out_d[p], 16 * it)
                        act.wait_ge(g_added, PAIRS * (b + 1))
                        act.activation(g_sb[p][:, :], g_ps[:, :], ACT.Copy, bias=-1.0).then_inc(g_out, 1)

            run(act, step)

        @block.vector
        def _(dve):
            for half in range(2):
                for p in (slice(0, 64), slice(64, 128)):
                    mine = k.two[p, :].rearrange("p (i two) -> p i two", two=2)[:, :, half]
                    dve.tensor_copy(sel[p, :, half, :], mine.unsqueeze(2).broadcast_to([64, PAIRS, 64])).then_inc(sel_done, 1)

            def step(it, s):
                n = STEPS * it + s
                par, i = s // PAIRS, s % PAIRS
                if exists(n, ALL):
                    if i == 0:
                        dve.wait_ge(op_in[par], 64 * it + 64)
                    wait(dve, part_done, n - 3)
                    dve.wait_ge(beta_f, n + 1)
                    dve.scalar_tensor_tensor(out=y[s % 4][:, :], in0=hT[par][:, :], scalar=agg[par][:, 0, i:i + 1],
                                             in1=beta_ps[s % 2][:, :], op0=ALU.subtract, op1=ALU.mult).then_inc(y_done, 1)
                if exists(n - 1, ALL):
                    yq = y[(s - 1) % 4]
                    a = agg[((s - 1) // PAIRS) % 2]
                    j = (s - 1) % PAIRS
                    dve.wait_ge(e_done, n)
                    dve.scalar_tensor_tensor(out=yq[:, :], in0=yq[:, :], scalar=a[:, 2, j:j + 1], in1=e[(s - 1) % 2][:, :],
                                             op0=ALU.add, op1=ALU.max).then_inc(t_done, 1)
                if exists(n - 2, ALL):
                    wait(dve, g_added, n - 3)
                    dve.wait_ge(coef_f, n - 1)
                    dve.wait_ge(t_done, n - 1)
                    dve.tensor_tensor(part[s % 2][:, :], y[(s - 2) % 4][:, :], coef_ps[:, :], ALU.mult).then_inc(part_done, 1)

            run(dve, step)


def mix(nc, k, w, d):
    with ExitStack() as ctx:
        sb, pb, sem = sbuf(nc, ctx, "mix"), psum(nc, ctx, "mix"), semaphores(nc, ctx, "mix")
        fcW = sb("fcW", [F, 128])
        fcb = sb("fcb", [128, 1])
        av = sb("av", [128, 1])
        av_b = sb("av_b", [128, 2, F])
        g = [sb(f"g{i}", [F, N]) for i in range(2)]
        ind = [sb(f"ind{i}", [F, N]) for i in range(2)]
        tg = [sb(f"tg{i}", [128, N]) for i in range(2)]
        ti = [sb(f"ti{i}", [128, N]) for i in range(2)]
        c = [sb(f"c{i}", [F, N]) for i in range(2)]
        o = [sb(f"o{i}", [F, N]) for i in range(2)]
        g_ps, i_ps, d_ps = pb("g_ps", [128, N]), pb("i_ps", [128, N]), pb("d_ps", [F, N])
        r_ps = pb("r_ps", [128, NT, F])
        (w_in, wide, u_f, tg_done, ti_done, d_f, c_done, diff_done, mixed, o_done, r_f, r_done) = (sem(n) for n in (
            "w_in", "wide", "u_f", "tg_done", "ti_done", "d_f", "c_done", "diff_done", "mixed", "o_done", "r_f",
            "r_done"))
        in_ = [sem(f"in{i}") for i in range(2)]
        block = ctx.enter_context(nc.Block())

        @block.sync
        def _(sp):
            sp.dma_start(fcW[:, :], w["fcW"]).then_inc(w_in, 16)
            sp.dma_start(fcb[:, :], w["fcb"].rearrange("(p o) -> p o", o=1)).then_inc(w_in, 16)
            sp.dma_start(av[:, :], w["av"].rearrange("(p o) -> p o", o=1)).then_inc(w_in, 16)
            for b in range(B):
                wait(sp, o_done, b - 1)
                sp.dma_start(g[b % 2][:, :], d["g"][b]).then_inc(in_[b % 2], 16)
                sp.dma_start(ind[b % 2][:, :], d["ind"][b]).then_inc(in_[b % 2], 16)

        @block.tensor
        def _(pe):
            pe.wait_ge(w_in, 48)
            pe.wait_ge(wide, 2)
            for n in range(B + 2):
                b = n
                if b < B:
                    pe.wait_ge(in_[b % 2], 32 * (b // 2 + 1))
                    wait(pe, tg_done, b)
                    wait(pe, ti_done, b)
                    for src, ps in ((g, g_ps), (ind, i_ps)):
                        for ch in range(2):
                            s = slice(512 * ch, 512 * ch + 512)
                            last = pe.matmul(ps[:, s], fcW[:, :], src[b % 2][:, s], start=True, stop=True)
                        last.then_inc(u_f, 1)
                b = n - 1
                if 0 <= b < B:
                    pe.wait_ge(ti_done, b + 1)
                    wait(pe, c_done, b)
                    for ch in range(2):
                        s = slice(512 * ch, 512 * ch + 512)
                        pe.matmul(d_ps[:, s], av_b[:, 0, :], ti[b % 2][:, s], start=True, stop=False)
                        last = pe.matmul(d_ps[:, s], av_b[:, 1, :], tg[b % 2][:, s], start=False, stop=True)
                    last.then_inc(d_f, 1)
                b = n - 2
                if 0 <= b < B:
                    pe.wait_ge(o_done, b + 1)
                    wait(pe, r_done, b)
                    for t in range(NT):
                        last = pe.transpose(r_ps[:, t, :], o[b % 2][:, 128 * t:128 * t + 128], k.ident[0:64, 0:64])
                    last.then_inc(r_f, 1)

        @block.scalar
        def _(act):
            act.wait_ge(w_in, 48)
            for n in range(B + 1):
                b = n
                if b < B:
                    wait(act, d_f, b - 1)
                    act.wait_ge(u_f, 2 * b + 1)
                    act.activation(tg[b % 2][:, :], g_ps[:, :], ACT.Tanh, bias=fcb[:, 0:1]).then_inc(tg_done, 1)
                    act.wait_ge(u_f, 2 * b + 2)
                    act.activation(ti[b % 2][:, :], i_ps[:, :], ACT.Tanh, bias=fcb[:, 0:1]).then_inc(ti_done, 1)
                b = n - 1
                if 0 <= b < B:
                    act.wait_ge(d_f, b + 1)
                    wait(act, mixed, b - 1)
                    act.activation(c[b % 2][:, :], d_ps[:, :], ACT.Tanh, scale=0.5).then_inc(c_done, 1)

        @block.vector
        def _(dve):
            dve.wait_ge(w_in, 48)
            dve.tensor_copy(av_b[:, 0, :], av[:, 0:1].broadcast_to([128, F])).then_inc(wide, 1)
            dve.tensor_scalar(av_b[:, 1, :], av[:, 0:1].broadcast_to([128, F]), -1.0, None, ALU.mult).then_inc(wide, 1)
            for n in range(B + 1):
                b = n
                if b < B:
                    p = b % 2
                    dve.wait_ge(in_[b % 2], 32 * (b // 2 + 1))
                    wait(dve, r_f, b - 1)
                    dve.tensor_tensor(o[p][:, :], ind[p][:, :], g[p][:, :], ALU.subtract).then_inc(diff_done, 1)
                    dve.wait_ge(diff_done, b + 1)
                    dve.wait_ge(c_done, b + 1)
                    dve.scalar_tensor_tensor(out=c[p][:, :], in0=c[p][:, :], scalar=1.0, in1=o[p][:, :], op0=ALU.add,
                                             op1=ALU.mult).then_inc(mixed, 1)
                    dve.wait_ge(mixed, b + 1)
                    dve.scalar_tensor_tensor(out=o[p][:, :], in0=c[p][:, :], scalar=0.5, in1=g[p][:, :], op0=ALU.mult,
                                             op1=ALU.add).then_inc(o_done, 1)
                b = n - 1
                if 0 <= b < B:
                    dve.wait_ge(r_f, b + 1)
                    xb = k.x[:, NT * b:NT * b + NT, :]
                    dve.tensor_tensor(xb, r_ps[:, :, :], xb, ALU.add).then_inc(r_done, 1)


def split_heads(nc, k, WhT, bhT, d):
    with ExitStack() as ctx:
        sb, pb, sem = sbuf(nc, ctx, "split_heads"), psum(nc, ctx, "split_heads"), semaphores(nc, ctx, "split_heads")
        x_cols = [sb(f"x_cols{i}", [128, 2, N], F32R) for i in range(2)]
        x_rows = [sb(f"x_rows{i}", [128, NT, 2, F], F32R) for i in range(2)]
        x_twice = [sb(f"x_twice{i}", [128, 4, 2, F]) for i in range(4)]
        wT = sb("wT", [128, HEADS, 2, F])
        g_stack = sb("g_stack", [128, HEADS, 2 * F], F32R)
        bias = sb("bias", [128, HEADS])
        bias_parts = sb("bias_parts", [128, HEADS, 2])
        xT = [pb(f"xT{i}", [128, 512]) for i in range(4)]
        g_ps = pb("g_ps", [128, HEADS, 2 * F])
        w_in, x_doubled, x_turned, x_hi, x_lo, rows_hi, rows_lo, g_f, g_hi, g_lo, bias_done, g_out = (sem(n) for n in (
            "w_in", "x_doubled", "x_turned", "x_hi", "x_lo", "rows_hi", "rows_lo", "g_f", "g_hi", "g_lo", "bias_done",
            "g_out"))
        cols_out = [sem(f"cols_out{i}") for i in range(2)]
        rows_out = [sem(f"rows_out{i}") for i in range(2)]
        block = ctx.enter_context(nc.Block())

        @block.sync
        def _(sp):
            for half in range(2):
                sp.dma_start(wT[:, :, half, :], WhT.rearrange("h d c -> d h c")).then_inc(w_in, 16)
            sp.dma_start(bias[:, :], bhT).then_inc(w_in, 16)
            for b in range(B):
                sp.wait_ge(rows_lo, b + 1)
                sp.dma_start(d["x_rows"][b], x_rows[b % 2][:, :, :, :].bitcast(F32)).then_inc(rows_out[b % 2], 16)
                sp.wait_ge(x_lo, 2 * b + 2)
                sp.dma_start(d["x_cols"][b], x_cols[b % 2][:, :, :].bitcast(F32)).then_inc(cols_out[b % 2], 16)
            sp.wait_ge(g_lo, 1)
            sp.dma_start(d["g_heads"].rearrange("h p c -> p h c"), g_stack[:, :, :].bitcast(F32)).then_inc(g_out, 16)
            sp.wait_ge(bias_done, 2)
            sp.dma_start(d["bias"].rearrange("h p c -> p h c"), bias_parts[:, :, :]).then_inc(g_out, 16)
            sp.wait_ge(g_out, 32)
            for p in range(2):
                sp.wait_ge(rows_out[p], 16 * (B // 2))
                sp.wait_ge(cols_out[p], 16 * (B // 2))

        @block.tensor
        def _(pe):
            for n in range(2 * B):
                pe.wait_ge(x_doubled, n + 1)
                wait(pe, x_lo, n - 3)
                for i in range(4):
                    last = pe.transpose(xT[n % 4][:, 128 * i:128 * i + 128],
                                        x_twice[n % 4][:, i, :, :].rearrange("p a c -> p (a c)"), k.ident[:, :])
                last.then_inc(x_turned, 1)
            pe.wait_ge(w_in, 48)
            for h in range(HEADS):
                w = wT[:, h, :, :].rearrange("p a c -> p (a c)")
                last = pe.matmul(g_ps[:, h, :], w, w, start=True, stop=True)
            last.then_inc(g_f, 1)

        @block.gpsimd
        def _(pool):
            for n in range(2 * B):
                wait(pool, x_turned, n - 3)
                pool.tensor_copy(x_twice[n % 4][:, :, :, :],
                                 k.x[:, 4 * n:4 * n + 4, :].unsqueeze(2).broadcast_to([128, 4, 2, F])).then_inc(x_doubled, 1)

        @block.scalar
        def _(act):
            for n in range(2 * B):
                b, half = n // 2, slice(512 * (n % 2), 512 * (n % 2) + 512)
                if n % 2 == 0:
                    wait(act, rows_out[b % 2], 16 * (b // 2))
                    act.activation(x_rows[b % 2][:, :, 0, :], k.x[:, NT * b:NT * b + NT, :], ACT.Copy).then_inc(rows_hi, 1)
                    wait(act, cols_out[b % 2], 16 * (b // 2))
                act.wait_ge(x_turned, n + 1)
                act.activation(x_cols[b % 2][:, 0, half], xT[n % 4][:, :], ACT.Copy).then_inc(x_hi, 1)
            act.wait_ge(g_f, 1)
            act.activation(g_stack[:, :, :], g_ps[:, :, :], ACT.Copy).then_inc(g_hi, 1)

        @block.vector
        def _(dve):
            for n in range(2 * B):
                b, half = n // 2, slice(512 * (n % 2), 512 * (n % 2) + 512)
                if n % 2 == 0:
                    dve.wait_ge(rows_hi, b + 1)
                    wait(dve, rows_out[b % 2], 16 * (b // 2))
                    dve.tensor_tensor(x_rows[b % 2][:, :, 1, :], k.x[:, NT * b:NT * b + NT, :],
                                      x_rows[b % 2][:, :, 0, :].bitcast(F32), ALU.subtract).then_inc(rows_lo, 1)
                    wait(dve, cols_out[b % 2], 16 * (b // 2))
                dve.wait_ge(x_hi, n + 1)
                dve.tensor_tensor(x_cols[b % 2][:, 1, half], xT[n % 4][:, :], x_cols[b % 2][:, 0, half].bitcast(F32),
                                  ALU.subtract).then_inc(x_lo, 1)
            dve.wait_ge(w_in, 48)
            for n, scale in enumerate((LEAK_UP, LEAK)):
                dve.tensor_scalar(bias_parts[:, :, n], bias[:, :], scale, None, ALU.mult).then_inc(bias_done, 1)
            dve.wait_ge(g_hi, 1)
            low = g_stack[64:128, :, :]
            dve.tensor_tensor(low, g_ps[64:128, :, :], low.bitcast(F32), ALU.subtract).then_inc(g_lo, 1)


def heads(nc, k, d, Wh, Wout):
    U = B * HEADS
    ITERS = U // 2
    J_ALL, C_ALL = U * 16, U * 2
    with ExitStack() as ctx:
        sb, pb, sem = sbuf(nc, ctx, "heads"), psum(nc, ctx, "heads"), semaphores(nc, ctx, "heads")
        x_cols = sb("x_cols", [128, 2 * 2 * N], F32R)
        g_st = [sb(f"g_st{i}", [128, 2 * F], F32R) for i in range(2)]
        x_rows = [sb(f"x_rows{i}", [128, NT, 2 * F], F32R) for i in range(2)]
        w_twice = [sb(f"w_twice{i}", [128, D]) for i in range(2)]
        bias = [sb(f"bias{i}", [128, 2]) for i in range(2)]
        w_out = [sb(f"w_out{i}", [128, F]) for i in range(2)]
        y_st = [sb(f"y_st{i}", [128, N], F32R) for i in range(2)]
        neg = [sb(f"neg{i}", [128, N]) for i in range(2)]
        nmax = sb("nmax", [128, 2, 1])
        P = [sb(f"P{i}", [128, 4, N]) for i in range(2)]
        den = [sb(f"den{i}", [128, 4]) for i in range(2)]
        rden = [sb(f"rden{i}", [128, 4]) for i in range(2)]
        PTh = [sb(f"PTh{i}", [128, 512], F32R) for i in range(4)]
        PTl = [sb(f"PTl{i}", [128, 512], F32R) for i in range(4)]
        rB = sb("rB", [128, 512])
        att = sb("att", [128, 512])
        pos = sb("pos", [128, 512])
        leak = sb("leak", [128, 512])
        cat = [sb(f"cat{i}", [128, 512]) for i in range(2)]
        S_ps = [pb(f"S_ps{i}", [128, N]) for i in range(2)]
        T_ps = [pb(f"T_ps{i}", [128, 512]) for i in range(2)]
        O_ps = [pb(f"O_ps{i}", [128, 512]) for i in range(2)]
        g_in = [sem(f"g_in{i}") for i in range(2)]
        late_in = [sem(f"late_in{i}") for i in range(2)]
        (x_in, s_filled, s_taken, y_hi, exp_done, turned, pt_hi, pt_lo, av_done, r_ready, rb_turned, rb_done, att_done,
         z_filled, z_done, cat_done, h2_done, acc_done, zeroed, max_turn, x_turn, load_turn) = (sem(n) for n in (
            "x_in", "s_filled", "s_taken", "y_hi", "exp_done", "turned", "pt_hi", "pt_lo", "av_done", "r_ready",
            "rb_turned", "rb_done", "att_done", "z_filled", "z_done", "cat_done", "h2_done", "acc_done", "zeroed",
            "max_turn", "x_turn", "load_turn"))
        block = ctx.enter_context(nc.Block())

        S_POS = [0, 1, 2, 3, 4, 5, 7, 8]
        Y_POS = 6

        def item(it, hp, pos):
            return 18 * it + (9 * hp + pos + 1)

        def s_bank(hp, pos):
            return S_ps[(9 * hp + pos + 1) % 2]

        def t_bank(c, n):
            return T_ps[(9 * c + n) % 2]

        def s_pos(it, hp, i):
            return i if isinstance(it, int) and it == ITERS - 1 and hp == 1 else S_POS[i]

        def last_unit(it, hp):
            return isinstance(it, int) and it == ITERS - 1 and hp == 1

        def exists(i, n):
            return not isinstance(i, int) or 0 <= i < n

        def run(eng, slot):
            for s in range(16):
                slot(0, s, False)
            with eng.Fori(1, ITERS - 1) as it:
                for s in range(16):
                    slot(it, s, False)
            for s in range(16):
                slot(ITERS - 1, s, False)
            for s in range(9):
                slot(ITERS, s, True)

        @block.sync
        def _(sp):
            def load_x(b):
                wait(sp, s_filled, 72 * b - 71)
                sp.sem_inc(load_turn, 1)
                wait(sp, x_in, 16 * b)
                sp.sem_inc(load_turn, 1)
                sp.dma_start(x_cols[:, bass.ds((b % 2) * (2 * N), 2 * N)].bitcast(F32),
                             d["x_cols"][bass.ds(b, 1)].rearrange("o p a n -> (o p) (a n)")).then_inc(x_in, 16)

            def load_g(u, h, par):
                wait(sp, s_filled, 9 * u - 17)
                sp.sem_inc(load_turn, 1)
                sp.dma_start(g_st[par][:, :].bitcast(F32), d["g_heads"][bass.ds(h, 1)].rearrange("o p c -> (o p) c")).then_inc(g_in[par], 16)

            def load_late(u, b, h, par):
                wait(sp, h2_done, 2 * u - 2)
                sp.sem_inc(load_turn, 1)
                sp.dma_start(x_rows[par][:, :, :].rearrange("p t c -> p (t c)").bitcast(F32),
                             d["x_rows"][bass.ds(b, 1)].rearrange("o p t a c -> (o p) (t a c)")).then_inc(late_in[par], 16)
                for half in range(2):
                    sp.dma_start(w_twice[par][64 * half:64 * half + 64, :],
                                 Wh[bass.ds(h, 1)].rearrange("o c d -> (o c) d")).then_inc(late_in[par], 16)
                sp.dma_start(bias[par][:, :], d["bias"][bass.ds(h, 1)].rearrange("o p c -> (o p) c")).then_inc(late_in[par], 16)
                sp.dma_start(w_out[par][:, :], Wout[bass.ds(h, 1)].rearrange("o d f -> (o d) f")).then_inc(late_in[par], 16)

            def iteration(b, i):
                for par in range(2):
                    u, h = 8 * b + (2 * i + par), 2 * i + par
                    load_g(u, h, par)
                    load_late(u, b, h, par)

            load_g(0, 0, 0)
            load_x(0)
            load_g(1, 1, 1)
            load_late(0, 0, 0, 0)
            load_late(1, 0, 1, 1)
            load_x(1)
            for i in range(1, 4):
                iteration(0, i)
            with sp.Fori(1, B - 1) as b:
                iteration(b, 0)
                load_x(b + 1)
                for i in range(1, 4):
                    iteration(b, i)
            for i in range(4):
                iteration(B - 1, i)

        @block.tensor
        def _(pe):
            def x_part(batch, part, c):
                at = (batch % 2) * (2 * N) + (N * part + 512 * c)
                return x_cols[:, at:at + 512] if isinstance(at, int) else x_cols[:, bass.ds(at, 512)]

            def project(it, nxt, par, bank, r):
                batch = (2 * it + nxt) // 8
                pe.wait_ge(g_in[par], 16 * (it + nxt // 2) + 16)
                pe.wait_ge(x_in, 16 * batch + 16)
                wait(pe, s_taken, r - 1)
                pe.sem_inc(x_turn, 1)
                for part in range(2):
                    for c in range(2):
                        last = pe.matmul(bank[:, 512 * c:512 * c + 512], g_st[par][:, :], x_part(batch, part, c),
                                         start=(part == 0), stop=(part == 1))
                last.then_inc(s_filled, 1)

            project(0, 0, 0, S_ps[0], 0)

            def slot(it, s, tail):
                hp, i = s // 8, s % 8
                if not tail:
                    pos = s_pos(it, hp, i)
                    r = item(it, hp, pos)
                    wait(pe, s_taken, 1 if isinstance(r, int) and r == 1 else r - 1)
                    pe.sem_inc(x_turn, 1)
                    ps = s_bank(hp, pos)
                    for part in range(2):
                        for c in range(2):
                            last = pe.matmul(ps[:, 512 * c:512 * c + 512], y_st[hp][:, 128 * i:128 * i + 128],
                                             x_part(it // 4, part, c), start=(part == 0), stop=(part == 1))
                    last.then_inc(s_filled, 1)
                    if i == 5 and not last_unit(it, hp):
                        project(it, hp + 1, 1 - hp, s_bank(hp, Y_POS), item(it, hp, Y_POS))
                if s % 4 == 0:
                    c = (s - 12) // 4
                    C = 4 * it + c
                    if exists(C, C_ALL):
                        wait(pe, cat_done, C + 1)
                        pe.matmul(O_ps[c % 2][0:F, :], w_out[(c // 2) % 2][:, :], cat[c % 2][:, :], start=True,
                                  stop=True).then_inc(h2_done, 1)
                for a in range(2):
                    n = 2 * s - 10 + a
                    J, c, j = 32 * it + n, n // 8, n % 8
                    if exists(J, J_ALL):
                        if j == 0:
                            wait(pe, exp_done, 16 * it + 4 * c + 4)
                        if j == 1:
                            wait(pe, rb_done, 4 * it + c)
                        else:
                            wait(pe, pt_lo, J if j == 0 else J - 1)
                        for q in range(4):
                            last = pe.transpose(t_bank(c, j)[:, 128 * q:128 * q + 128], P[c % 2][:, q, 128 * j:128 * j + 128],
                                                k.ident[:, :])
                        last.then_inc(turned, 1)
                    n = 2 * s - 12 + a
                    V, c, v = 32 * it + n, n // 8, n % 8
                    if exists(V, J_ALL):
                        u = c // 2
                        if v == 0:
                            wait(pe, acc_done, 4 * it + c - 1)
                            pe.wait_ge(late_in[u % 2], 80 * (it + u // 2) + 80)
                        wait(pe, pt_lo, V + 1)
                        for part in (PTh, PTl):
                            last = pe.matmul(O_ps[c % 2][:, :], x_rows[u % 2][:, v, :], part[v % 4][:, :],
                                             start=(v == 0 and part is PTh), stop=(v == 7 and part is PTl))
                        last.then_inc(av_done, 1)
                if s % 4 == 0:
                    c = (s - 8) // 4
                    C = 4 * it + c
                    if exists(C, C_ALL):
                        wait(pe, r_ready, C + 1)
                        wait(pe, pt_lo, 8 * C + 7)
                        for q in range(4):
                            last = pe.transpose(t_bank(c, 8)[:, 128 * q:128 * q + 128],
                                                rden[c % 2][:, q:q + 1].broadcast_to([128, 128]), k.ident[:, :])
                        last.then_inc(rb_turned, 1)
                if s % 4 == 2:
                    c = (s - 10) // 4
                    C = 4 * it + c
                    if exists(C, C_ALL):
                        wait(pe, att_done, C + 1)
                        pe.matmul(O_ps[c % 2][:, :], w_twice[(c // 2) % 2][:, :], att[:, :], start=True,
                                  stop=True).then_inc(z_filled, 1)

            run(pe, slot)

        @block.scalar
        def _(act):
            def take_hi(r, par, bank):
                act.wait_ge(s_filled, r + 1)
                act.activation(y_st[par][:, :], bank[:, :], ACT.Copy).then_inc(y_hi, 1)

            take_hi(0, 0, S_ps[0])

            def slot(it, s, tail):
                hp, i = s // 8, s % 8
                for a in range(2):
                    n = 2 * s - 10 + a
                    J, c, j = 32 * it + n, n // 8, n % 8
                    if exists(J, J_ALL):
                        act.wait_ge(turned, J + 1)
                        wait(act, av_done, J - 3)
                        act.activation(PTh[j % 4][:, :], t_bank(c, j)[:, :], ACT.Copy).then_inc(pt_hi, 1)
                if not tail:
                    r = item(it, hp, s_pos(it, hp, i))
                    c = s // 4
                    act.wait_ge(s_taken, r + 1)
                    if i % 4 == 0:
                        wait(act, turned, 32 * it + 8 * (c - 1))
                    act.activation(P[c % 2][:, i % 4, :], neg[i % 2][:, :], ACT.Exp, bias=nmax[:, i % 2, :], scale=-1.0,
                                   accum_out=den[c % 2][:, i % 4:i % 4 + 1]).then_inc(exp_done, 1)
                    if i == 5 and not last_unit(it, hp):
                        take_hi(item(it, hp, Y_POS), 1 - hp, s_bank(hp, Y_POS))
                if s % 4 == 0:
                    c = (s - 8) // 4
                    C = 4 * it + c
                    if exists(C, C_ALL):
                        wait(act, rb_turned, C + 1)
                        wait(act, att_done, C)
                        act.activation(rB[:, :], t_bank(c, 8)[:, :], ACT.Copy).then_inc(rb_done, 1)
                if s % 4 == 2:
                    c = (s - 10) // 4
                    C = 4 * it + c
                    par = (c // 2) % 2
                    if exists(C, C_ALL):
                        wait(act, z_filled, C + 1)
                        wait(act, cat_done, C)
                        act.activation(pos[:, :], O_ps[c % 2][:, :], ACT.Relu, bias=bias[par][:, 0:1], scale=LEAK_UP)
                        act.activation(leak[:, :], O_ps[c % 2][:, :], ACT.Identity, bias=bias[par][:, 1:2],
                                       scale=LEAK).then_inc(z_done, 1)

            run(act, slot)

        @block.gpsimd
        def _(pool):
            def slot(it, s, tail):
                if s % 4 == 3:
                    c = (s - 11) // 4
                    C = 4 * it + c
                    if exists(C, C_ALL):
                        pool.wait_ge(z_done, C + 1)
                        wait(pool, h2_done, C - 1)
                        pool.tensor_tensor(cat[c % 2][:, :], pos[:, :], leak[:, :], ALU.add).then_inc(cat_done, 1)

            run(pool, slot)

        @block.vector
        def _(dve):
            def take_lo(y_count, par, bank):
                dve.wait_ge(y_hi, y_count)
                low = y_st[par][64:128, :]
                dve.tensor_tensor(low, bank[64:128, :], low.bitcast(F32), ALU.subtract).then_inc(s_taken, 1)

            dve.memset(k.acc[:, :], 0.0).then_inc(zeroed, 1)
            take_lo(1, 0, S_ps[0])
            dve.wait_ge(zeroed, 1)

            def slot(it, s, tail):
                hp, i = s // 8, s % 8
                if not tail:
                    pos = s_pos(it, hp, i)
                    r = item(it, hp, pos)
                    wait(dve, exp_done, 16 * it + (s - 1))
                    dve.wait_ge(s_filled, r + 1)
                    dve.sem_inc(max_turn, 1)
                    dve.tensor_tensor_reduce(neg[i % 2][:, :], s_bank(hp, pos)[:, :], k.mask[:, i, :], -1.0, 3.0e38,
                                             ALU.add, ALU.min, nmax[:, i % 2, :]).then_inc(s_taken, 1)
                    if i == 5 and not last_unit(it, hp):
                        take_lo(2 * it + hp + 2, 1 - hp, s_bank(hp, Y_POS))
                for a in range(2):
                    n = 2 * s - 10 + a
                    J, c, j = 32 * it + n, n // 8, n % 8
                    if exists(J, J_ALL):
                        dve.wait_ge(pt_hi, J + 1)
                        dve.tensor_tensor(PTl[j % 4][:, :], t_bank(c, j)[:, :], PTh[j % 4][:, :].bitcast(F32),
                                          ALU.subtract).then_inc(pt_lo, 1)
                if s % 4 == 1:
                    c = (s - 5) // 4
                    C = 4 * it + c
                    if exists(C, C_ALL):
                        wait(dve, exp_done, 4 * C + 4)
                        wait(dve, rb_turned, C - 1)
                        dve.reciprocal(rden[c % 2][:, :], den[c % 2][:, :]).then_inc(r_ready, 1)
                    c = (s - 9) // 4
                    C = 4 * it + c
                    if exists(C, C_ALL):
                        wait(dve, av_done, 8 * C + 8)
                        wait(dve, rb_done, C + 1)
                        wait(dve, z_filled, C)
                        dve.tensor_tensor(att[:, :], O_ps[c % 2][:, :], rB[:, :], ALU.mult).then_inc(att_done, 1)
                if s % 4 == 0:
                    c = (s - 12) // 4
                    C = 4 * it + c
                    if exists(C, C_ALL):
                        at = ((2 * it + c // 2) // 8) * N + 512 * (c % 2)
                        mine = k.acc[:, at:at + 512] if isinstance(at, int) else k.acc[:, bass.ds(at, 512)]
                        wait(dve, h2_done, C + 1)
                        dve.tensor_tensor(mine, O_ps[c % 2][0:F, :], mine, ALU.add).then_inc(acc_done, 1)

            run(dve, slot)


def split_output(nc, k, d):
    with ExitStack() as ctx:
        sb, pb, sem = sbuf(nc, ctx, "split_output"), psum(nc, ctx, "split_output"), semaphores(nc, ctx, "split_output")
        hi_lo = [sb(f"hi_lo{i}", [128, N], F32R) for i in range(2)]
        lo_hi = [sb(f"lo_hi{i}", [128, N], F32R) for i in range(2)]
        rows = [sb(f"rows{i}", [128, NT, F]) for i in range(2)]
        r_ps = [pb(f"r_ps{i}", [128, NT, F]) for i in range(2)]
        hi_done, lo_done, turned, rows_done = (sem(n) for n in ("hi_done", "lo_done", "turned", "rows_done"))
        out_d = [sem(f"out_d{i}") for i in range(2)]
        block = ctx.enter_context(nc.Block())

        @block.sync
        def _(sp):
            for b in range(B):
                p = b % 2
                sp.wait_ge(rows_done, b + 1)
                sp.dma_start(d["rows"][b], rows[p][:, :, :]).then_inc(out_d[p], 16)
                sp.wait_ge(lo_done, b + 1)
                sp.dma_start(d["hi_lo"][b], hi_lo[p][:, :].bitcast(F32)).then_inc(out_d[p], 16)
                sp.dma_start(d["lo_hi"][b], lo_hi[p][:, :].bitcast(F32)).then_inc(out_d[p], 16)
            for p in range(2):
                sp.wait_ge(out_d[p], 48 * (B // 2))

        @block.tensor
        def _(pe):
            for b in range(B):
                wait(pe, rows_done, b - 1)
                for t in range(NT):
                    last = pe.transpose(r_ps[b % 2][:, t, :], k.acc[:, N * b + 128 * t:N * b + 128 * t + 128], k.ident[0:64, 0:64])
                last.then_inc(turned, 1)

        @block.scalar
        def _(act):
            for b in range(B):
                p = b % 2
                mine = k.acc[:, N * b:N * b + N]
                wait(act, out_d[p], 48 * (b // 2))
                act.activation(hi_lo[p][0:64, :], mine, ACT.Copy).then_inc(hi_done, 1)
                act.activation(lo_hi[p][64:128, :], mine, ACT.Copy).then_inc(hi_done, 1)

        @block.vector
        def _(dve):
            for b in range(B):
                p = b % 2
                mine = k.acc[:, N * b:N * b + N]
                wait(dve, out_d[p], 48 * (b // 2))
                dve.wait_ge(turned, b + 1)
                dve.tensor_copy(rows[p][:, :, :], r_ps[p][:, :, :]).then_inc(rows_done, 1)
                dve.wait_ge(hi_done, 2 * b + 2)
                hi = hi_lo[p][0:64, :].bitcast(F32)
                dve.tensor_tensor(hi_lo[p][64:128, :], mine, hi, ALU.subtract)
                dve.tensor_tensor(lo_hi[p][0:64, :], mine, hi, ALU.subtract).then_inc(lo_done, 1)


def split_scores(nc, k, a, d):
    with ExitStack() as ctx:
        sb, pb, sem = sbuf(nc, ctx, "split_scores"), psum(nc, ctx, "split_scores"), semaphores(nc, ctx, "split_scores")
        a1 = sb("a1", [F, 1])
        a2 = sb("a2", [F, 1])
        a2_b = sb("a2_b", [F, 128])
        xT = [sb(f"xT{i}", [F, N]) for i in range(2)]
        s2 = [sb(f"s2{i}", [128, N]) for i in range(2)]
        s1 = [sb(f"s1{i}", [128, NT]) for i in range(2)]
        t_ps = pb("t_ps", [F, N])
        s2_ps = [pb(f"s2_ps{i}", [128, N]) for i in range(2)]
        s1_ps = [pb(f"s1_ps{i}", [128, NT]) for i in range(2)]
        a_in, wide, turned, xT_done, s_f, s_done = (sem(n) for n in ("a_in", "wide", "turned", "xT_done", "s_f", "s_done"))
        out_d = [sem(f"out_d{i}") for i in range(2)]
        block = ctx.enter_context(nc.Block())

        @block.sync
        def _(sp):
            sp.dma_start(a1[:, :], a[0:F, :]).then_inc(a_in, 16)
            sp.dma_start(a2[:, :], a[F:2 * F, :]).then_inc(a_in, 16)
            for b in range(B):
                sp.wait_ge(s_done, 2 * b + 2)
                sp.dma_start(d["s2"][b], s2[b % 2][:, :]).then_inc(out_d[b % 2], 16)
                sp.dma_start(d["s1"][b], s1[b % 2][:, :]).then_inc(out_d[b % 2], 16)
            for p in range(2):
                sp.wait_ge(out_d[p], 32 * (B // 2))

        @block.tensor
        def _(pe):
            pe.wait_ge(wide, 1)
            for n in range(B + 1):
                if n < B:
                    wait(pe, xT_done, n)
                    for t in range(NT):
                        last = pe.transpose(t_ps[:, 128 * t:128 * t + 128], k.x[:, NT * n + t, :], k.ident[:, :])
                    last.then_inc(turned, 1)
                b = n - 1
                if b >= 0:
                    pe.wait_ge(xT_done, b + 1)
                    wait(pe, s_done, 2 * (b - 1))
                    for c in range(2):
                        pe.matmul(s2_ps[b % 2][:, 512 * c:512 * c + 512], a2_b[:, :], xT[b % 2][:, 512 * c:512 * c + 512],
                                  start=True, stop=True)
                    for t in range(NT):
                        last = pe.matmul(s1_ps[b % 2][:, t:t + 1], xT[b % 2][:, 128 * t:128 * t + 128], a1[:, :],
                                         start=True, stop=True)
                    last.then_inc(s_f, 1)

        @block.scalar
        def _(act):
            for b in range(B):
                act.wait_ge(turned, b + 1)
                wait(act, s_f, b - 1)
                act.activation(xT[b % 2][:, :], t_ps[:, :], ACT.Copy).then_inc(xT_done, 1)

        @block.vector
        def _(dve):
            dve.wait_ge(a_in, 32)
            dve.tensor_copy(a2_b[:, :], a2[:, 0:1].broadcast_to([F, 128])).then_inc(wide, 1)
            for b in range(B):
                dve.wait_ge(s_f, b + 1)
                wait(dve, out_d[b % 2], 32 * (b // 2))
                dve.tensor_copy(s2[b % 2][:, :], s2_ps[b % 2][:, :]).then_inc(s_done, 1)
                dve.tensor_copy(s1[b % 2][:, :], s1_ps[b % 2][:, :]).then_inc(s_done, 1)


def attention(nc, k, stage, products, d, b_out=None):
    ITERS = B // 2
    J_ALL, C_ALL = B * 16, B * 2
    with ExitStack() as ctx:
        sb, pb, sem = sbuf(nc, ctx, stage), psum(nc, ctx, stage), semaphores(nc, ctx, stage)
        if products:
            ops = [[sb(f"{n}{i}", [128, N], F32R) for n in ("hi_lo", "lo_hi")] for i in range(2)]
            S_ps = [pb(f"S_ps{i}", [128, N]) for i in range(2)]
            bias = sb("bias", [128, F])
        else:
            s2 = [sb(f"s2_{i}", [128, N]) for i in range(2)]
            s1 = [sb(f"s1_{i}", [128, NT]) for i in range(2)]
            z = [sb(f"z{i}", [128, N]) for i in range(2)]
            leaky = [sb(f"leaky{i}", [128, N]) for i in range(2)]
        rows = [sb(f"rows{i}", [128, NT, F]) for i in range(2)]
        neg = [sb(f"neg{i}", [128, N]) for i in range(2)]
        nmax = sb("nmax", [128, 2, 1])
        P = [sb(f"P{i}", [128, 4, N]) for i in range(2)]
        den = [sb(f"den{i}", [128, 4]) for i in range(2)]
        rden = [sb(f"rden{i}", [128, 4]) for i in range(2)]
        PT = [sb(f"PT{i}", [128, 512]) for i in range(4)]
        att = [sb(f"att{i}", [F, 512]) for i in range(2)]
        o1 = [sb(f"o1{i}", [128, 4, F]) for i in range(2)]
        low = sb("low", [128, 4, F])
        elow = sb("elow", [128, 4, F])
        up = sb("up", [128, 4, F])
        T_ps = [pb(f"T_ps{i}", [128, 512]) for i in range(2)]
        O_ps = pb("O_ps", [F, 512])
        F_ps = pb("F_ps", [128, 4, F])
        op_in = [sem(f"op_in{i}") for i in range(2)]
        pt_done = [sem(f"pt_done{i}") for i in range(2)]
        (bias_in, s_filled, s_taken, z_done, leaky_done, exp_done, turned, av_done, att_done, f_turned, r_ready, o1_done,
         low_done, elow_done, out_step, out_turn, max_turn, f_turn, x_done) = (sem(n) for n in (
            "bias_in", "s_filled", "s_taken", "z_done", "leaky_done", "exp_done", "turned", "av_done", "att_done",
            "f_turned", "r_ready", "o1_done", "low_done", "elow_done", "out_step", "out_turn", "max_turn", "f_turn", "x_done"))
        block = ctx.enter_context(nc.Block())

        def exists(i, n):
            return not isinstance(i, int) or 0 <= i < n

        def run(eng, slot):
            for s in range(16):
                slot(0, s)
            with eng.Fori(1, ITERS - 1) as it:
                for s in range(16):
                    slot(it, s)
            for s in range(16):
                slot(ITERS - 1, s)
            for s in range(9):
                slot(ITERS, s)

        @block.sync
        def _(sp):
            def load(b, par):
                wait(sp, av_done, 16 * (b - 1))
                if products:
                    for n, name in enumerate(("hi_lo", "lo_hi")):
                        sp.dma_start(ops[par][n][:, :].bitcast(F32), one(d[name][bass.ds(b, 1)])).then_inc(op_in[par], 16)
                    sp.dma_start(rows[par][:, :, :].rearrange("p t c -> p (t c)"),
                                 d["rows"][bass.ds(b, 1)].rearrange("o p t c -> (o p) (t c)")).then_inc(op_in[par], 16)
                else:
                    sp.dma_start(s2[par][:, :], one(d["s2"][bass.ds(b, 1)])).then_inc(op_in[par], 16)
                    sp.dma_start(s1[par][:, :], one(d["s1"][bass.ds(b, 1)])).then_inc(op_in[par], 16)
                    sp.dma_start(rows[par][:, :, :],
                                 d["x"][bass.ds(b, 1)].rearrange("o (t p) c -> (o p) t c", p=128)).then_inc(op_in[par], 16)

            if products:
                sp.dma_start(bias[:, :], b_out.rearrange("(o f) -> o f", o=1).broadcast_to([128, F])).then_inc(bias_in, 16)
            load(0, 0)
            load(1, 1)
            with sp.Fori(1, ITERS) as it:
                load(2 * it, 0)
                load(2 * it + 1, 1)

        T_PAR = [0, 1]

        @block.tensor
        def _(pe):
            def slot(it, s):
                G = 16 * it + s
                hp, i = s // 8, s % 8
                if exists(G, 8 * B):
                    if i == 0:
                        pe.wait_ge(op_in[hp], 48 * it + 48)
                    if products:
                        wait(pe, s_taken, G - 1)
                        tile = slice(128 * i, 128 * i + 128)
                        for n in range(2):
                            for c in range(2):
                                ch = slice(512 * c, 512 * c + 512)
                                last = pe.matmul(S_ps[i % 2][:, ch], ops[hp][0][:, tile], ops[hp][n][:, ch], start=(n == 0),
                                                 stop=(n == 1))
                        last.then_inc(s_filled, 1)
                for a in range(2):
                    J = 32 * it + (2 * s - 10 + a)
                    j = (2 * s - 10 + a) % 8
                    if exists(J, J_ALL):
                        if j == 0:
                            wait(pe, exp_done, 16 * it + 4 * ((2 * s - 10 + a) // 8) + 4)
                        wait(pe, pt_done[a], 16 * it + (2 * s - 10) // 2)
                        for q in range(4):
                            last = pe.transpose(T_ps[a][:, 128 * q:128 * q + 128],
                                                P[((2 * s - 10 + a) // 8) % 2][:, q, 128 * j:128 * j + 128], k.ident[:, :])
                        last.then_inc(turned, 1)
                    V = 32 * it + (2 * s - 12 + a)
                    v = (2 * s - 12 + a) % 8
                    if exists(V, J_ALL):
                        hpar = ((2 * s - 12 + a) // 16) % 2
                        wait(pe, pt_done[a], 16 * it + (2 * s - 12) // 2 + 1)
                        if v == 0:
                            wait(pe, att_done, 4 * it + (2 * s - 12) // 8)
                        pe.matmul(O_ps[:, :], rows[hpar][:, v, :], PT[v % 4][:, :], start=(v == 0),
                                  stop=(v == 7)).then_inc(av_done, 1)
                if s % 4 == 2:
                    C = 4 * it + (s - 10) // 4
                    if exists(C, C_ALL):
                        wait(pe, att_done, C + 1)
                        wait(pe, o1_done, C)
                        pe.sem_inc(f_turn, 1)
                        for q in range(4):
                            last = pe.transpose(F_ps[:, q, :], att[((s - 10) // 4) % 2][:, 128 * q:128 * q + 128],
                                                k.ident[0:64, 0:64])
                        last.then_inc(f_turned, 1)

            run(pe, slot)

        @block.scalar
        def _(act):
            def take(it, s, a):
                J = 32 * it + (2 * s - 10 + a)
                if exists(J, J_ALL):
                    act.wait_ge(turned, J + 1)
                    wait(act, av_done, J - 3)
                    act.activation(PT[(2 * s - 10 + a) % 4][:, :], T_ps[a][:, :], ACT.Copy).then_inc(pt_done[a], 1)

            def scores(it, s):
                G = 16 * it + s
                hp, i = (s // 8) % 2, s % 8
                if exists(G, 8 * B):
                    if i == 0:
                        act.wait_ge(op_in[hp], 48 * (it + s // 16) + 48)
                    wait(act, leaky_done, G - 1)
                    act.activation(z[i % 2][:, :], s2[hp][:, :], ACT.Identity, bias=s1[hp][:, i:i + 1]).then_inc(z_done, 1)

            if not products:
                scores(0, 0)

            def slot(it, s):
                G = 16 * it + s
                hp, i = s // 8, s % 8
                if s % 4 == 2:
                    C = 4 * it + (s - 10) // 4
                    if exists(C, C_ALL):
                        act.wait_ge(av_done, 8 * C + 8)
                        wait(act, f_turned, C - 1)
                        act.activation(att[((s - 10) // 4) % 2][:, :], O_ps[:, :], ACT.Copy).then_inc(att_done, 1)
                take(it, s, 0)
                if not products:
                    scores(it, s + 1)
                if exists(G, 8 * B):
                    act.wait_ge(s_taken, G + 1)
                    if i % 4 == 0:
                        wait(act, turned, 32 * it + 8 * (s // 4 - 1))
                    act.activation(P[(s // 4) % 2][:, i % 4, :], neg[i % 2][:, :], ACT.Exp, bias=nmax[:, i % 2, :], scale=-1.0,
                                   accum_out=den[(s // 4) % 2][:, i % 4:i % 4 + 1]).then_inc(exp_done, 1)
                if s % 4 == 0 and not products:
                    C = 4 * it + (s - 12) // 4
                    if exists(C, C_ALL):
                        act.wait_ge(low_done, C + 1)
                        act.activation(elow[:, :, :], low[:, :, :], ACT.Exp).then_inc(elow_done, 1)

            run(act, slot)

        @block.gpsimd
        def _(pool):
            if products:
                pool.wait_ge(bias_in, 16)

            def slot(it, s):
                if s % 4 == 3:
                    C = 4 * it + (s - 11) // 4
                    if exists(C, C_ALL):
                        o = o1[((s - 11) // 4) % 2]
                        xs = k.x[:, bass.ds(4 * C, 4), :]
                        pool.wait_ge(o1_done, C + 1)
                        if products:
                            pool.sem_inc(out_turn, 1)
                            pool.tensor_tensor(low[:, :, :], o[:, :, :], bias[:, :].unsqueeze(1).broadcast_to([128, 4, F]),
                                               ALU.add).then_inc(out_step, 1)
                            pool.wait_ge(out_step, 3 * C + 1)
                            pool.sem_inc(out_turn, 1)
                            pool.tensor_scalar(up[:, :, :], low[:, :, :], 0.0, 0.99, ALU.max, ALU.mult)
                            pool.tensor_scalar(elow[:, :, :], low[:, :, :], 0.01, 1.0, ALU.mult, ALU.mult).then_inc(out_step, 1)
                            pool.wait_ge(out_step, 3 * C + 2)
                        else:
                            wait(pool, elow_done, C)
                            pool.sem_inc(out_turn, 1)
                            pool.tensor_scalar(low[:, :, :], o[:, :, :], 0.0, 0.0, ALU.min, ALU.add).then_inc(low_done, 1)
                            pool.tensor_scalar(up[:, :, :], o[:, :, :], 0.0, -1.0, ALU.max, ALU.add).then_inc(out_step, 1)
                            pool.wait_ge(out_step, 2 * C + 1)
                            pool.wait_ge(elow_done, C + 1)
                        pool.sem_inc(out_turn, 1)
                        pool.tensor_tensor(up[:, :, :], up[:, :, :], elow[:, :, :], ALU.add).then_inc(out_step, 1)
                        pool.wait_ge(out_step, (3 if products else 2) * (C + 1))
                        pool.sem_inc(out_turn, 1)
                        pool.tensor_tensor(xs, xs, up[:, :, :], ALU.add).then_inc(x_done, 1)
                        pool.wait_ge(x_done, C + 1)

            run(pool, slot)

        @block.vector
        def _(dve):
            def slot(it, s):
                G = 16 * it + s
                i = s % 8
                if exists(G, 8 * B):
                    if not products:
                        dve.wait_ge(z_done, G + 1)
                        wait(dve, s_taken, G - 1)
                        dve.scalar_tensor_tensor(out=leaky[i % 2][:, :], in0=z[i % 2][:, :], scalar=0.2, in1=z[i % 2][:, :],
                                                 op0=ALU.mult, op1=ALU.max).then_inc(leaky_done, 1)
                for a in ([1] if products else [1]):
                    J = 32 * it + (2 * s - 10 + a)
                    if exists(J, J_ALL) and not products:
                        dve.wait_ge(turned, J + 1)
                        wait(dve, av_done, J - 3)
                        dve.tensor_copy(PT[(2 * s - 10 + a) % 4][:, :], T_ps[a][:, :]).then_inc(pt_done[a], 1)
                if exists(G, 8 * B):
                    wait(dve, exp_done, G - 1)
                    dve.wait_ge(s_filled if products else leaky_done, G + 1)
                    dve.sem_inc(max_turn, 1)
                    dve.tensor_tensor_reduce(neg[i % 2][:, :], S_ps[i % 2][:, :] if products else leaky[i % 2][:, :],
                                             k.mask[:, i, :], -1.0, 3.0e38, ALU.add, ALU.min, nmax[:, i % 2, :]).then_inc(s_taken, 1)
                J = 32 * it + (2 * s - 10 + 1)
                if exists(J, J_ALL) and products:
                    dve.wait_ge(turned, J + 1)
                    wait(dve, av_done, J - 3)
                    dve.tensor_copy(PT[(2 * s - 10 + 1) % 4][:, :], T_ps[1][:, :]).then_inc(pt_done[1], 1)
                if s % 4 == 1:
                    C = 4 * it + (s - 5) // 4
                    if exists(C, C_ALL):
                        wait(dve, exp_done, 4 * C + 4)
                        wait(dve, o1_done, C - 1)
                        dve.reciprocal(rden[((s - 5) // 4) % 2][:, :], den[((s - 5) // 4) % 2][:, :]).then_inc(r_ready, 1)
                if s % 4 == 3:
                    C = 4 * it + (s - 11) // 4
                    if exists(C, C_ALL):
                        q = ((s - 11) // 4) % 2
                        dve.wait_ge(f_turned, C + 1)
                        dve.wait_ge(r_ready, C + 1)
                        wait(dve, x_done, C - 1)
                        dve.tensor_tensor(o1[q][:, :, :], F_ps[:, :, :], rden[q][:, :].unsqueeze(2).broadcast_to([128, 4, F]),
                                          ALU.mult).then_inc(o1_done, 1)

            run(dve, slot)


def causal(nc, k, w):
    PAIRS = B // 2
    STEPS = 3
    R = STEPS * PAIRS
    with ExitStack() as ctx:
        sb, pb, sem = sbuf(nc, ctx, "causal"), psum(nc, ctx, "causal"), semaphores(nc, ctx, "causal")
        w1v, w1e, w2 = (sb(n, [128, 128]) for n in ("w1v", "w1e", "w2"))
        b1 = sb("b1", [128, 1])
        b2 = sb("b2", [128, 1])
        b2_b = sb("b2_b", [128, 128])
        given = sb("given", [1, F])
        v = sb("v", [128, NT, B, F])
        v_hi = sb("v_hi", [128, NT, B, F], F32R)
        v_lo = sb("v_lo", [128, NT, B, F], F32R)
        vT = [sb(f"vT{p}", [128, N]) for p in range(PAIRS)]
        eff = [sb(f"eff{i}", [128, N]) for i in range(2)]
        h = [sb(f"h{i}", [128, N]) for i in range(2)]
        e_ps = [pb(f"e_ps{i}", [128, N]) for i in range(2)]
        h_ps = pb("h_ps", [128, N])
        v_ps = pb("v_ps", [128, N])
        (zeroed, w_in, given_in, v_copied, given_set, v_hi_done, v_lo_done, vT_turned, vT_taken, e_f, e_done, h_f, h_done, vT_f,
         vT_done, v_f, v_done, x_done) = (sem(n) for n in (
            "zeroed", "w_in", "given_in", "v_copied", "given_set", "v_hi_done", "v_lo_done", "vT_turned", "vT_taken", "e_f",
            "e_done", "h_f", "h_done", "vT_f", "vT_done", "v_f", "v_done", "x_done"))
        block = ctx.enter_context(nc.Block())

        def of_pair(t, p):
            return t[:, :, 2 * p:2 * p + 2, :]

        @block.sync
        def _(sp):
            sp.dma_start(given[:, :], w["intervention"]).then_inc(given_in, 16)
            for half in range(2):
                s = slice(64 * half, 64 * half + 64)
                sp.dma_start(b1[s, :], w["b1"].rearrange("(p o) -> p o", o=1)).then_inc(w_in, 16)
                sp.dma_start(b2[s, :], w["b2"].rearrange("(p o) -> p o", o=1)).then_inc(w_in, 16)
                sp.dma_start(b2_b[:, s], w["b2"].rearrange("(o f) -> o f", o=1).broadcast_to([128, F])).then_inc(w_in, 16)
            sp.wait_ge(zeroed, 3)
            for half in range(2):
                s = slice(64 * half, 64 * half + 64)
                sp.dma_start(w1v[s, s], w["W1T"][0:F, :]).then_inc(w_in, 16)
                sp.dma_start(w1e[s, s], w["W1T"][F:2 * F, :]).then_inc(w_in, 16)
                sp.dma_start(w2[s, s], w["W2T"]).then_inc(w_in, 16)

        @block.gpsimd
        def _(pool):
            for t in (w1v, w1e, w2):
                pool.memset(t[:, :], 0.0).then_inc(zeroed, 1)
            for p in range(PAIRS):
                q = R - PAIRS + p
                pool.wait_ge(v_done, q + 1)
                for b in (2 * p, 2 * p + 1):
                    xb = k.x[:, NT * b:NT * b + NT, :]
                    pool.tensor_tensor(xb, xb, v[:, :, b, :], ALU.add).then_inc(x_done, 1)

        @block.tensor
        def _(pe):
            for p in range(PAIRS):
                pe.wait_ge(given_set, 1)
                for t in range(NT):
                    last = pe.transpose((e_ps[p % 2] if p < 2 else (h_ps, v_ps)[p % 2])[:, 128 * t:128 * t + 128],
                                        of_pair(v, p)[:, t].rearrange("p b c -> p (b c)"), k.ident[:, :])
                last.then_inc(vT_turned, 1)
            pe.wait_ge(w_in, 16 * 12)
            pe.wait_ge(vT_taken, PAIRS)
            for n in range(R + 2):
                if n < R:
                    p = n % PAIRS
                    pe.wait_ge(v_hi_done, n + 1)
                    pe.wait_ge(v_lo_done, n + 1)
                    wait(pe, e_done, n - 1)
                    for t in range(NT):
                        for m, part in enumerate((v_hi, v_lo)):
                            for c in range(2):
                                last = pe.matmul(e_ps[n % 2][:, 512 * c:512 * c + 512],
                                                 of_pair(part, p)[:, t].rearrange("p b c -> p (b c)"),
                                                 k.adjT[:, t, 512 * c:512 * c + 512], start=(t == 0 and m == 0),
                                                 stop=(t == NT - 1 and m == 1))
                    last.then_inc(e_f, 1)
                q = n - 1
                if 0 <= q < R:
                    pe.wait_ge(e_done, q + 1)
                    wait(pe, h_done, q)
                    wait(pe, vT_done, q - PAIRS + 1)
                    for m in range(2):
                        for c in range(2):
                            ch = slice(512 * c, 512 * c + 512)
                            last = pe.matmul(h_ps[:, ch], (w1v, w1e)[m][:, :], (vT[q % PAIRS], eff[q % 2])[m][:, ch],
                                             start=(m == 0), stop=(m == 1))
                    last.then_inc(h_f, 1)
                q = n - 2
                if 0 <= q < R:
                    pe.wait_ge(h_done, q + 1)
                    wait(pe, v_done, q)
                    if q < R - PAIRS:
                        for c in range(2):
                            ch = slice(512 * c, 512 * c + 512)
                            last = pe.matmul(v_ps[:, ch], w2[:, :], h[q % 2][:, ch], start=True, stop=True)
                        last.then_inc(vT_f, 1)
                        pe.wait_ge(vT_done, q + 1)
                    for t in range(NT):
                        last = pe.matmul(v_ps[:, 128 * t:128 * t + 128], h[q % 2][:, 128 * t:128 * t + 128], w2[:, :],
                                         start=True, stop=True)
                    last.then_inc(v_f, 1)

        @block.scalar
        def _(act):
            act.wait_ge(given_set, 1)
            for p in range(PAIRS):
                act.activation(of_pair(v_hi, p), of_pair(v, p), ACT.Copy).then_inc(v_hi_done, 1)
            act.wait_ge(w_in, 16 * 12)
            for n in range(R + 2):
                if n < R:
                    act.wait_ge(e_f, n + 1)
                    wait(act, h_f, n - 1)
                    act.activation(eff[n % 2][:, :], e_ps[n % 2][:, :], ACT.Copy).then_inc(e_done, 1)
                q = n - 1
                if 0 <= q < R:
                    act.wait_ge(h_f, q + 1)
                    wait(act, v_f, q - 1)
                    act.activation(h[q % 2][:, :], h_ps[:, :], ACT.Relu, bias=b1[:, 0:1]).then_inc(h_done, 1)
                q = n - 2
                if 0 <= q < R - PAIRS:
                    act.wait_ge(vT_f, q + 1)
                    act.activation(vT[q % PAIRS][:, :], v_ps[:, :], ACT.Identity, bias=b2[:, 0:1]).then_inc(vT_done, 1)
                    act.wait_ge(v_done, q + 1)
                    act.activation(of_pair(v_hi, q % PAIRS), of_pair(v, q % PAIRS), ACT.Copy).then_inc(v_hi_done, 1)

        @block.vector
        def _(dve):
            dve.tensor_copy(v[:, :, :, :].rearrange("p t b c -> p b t c"),
                            k.x[:, :, :].rearrange("p (b t) c -> p b t c", b=B)).then_inc(v_copied, 1)
            dve.wait_ge(v_copied, 1)
            dve.wait_ge(given_in, 16)
            dve.tensor_copy(v[0:1, 0, :, :], given[:, :].unsqueeze(1).broadcast_to([1, B, F])).then_inc(given_set, 1)
            for p in range(PAIRS):
                dve.wait_ge(v_hi_done, p + 1)
                dve.wait_ge(given_set, 1)
                dve.tensor_tensor(of_pair(v_lo, p), of_pair(v, p), of_pair(v_hi, p).bitcast(F32), ALU.subtract).then_inc(v_lo_done, 1)
            for p in range(PAIRS):
                dve.wait_ge(vT_turned, p + 1)
                dve.tensor_copy(vT[p][:, :], (e_ps[p % 2] if p < 2 else (h_ps, v_ps)[p % 2])[:, :]).then_inc(vT_taken, 1)
            dve.wait_ge(w_in, 16 * 12)
            for q in range(R):
                dve.wait_ge(v_f, q + 1)
                dve.tensor_tensor(of_pair(v, q % PAIRS), v_ps[:, :].rearrange("p (t b c) -> p t b c", t=NT, b=2),
                                  b2_b[:, :].rearrange("p (b c) -> p b c", b=2).unsqueeze(1).broadcast_to([128, NT, 2, F]),
                                  ALU.add).then_inc(v_done, 1)
                if q < R - PAIRS:
                    dve.wait_ge(v_hi_done, PAIRS + q + 1)
                    dve.tensor_tensor(of_pair(v_lo, q % PAIRS), of_pair(v, q % PAIRS), of_pair(v_hi, q % PAIRS).bitcast(F32),
                                      ALU.subtract).then_inc(v_lo_done, 1)


def program(nc, a, out):
    with ExitStack() as ctx:
        sb = sbuf(nc, ctx, "program")
        k = Shared()
        k.ident = sb("ident", [128, 128])
        k.x = sb("x", [128, B * NT, F])
        k.mask = sb("mask", [128, NT, N], BF16)
        k.adjT = sb("adjT", [128, NT, N], F32R)

        def scratch(name, shape):
            return nc.dram_tensor(name, shape, F32, kind="Internal").ap()

        d = {"hT": scratch("hT_d", [B, 128, N]), "beta": scratch("beta_d", [B, 128, N]), "coef": scratch("coef_d", [B, 128, N]),
             "agg": scratch("agg_d", [B, 128, 3, EDGES // 2]), "g": scratch("g_d", [B, F, N]), "ind": scratch("ind_d", [B, F, N])}
        w = {"W": a["L0_gnn_W"], "a_node": a["L0_gnn_a_node"], "a_gn": a["L0_gnn_a_gn"], "a_ge": a["L0_gnn_a_ge"],
             "fcW": a["L0_gnn_fcW"], "fcb": a["L0_gnn_fcb"], "av": a["L0_gnn_av"]}
        with ExitStack() as hyper:
            sb = sbuf(nc, hyper, "hypergraph")
            k.two = sb("two", [128, 64])
            k.mask_ne = sb("mask_ne", [128, NT, EDGES], BF16)
            k.mask_en = sb("mask_en", [EDGES, N], BF16)
            setup(nc, k, a["x"], a["adj"], a["adjT"], a["L0_gnn_H"], a["HT"])
            industry(nc, k, a["xT"], a["L0_gnn_W_ind"], d["ind"])
            hyperedges(nc, k, a["xT"], w, d)
            messages(nc, k, d)
            mix(nc, k, w, d)
        x_d = scratch("x_d", [B, N, F])
        layernorm(nc, k, "norm0", x_d)

        with ExitStack() as graph:
            k.acc = graph.enter_context(nc.sbuf_tensor("acc", [F, B * N], F32))
            d["x_cols"], d["x_rows"] = scratch("x_cols_d", [B, 128, 2, N]), scratch("x_rows_d", [B, 128, NT, 2, F])
            d["g_heads"], d["bias"] = scratch("g_heads_d", [HEADS, 128, 2 * F]), scratch("bias_d", [HEADS, 128, 2])
            d["rows"], d["hi_lo"], d["lo_hi"] = scratch("rows_d", [B, 128, NT, F]), scratch("hi_lo_d", [B, 128, N]), scratch("lo_hi_d", [B, 128, N])
            split_heads(nc, k, a["WhT"], a["bhT"], d)
            heads(nc, k, d, a["L1_gnn_Wh"], a["L1_gnn_W_out"].rearrange("(h d) f -> h d f", h=HEADS))
            split_output(nc, k, d)
            attention(nc, k, "output_layer", True, d, a["L1_gnn_b_out"])
        layernorm(nc, k, "norm1", x_d)

        d["x"], d["s2"], d["s1"] = x_d, scratch("s2_d", [B, 128, N]), scratch("s1_d", [B, 128, NT])
        split_scores(nc, k, a["L2_gnn_a"], d)
        attention(nc, k, "threshold_layer", False, d)
        layernorm(nc, k, "norm2", x_d)

        causal(nc, k, {"intervention": a["L3_gnn_intervention_value"], "W1T": a["W1T"], "W2T": a["W2T"],
                       "b1": a["L3_gnn_b1"], "b2": a["L3_gnn_b2"]})
        layernorm(nc, k, "norm3", out)


_INS = ['x', 'adj', 'L0_gnn_H', 'L0_gnn_W', 'L0_gnn_W_ind', 'L0_gnn_a_node', 'L0_gnn_a_gn', 'L0_gnn_a_ge', 'L0_gnn_fcW', 'L0_gnn_fcb',
        'L0_gnn_av', 'L1_gnn_Wh', 'L1_gnn_bh', 'L1_gnn_W_out', 'L1_gnn_b_out', 'L2_gnn_a', 'L3_gnn_intervention_value',
        'L3_gnn_W1', 'L3_gnn_b1', 'L3_gnn_W2', 'L3_gnn_b2']


def kernel(**inputs):
    import numpy as _np
    import concourse.bacc as _bacc
    from concourse import mybir as _mybir
    from concourse.bass_utils import run_bass_kernel_spmd as _run

    given = {name: _np.asarray(inputs[name]) for name in _INS}
    given["xT"] = given["x"].transpose(0, 2, 1)
    given["adjT"] = given["adj"].T
    given["HT"] = given["L0_gnn_H"].T
    given["WhT"] = given["L1_gnn_Wh"].transpose(0, 2, 1)
    given["bhT"] = given.pop("L1_gnn_bh").T
    given["W1T"] = given.pop("L3_gnn_W1").T
    given["W2T"] = given.pop("L3_gnn_W2").T
    nc = _bacc.Bacc("TRN2", target_bir_lowering=False, num_devices=1)
    arrays, args = {}, {}
    for name, v in given.items():
        v = _np.ascontiguousarray(v)
        arrays[f"in_{name}_dram"] = v
        args[name] = nc.dram_tensor(f"in_{name}_dram", v.shape, _mybir.dt.from_np(v.dtype), kind="ExternalInput").ap()
    out = nc.dram_tensor("out_0_dram", (B, N, F), _mybir.dt.float32, kind="ExternalOutput").ap()
    program(nc, args, out)
    r = _run(nc, [arrays], core_ids=[0])
    return r.results[0]["out_0_dram"]
```

```python
import concourse.bass as bass
from concourse import mybir
from contextlib import ExitStack

F32 = mybir.dt.float32
F32R = mybir.dt.float32r
BF16 = mybir.dt.bfloat16
ALU = mybir.AluOpType
ACT = mybir.ActivationFunctionType
AX_X = mybir.AxisListType.X

B, N, F = 8, 1024, 64
HEADS, D = 8, 128
EDGES = 64
NT = N // 128
MASKED = -1e30
EPS = 1e-5
LEAK = 0.01
LEAK_UP = 1.0 - LEAK




class Shared:
    pass


def wait(eng, sem, value):
    if not isinstance(value, int) or value > 0:
        eng.wait_ge(sem, value)


def sbuf(nc, ctx, stage):
    return lambda name, shape, dt=F32: ctx.enter_context(nc.sbuf_tensor(f"{stage}_{name}", shape, dt))


def psum(nc, ctx, stage):
    return lambda name, shape, dt=F32: ctx.enter_context(nc.psum_tensor(f"{stage}_{name}", shape, dt))


def semaphores(nc, ctx, stage):
    mine = []
    ctx.callback(lambda: (nc.all_engine_barrier(), nc.clear_and_free_semaphores(mine), nc.all_engine_barrier()))

    def new(name):
        mine.append(nc.alloc_semaphore(name=f"{stage}_{name}"))
        return mine[-1]
    return new


def one(ap):
    return ap.rearrange("o p n -> (o p) n")


def setup(nc, k, adj, H, HT):
    with ExitStack() as ctx:
        sb, pb, sem = sbuf(nc, ctx, "setup"), psum(nc, ctx, "setup"), semaphores(nc, ctx, "setup")
        raw = sb("raw", [128, NT, N])
        turned = [pb(f"turned{i}", [128, NT, 128]) for i in range(2)]
        raw_h = sb("raw_h", [128, NT, EDGES])
        raw_ht = sb("raw_ht", [EDGES, N])
        h_in, ident_step, two_step, adj_turned, adjT_done = (sem(n) for n in (
            "h_in", "ident_step", "two_step", "adj_turned", "adjT_done"))
        adj_in = [sem(f"adj_in{t}") for t in range(NT)]
        block = ctx.enter_context(nc.Block())

        @block.sync
        def _(sp):
            for t in range(0, NT, 2):
                sp.dma_start(raw[:, t, :], adj[128 * t:128 * t + 128, :]).then_inc(adj_in[t], 16)
            sp.dma_start(raw_h[:, :, :], H.rearrange("(t p) e -> p t e", p=128)).then_inc(h_in, 16)
            sp.dma_start(raw_ht[:, :], HT).then_inc(h_in, 16)

        @block.scalar
        def _(act):
            for t in range(1, NT, 2):
                act.dma_start(raw[:, t, :], adj[128 * t:128 * t + 128, :]).then_inc(adj_in[t], 16)
            for t in range(NT):
                act.wait_ge(adj_turned, t + 1)
                act.activation(k.adjT[:, :, 128 * t:128 * t + 128], turned[t % 2][:, :, :], ACT.Copy).then_inc(adjT_done, 1)

        @block.tensor
        def _(pe):
            pe.wait_ge(ident_step, 2)
            for t in range(NT):
                pe.wait_ge(adj_in[t], 16)
                wait(pe, adjT_done, t - 1)
                for m in range(NT):
                    last = pe.transpose(turned[t % 2][:, m, :], raw[:, t, 128 * m:128 * m + 128], k.ident[:, :])
                last.then_inc(adj_turned, 1)

        @block.gpsimd
        def _(pool):
            pool.memset(k.ident[:, :], 1.0).then_inc(ident_step, 1)
            pool.wait_ge(ident_step, 1)
            pool.affine_select(out=k.ident[:, :], in_=k.ident[:, :], compare_op=ALU.is_equal, fill=0.0, base=0,
                               pattern=[[-1, 128]], channel_multiplier=1).then_inc(ident_step, 1)

        @block.vector
        def _(dve):
            dve.wait_ge(h_in, 32)
            dve.tensor_scalar(k.mask_ne[:, :, :], raw_h[:, :, :], 0.0, MASKED, ALU.is_le, ALU.mult)
            dve.tensor_scalar(k.mask_en[:, :], raw_ht[:, :], 0.0, MASKED, ALU.is_le, ALU.mult)
            dve.wait_ge(ident_step, 2)
            dve.tensor_copy(k.two[0:64, :], k.ident[0:64, 0:64]).then_inc(two_step, 1)
            dve.tensor_copy(k.two[64:128, :], k.ident[64:128, 64:128]).then_inc(two_step, 1)
            for t in range(NT):
                dve.wait_ge(adj_in[t], 16)
                dve.tensor_scalar(k.mask[:, t, :], raw[:, t, :], 0.0, MASKED, ALU.is_equal, ALU.mult)


def layernorm(nc, k, stage, x_d):
    Q = 4
    G = B * NT // Q
    with ExitStack() as ctx:
        sb, sem = sbuf(nc, ctx, stage), semaphores(nc, ctx, stage)
        total = sb("total", [128, Q, G])
        mean = sb("mean", [128, Q, G])
        square = [sb(f"square{i}", [128, G, F]) for i in range(2)]
        spread = sb("spread", [128, Q, G])
        var = sb("var", [128, Q, G])
        std = sb("std", [128, Q, G])
        rstd = sb("rstd", [128, Q, G])
        summed, meant, centred, squared, spread_done, var_done, std_done, rstd_done, scaled, out_d = (sem(n) for n in (
            "summed", "meant", "centred", "squared", "spread_done", "var_done", "std_done", "rstd_done", "scaled",
            "out_d"))
        block = ctx.enter_context(nc.Block())

        def part(q):
            return k.x[:, G * q:G * q + G, :]

        def wide(t, q):
            return t[:, q, :].unsqueeze(2).broadcast_to([128, G, F])

        @block.sync
        def _(sp):
            per = B // Q
            if x_d is None:
                return
            for q in range(Q):
                sp.wait_ge(scaled, q + 1)
                sp.dma_start(x_d[per * q:per * q + per].rearrange("b (t p) c -> p (b t) c", p=128), part(q)).then_inc(out_d, 16)
            sp.wait_ge(out_d, 16 * Q)

        @block.scalar
        def _(act):
            for q in range(Q + 1):
                if q < Q:
                    act.wait_ge(centred, q + 1)
                    wait(act, spread_done, q - 1)
                    act.activation(square[q % 2][:, :, :], part(q), ACT.Square).then_inc(squared, 1)
                if q >= 1:
                    act.wait_ge(var_done, q)
                    act.activation(std[:, q - 1, :], var[:, q - 1, :], ACT.Sqrt).then_inc(std_done, 1)

        @block.vector
        def _(dve):
            def centre(q):
                dve.reduce_sum(total[:, q, :], part(q), axis=AX_X).then_inc(summed, 1)
                dve.wait_ge(summed, q + 1)
                dve.tensor_scalar(mean[:, q, :], total[:, q, :], 1.0 / F, None, ALU.mult).then_inc(meant, 1)
                dve.wait_ge(meant, q + 1)
                dve.tensor_tensor(part(q), part(q), wide(mean, q), ALU.subtract).then_inc(centred, 1)

            def variance(q):
                dve.wait_ge(squared, q + 1)
                dve.reduce_sum(spread[:, q, :], square[q % 2][:, :, :], axis=AX_X).then_inc(spread_done, 1)
                dve.wait_ge(spread_done, q + 1)
                dve.tensor_scalar(var[:, q, :], spread[:, q, :], 1.0 / F, EPS, ALU.mult, ALU.add).then_inc(var_done, 1)

            def scale(q):
                dve.wait_ge(std_done, q + 1)
                dve.reciprocal(rstd[:, q, :], std[:, q, :]).then_inc(rstd_done, 1)
                dve.wait_ge(rstd_done, q + 1)
                dve.wait_ge(squared, q + 1)
                dve.tensor_tensor(part(q), part(q), wide(rstd, q), ALU.mult).then_inc(scaled, 1)

            for q in range(Q + 2):
                if q < Q:
                    centre(q)
                if 1 <= q < Q + 1:
                    variance(q - 1)
                if q >= 2:
                    scale(q - 2)


def industry(nc, k, x, xT, W_ind, ind_d):
    with ExitStack() as ctx:
        sb, pb, sem = sbuf(nc, ctx, "industry"), psum(nc, ctx, "industry"), semaphores(nc, ctx, "industry")
        xT_sb = sb("xT_sb", [F, B, N])
        w = sb("w", [F, F])
        ones = sb("ones", [128, 128], F32R)
        ones_raw = sb("ones_raw", [128, 128])
        deg = sb("deg", [128, N])
        rdeg = sb("rdeg", [128, N])
        v_hi = sb("v_hi", [128, NT, B, F], F32R)
        v_lo = sb("v_lo", [128, NT, B, F], F32R)
        out = [sb(f"out{i}", [128, N]) for i in range(2)]
        v_ps = [pb(f"v_ps{i}", [128, NT, F]) for i in range(2)]
        o_ps = [pb(f"o_ps{i}", [128, N]) for i in range(2)]
        d_ps = pb("d_ps", [128, N])
        (rows_in, w_in, ones_step, deg_sum, deg_step, v_filled, v_hi_done, v_lo_done, o_filled, o_scaled) = (sem(n) for n in (
            "rows_in", "w_in", "ones_step", "deg_sum", "deg_step", "v_filled", "v_hi_done", "v_lo_done", "o_filled",
            "o_scaled"))
        x_in = [sem(f"x_in{b}") for b in range(B)]
        out_d = [sem(f"out_d{i}") for i in range(2)]
        block = ctx.enter_context(nc.Block())

        @block.sync
        def _(sp):
            sp.dma_start(w[:, :], W_ind).then_inc(w_in, 16)
            for b in range(B):
                sp.dma_start(xT_sb[:, b, :], xT[b]).then_inc(x_in[b], 16)
            sp.dma_start(k.x[:, :, :], x.rearrange("b (t p) c -> p (b t) c", p=128)).then_inc(rows_in, 16)
            for p in range(B // 2):
                sp.wait_ge(o_scaled, p + 1)
                sp.dma_start(ind_d[2 * p:2 * p + 2].rearrange("b c n -> (b c) n"), out[p % 2][:, :]).then_inc(out_d[p % 2], 16)
            sp.wait_ge(rows_in, 16)
            for i in range(2):
                sp.wait_ge(out_d[i], 16 * (B // 4))

        @block.tensor
        def _(pe):
            pe.wait_ge(ones_step, 2)
            for c in range(2):
                for t in range(NT):
                    last = pe.matmul(d_ps[:, 512 * c:512 * c + 512], ones[:, :], k.adjT[:, t, 512 * c:512 * c + 512],
                                     start=(t == 0), stop=(t == NT - 1))
            last.then_inc(deg_sum, 1)
            pe.wait_ge(w_in, 16)
            for b in range(B):
                pe.wait_ge(x_in[b], 16)
                if b >= 2:
                    pe.wait_ge(v_lo_done, b - 1)
                for t in range(NT):
                    last = pe.matmul(v_ps[b % 2][:, t, :], xT_sb[:, b, 128 * t:128 * t + 128], w[:, :], start=True, stop=True)
                last.then_inc(v_filled, 1)
            for p in range(B // 2):
                pe.wait_ge(v_lo_done, 2 * p + 2)
                if p >= 2:
                    pe.wait_ge(o_scaled, p - 1)
                for t in range(NT):
                    for n, v in enumerate((v_hi, v_lo)):
                        for c in range(2):
                            last = pe.matmul(o_ps[p % 2][:, 512 * c:512 * c + 512],
                                             v[:, t, 2 * p:2 * p + 2, :].rearrange("p b c -> p (b c)"),
                                             k.adjT[:, t, 512 * c:512 * c + 512], start=(t == 0 and n == 0),
                                             stop=(t == NT - 1 and n == 1))
                last.then_inc(o_filled, 1)

        @block.scalar
        def _(act):
            for b in range(B):
                act.wait_ge(v_filled, b + 1)
                act.activation(v_hi[:, :, b, :], v_ps[b % 2][:, :, :], ACT.Copy).then_inc(v_hi_done, 1)

        @block.vector
        def _(dve):
            dve.memset(ones_raw[:, :], 1.0).then_inc(ones_step, 1)
            dve.wait_ge(ones_step, 1)
            dve.tensor_copy(ones[:, :], ones_raw[:, :]).then_inc(ones_step, 1)
            dve.wait_ge(deg_sum, 1)
            dve.tensor_scalar(deg[:, :], d_ps[:, :], 1.0, None, ALU.max).then_inc(deg_step, 1)
            dve.wait_ge(deg_step, 1)
            dve.reciprocal(rdeg[:, :], deg[:, :]).then_inc(deg_step, 1)
            for b in range(B):
                dve.wait_ge(v_hi_done, b + 1)
                dve.tensor_tensor(v_lo[:, :, b, :], v_ps[b % 2][:, :, :], v_hi[:, :, b, :].bitcast(F32),
                                  ALU.subtract).then_inc(v_lo_done, 1)
            dve.wait_ge(deg_step, 2)
            for p in range(B // 2):
                dve.wait_ge(o_filled, p + 1)
                if p >= 2:
                    dve.wait_ge(out_d[p % 2], 16 * (p // 2))
                dve.tensor_tensor(out[p % 2][:, :], o_ps[p % 2][:, :], rdeg[:, :], ALU.mult).then_inc(o_scaled, 1)


def hyperedges(nc, k, xT, w, d):
    L = 4
    with ExitStack() as ctx:
        sb, pb, sem = sbuf(nc, ctx, "hyperedges"), psum(nc, ctx, "hyperedges"), semaphores(nc, ctx, "hyperedges")
        W2 = sb("W2", [F, 2, F])
        vecs = sb("vecs", [F, 3])
        a_both = sb("a_both", [F, 2 * EDGES])
        fcW = sb("fcW", [F, 128])
        fcb = sb("fcb", [128, 1])
        av = sb("av", [128, 1])
        av_b = sb("av_b", [128, 128])

        def lanes(name, shape, dt=F32):
            return [sb(f"{name}{i}", shape, dt) for i in range(L)]

        xT_sb = lanes("xT_sb", [F, N])
        hT2 = lanes("hT2", [128, N])
        rows = lanes("rows", [128, NT, F])
        s_e = lanes("s_e", [EDGES, N])
        p_e = lanes("p_e", [EDGES, N])
        alpha = lanes("alpha", [EDGES, N])
        nmax = lanes("nmax", [EDGES, 1])
        den = lanes("den", [EDGES, 1])
        rden = lanes("rden", [EDGES, 1])
        agg2 = lanes("agg2", [EDGES, 2, F])
        aggT = lanes("aggT", [128, EDGES])
        agg = lanes("agg", [128, 3, EDGES // 2])
        low = lanes("low", [F, EDGES])
        elow = lanes("elow", [F, EDGES])
        he = lanes("he", [F, EDGES])
        tu = lanes("tu", [128, EDGES])
        qh = lanes("qh", [EDGES, 1])
        alphaT = coef = lanes("coef", [128, NT, EDGES])
        top = lanes("top", [128, NT])
        weight = lanes("weight", [128, NT])
        rweight = lanes("rweight", [128, NT])
        beta_st = lanes("beta_st", [128, N], F32R)
        coef_st = lanes("coef_st", [128, N], F32R)
        Z = [pb(f"Z{i}", [128, N]) for i in range(L)]
        names = ("w_in wide hT rows_f hT_sb rows_sb s_f s_sb s_leaky s_top p_sb alpha_done rden_done alphaT_f "
                 "alphaT_sb agg_f agg_done aggT_f aggT_sb low_done elow_done he_part he_done u_f tu_done q_done se_f "
                 "th_done lg_done top_done lg_less coef_exp weight_done rweight_done coef_done beta_done beta_hi beta_lo "
                 "coefT_f coef_hi coef_lo agg_parts out_d").split()
        S = dict((n, sem(n)) for n in names)
        x_in = [sem(f"x_in{l}") for l in range(L)]
        block = ctx.enter_context(nc.Block())
        lane_of = [(g * L + l, l) for g in range(B // L) for l in range(L)]

        def groups():
            for g in range(B // L):
                yield [(g * L + l, l) for l in range(L)]

        @block.sync
        def _(sp):
            def col(v):
                return v.rearrange("(p o) -> p o", o=1)
            for half in range(2):
                sp.dma_start(W2[:, half, :], w["W"]).then_inc(S["w_in"], 16)
            for n, name in enumerate(("a_node", "a_gn", "a_ge")):
                sp.dma_start(vecs[:, n:n + 1], col(w[name])).then_inc(S["w_in"], 16)
            sp.dma_start(fcW[:, :], w["fcW"]).then_inc(S["w_in"], 16)
            sp.dma_start(fcb[:, :], col(w["fcb"])).then_inc(S["w_in"], 16)
            sp.dma_start(av[:, :], col(w["av"])).then_inc(S["w_in"], 16)
            for bs in groups():
                for b, l in bs:
                    if b >= L:
                        sp.wait_ge(S["rows_f"], b - L + 1)
                    sp.dma_start(xT_sb[l][:, :], xT[b]).then_inc(x_in[l], 16)
                for b, l in bs:
                    sp.wait_ge(S["agg_parts"], b + 1)
                    sp.dma_start(d["agg"][b], agg[l][:, :, :]).then_inc(S["out_d"], 16)
                    sp.wait_ge(S["hT_sb"], b + 1)
                    sp.dma_start(d["hT"][b], hT2[l][:, :]).then_inc(S["out_d"], 16)
                    sp.wait_ge(S["beta_lo"], b + 1)
                    sp.dma_start(d["beta"][b], beta_st[l][:, :].bitcast(F32)).then_inc(S["out_d"], 16)
                    sp.wait_ge(S["coef_lo"], b + 1)
                    sp.dma_start(d["coef"][b], coef_st[l][:, :].bitcast(F32)).then_inc(S["out_d"], 16)
            sp.wait_ge(S["out_d"], 64 * B)

        @block.tensor
        def _(pe):
            pe.wait_ge(S["w_in"], 16 * 8)
            pe.wait_ge(S["wide"], 3)
            for bs in groups():
                for b, l in bs:
                    pe.wait_ge(x_in[l], 16 * (b // L + 1))
                    wait(pe, S["coef_lo"], b - L + 1)
                    for c in range(2):
                        last = pe.matmul(Z[l][:, 512 * c:512 * c + 512], W2[:, :, :].rearrange("p a c -> p (a c)"),
                                         xT_sb[l][:, 512 * c:512 * c + 512], start=True, stop=True)
                    last.then_inc(S["hT"], 1)
                for b, l in bs:
                    pe.wait_ge(S["hT_sb"], b + 1)
                    for t in range(NT):
                        last = pe.transpose(Z[l][:, F * t:F * t + F], hT2[l][0:F, 128 * t:128 * t + 128], k.ident[0:64, 0:64])
                    last.then_inc(S["rows_f"], 1)
                for b, l in bs:
                    pe.wait_ge(S["rows_sb"], b + 1)
                    for c in range(2):
                        last = pe.matmul(Z[l][:, 512 * c:512 * c + 512], a_both[:, :],
                                         hT2[l][0:F, 512 * c:512 * c + 512], start=True, stop=True)
                    last.then_inc(S["s_f"], 1)
                for b, l in bs:
                    pe.wait_ge(S["p_sb"], b + 1)
                    pe.wait_ge(S["alpha_done"], b + 1)
                    for t in range(NT):
                        last = pe.transpose(Z[l][:, EDGES * t:EDGES * t + EDGES], alpha[l][:, 128 * t:128 * t + 128],
                                            k.ident[0:64, 0:64])
                    last.then_inc(S["alphaT_f"], 1)
                for b, l in bs:
                    pe.wait_ge(S["alphaT_sb"], b + 1)
                    for t in range(NT):
                        last = pe.matmul(Z[l][0:EDGES, 0:F], alphaT[l][:, t, :], rows[l][:, t, :], start=(t == 0),
                                         stop=(t == NT - 1))
                    last.then_inc(S["agg_f"], 1)
                for b, l in bs:
                    pe.wait_ge(S["agg_done"], b + 1)
                    pe.transpose(Z[l][:, 0:EDGES], agg2[l][:, :, :].rearrange("p a c -> p (a c)"),
                                 k.ident[0:64, 0:64]).then_inc(S["aggT_f"], 1)
                for b, l in bs:
                    pe.wait_ge(S["he_done"], b + 1)
                    pe.matmul(Z[l][:, 0:EDGES], fcW[:, :], he[l][:, :], start=True, stop=True)
                    pe.matmul(Z[l][0:EDGES, 512:513], aggT[l][0:F, :], vecs[:, 2:3], start=True, stop=True).then_inc(S["u_f"], 1)
                for b, l in bs:
                    pe.wait_ge(S["tu_done"], b + 1)
                    pe.wait_ge(S["q_done"], b + 1)
                    pe.matmul(Z[l][:, 0:EDGES], av_b[:, :], tu[l][:, :], start=True, stop=True).then_inc(S["se_f"], 1)
                for b, l in bs:
                    pe.wait_ge(S["coef_done"], b + 1)
                    for t in range(NT):
                        last = pe.transpose(Z[l][0:EDGES, 128 * t:128 * t + 128], coef[l][:, t, :], k.ident[:, :])
                    last.then_inc(S["coefT_f"], 1)

        @block.scalar
        def _(act):
            for bs in groups():
                for b, l in bs:
                    act.wait_ge(S["rows_f"], b + 1)
                    act.activation(rows[l][:, :, :].rearrange("p t c -> p (t c)"), Z[l][:, 0:512], ACT.Copy).then_inc(S["rows_sb"], 1)
                for b, l in bs:
                    act.wait_ge(S["s_f"], b + 1)
                    act.activation(s_e[l][:, :], Z[l][0:EDGES, :], ACT.Copy).then_inc(S["s_sb"], 1)
                    act.activation(p_e[l][:, :], Z[l][EDGES:2 * EDGES, :], ACT.Copy).then_inc(S["p_sb"], 1)
                for b, l in bs:
                    act.wait_ge(S["s_top"], b + 1)
                    act.activation(alpha[l][:, :], alpha[l][:, :], ACT.Exp, bias=nmax[l][:, 0:1], scale=-1.0,
                                   accum_out=den[l][:, 0:1]).then_inc(S["alpha_done"], 1)
                for b, l in bs:
                    act.wait_ge(S["low_done"], b + 1)
                    act.activation(elow[l][:, :], low[l][:, :], ACT.Exp).then_inc(S["elow_done"], 1)
                for b, l in bs:
                    act.wait_ge(S["u_f"], b + 1)
                    act.activation(tu[l][:, :], Z[l][:, 0:EDGES], ACT.Tanh, bias=fcb[:, 0:1]).then_inc(S["tu_done"], 1)
                    act.activation(qh[l][:, :], Z[l][0:EDGES, 512:513], ACT.Copy, scale=0.5).then_inc(S["q_done"], 1)
                for b, l in bs:
                    act.wait_ge(S["q_done"], b + 1)
                    act.activation(p_e[l][:, :], p_e[l][:, :], ACT.Tanh, bias=qh[l][:, 0:1], scale=0.5).then_inc(S["th_done"], 1)
                for b, l in bs:
                    act.wait_ge(S["lg_less"], b + 1)
                    act.activation(coef[l][:, :, :], coef[l][:, :, :], ACT.Exp).then_inc(S["coef_exp"], 1)
                for b, l in bs:
                    act.wait_ge(S["beta_done"], b + 1)
                    act.activation(beta_st[l][0:64, :], p_e[l][:, :], ACT.Copy).then_inc(S["beta_hi"], 1)
                for b, l in bs:
                    act.wait_ge(S["coefT_f"], b + 1)
                    act.activation(coef_st[l][0:64, :], Z[l][0:EDGES, :], ACT.Copy).then_inc(S["coef_hi"], 1)

        @block.vector
        def _(dve):
            dve.wait_ge(S["w_in"], 16 * 8)
            dve.tensor_copy(a_both[:, 0:EDGES], vecs[:, 0:1].broadcast_to([F, EDGES])).then_inc(S["wide"], 1)
            dve.tensor_copy(a_both[:, EDGES:2 * EDGES], vecs[:, 1:2].broadcast_to([F, EDGES])).then_inc(S["wide"], 1)
            dve.tensor_copy(av_b[:, :], av[:, 0:1].broadcast_to([128, 128])).then_inc(S["wide"], 1)
            for bs in groups():
                for b, l in bs:
                    dve.wait_ge(S["hT"], b + 1)
                    wait(dve, S["out_d"], 64 * (b // L) * L)
                    dve.tensor_copy(hT2[l][:, :], Z[l][:, :]).then_inc(S["hT_sb"], 1)
                for b, l in bs:
                    dve.wait_ge(S["s_sb"], b + 1)
                    dve.scalar_tensor_tensor(out=s_e[l][:, :], in0=s_e[l][:, :], scalar=0.2, in1=s_e[l][:, :], op0=ALU.mult,
                                             op1=ALU.max).then_inc(S["s_leaky"], 1)
                for b, l in bs:
                    dve.wait_ge(S["s_leaky"], b + 1)
                    dve.tensor_tensor_reduce(alpha[l][:, :], s_e[l][:, :], k.mask_en[:, :], -1.0, 3.0e38, ALU.add, ALU.min,
                                             nmax[l][:, 0:1]).then_inc(S["s_top"], 1)
                for b, l in bs:
                    dve.wait_ge(S["alpha_done"], b + 1)
                    dve.reciprocal(rden[l][:, :], den[l][:, :]).then_inc(S["rden_done"], 1)
                for b, l in bs:
                    dve.wait_ge(S["alphaT_f"], b + 1)
                    dve.tensor_copy(alphaT[l][:, :, :].rearrange("p t e -> p (t e)"), Z[l][:, 0:512]).then_inc(S["alphaT_sb"], 1)
                for b, l in bs:
                    dve.wait_ge(S["agg_f"], b + 1)
                    dve.wait_ge(S["rden_done"], b + 1)
                    dve.tensor_scalar(agg2[l][:, :, :], Z[l][0:EDGES, 0:F].unsqueeze(1).broadcast_to([EDGES, 2, F]),
                                      rden[l][:, 0:1], None, ALU.mult).then_inc(S["agg_done"], 1)
                for b, l in bs:
                    dve.wait_ge(S["aggT_f"], b + 1)
                    dve.tensor_copy(aggT[l][:, :], Z[l][:, 0:EDGES]).then_inc(S["aggT_sb"], 1)
                for b, l in bs:
                    dve.wait_ge(S["aggT_sb"], b + 1)
                    for half in range(2):
                        p = slice(64 * half, 64 * half + 64)
                        mine = aggT[l][p, :].rearrange("p (i two) -> p i two", two=2)[:, :, half]
                        dve.tensor_copy(agg[l][p, 0, :], mine)
                        dve.tensor_scalar(agg[l][p, 1, :], mine, -1.0, None, ALU.mult)
                        last = dve.tensor_scalar(agg[l][p, 2, :], mine, 1.0, None, ALU.add)
                    last.then_inc(S["agg_parts"], 1)
                    dve.tensor_scalar(low[l][:, :], aggT[l][0:F, :], 0.0, None, ALU.min).then_inc(S["low_done"], 1)
                for b, l in bs:
                    dve.wait_ge(S["elow_done"], b + 1)
                    dve.scalar_tensor_tensor(out=low[l][:, :], in0=aggT[l][0:F, :], scalar=0.0, in1=elow[l][:, :], op0=ALU.max,
                                             op1=ALU.add).then_inc(S["he_part"], 1)
                for b, l in bs:
                    dve.wait_ge(S["he_part"], b + 1)
                    dve.tensor_scalar(he[l][:, :], low[l][:, :], -1.0, None, ALU.add).then_inc(S["he_done"], 1)
                for b, l in bs:
                    dve.wait_ge(S["se_f"], b + 1)
                    dve.tensor_tensor(coef[l][:, :, :], Z[l][:, 0:EDGES].unsqueeze(1).broadcast_to([128, NT, EDGES]),
                                      k.mask_ne[:, :, :], ALU.add).then_inc(S["lg_done"], 1)
                for b, l in bs:
                    dve.wait_ge(S["lg_done"], b + 1)
                    dve.tensor_reduce(top[l][:, :], coef[l][:, :, :], AX_X, ALU.max).then_inc(S["top_done"], 1)
                for b, l in bs:
                    dve.wait_ge(S["top_done"], b + 1)
                    dve.tensor_tensor(coef[l][:, :, :], coef[l][:, :, :],
                                      top[l][:, :].unsqueeze(2).broadcast_to([128, NT, EDGES]), ALU.subtract).then_inc(S["lg_less"], 1)
                for b, l in bs:
                    dve.wait_ge(S["th_done"], b + 1)
                    dve.tensor_scalar(p_e[l][:, :], p_e[l][:, :], 0.5, 0.5, ALU.mult, ALU.add).then_inc(S["beta_done"], 1)
                for b, l in bs:
                    dve.wait_ge(S["coef_exp"], b + 1)
                    dve.reduce_sum(weight[l][:, :], coef[l][:, :, :], axis=AX_X).then_inc(S["weight_done"], 1)
                for b, l in bs:
                    dve.wait_ge(S["weight_done"], b + 1)
                    dve.reciprocal(rweight[l][:, :], weight[l][:, :]).then_inc(S["rweight_done"], 1)
                for b, l in bs:
                    dve.wait_ge(S["rweight_done"], b + 1)
                    dve.tensor_tensor(coef[l][:, :, :], coef[l][:, :, :],
                                      rweight[l][:, :].unsqueeze(2).broadcast_to([128, NT, EDGES]), ALU.mult).then_inc(S["coef_done"], 1)
                for b, l in bs:
                    dve.wait_ge(S["beta_hi"], b + 1)
                    dve.tensor_tensor(beta_st[l][64:128, :], p_e[l][:, :], beta_st[l][0:64, :].bitcast(F32),
                                      ALU.subtract).then_inc(S["beta_lo"], 1)
                for b, l in bs:
                    dve.wait_ge(S["coef_hi"], b + 1)
                    dve.tensor_tensor(coef_st[l][64:128, :], Z[l][0:EDGES, :], coef_st[l][0:64, :].bitcast(F32),
                                      ALU.subtract).then_inc(S["coef_lo"], 1)


def messages(nc, k, d):
    PAIRS = EDGES // 2
    STEPS = 2 * PAIRS
    ITERS = B // 2
    ALL = B * PAIRS
    with ExitStack() as ctx:
        sb, pb, sem = sbuf(nc, ctx, "messages"), psum(nc, ctx, "messages"), semaphores(nc, ctx, "messages")
        sel = sb("sel", [128, PAIRS, 2, 64], F32R)
        hT = [sb(f"hT{i}", [128, N]) for i in range(2)]
        beta = [sb(f"beta{i}", [128, N], F32R) for i in range(2)]
        coef = [sb(f"coef{i}", [128, N], F32R) for i in range(2)]
        agg = [sb(f"agg{i}", [128, 3, PAIRS]) for i in range(2)]
        y = [sb(f"y{i}", [128, N]) for i in range(8)]
        e = [sb(f"e{i}", [128, N]) for i in range(4)]
        part = [sb(f"part{i}", [128, N]) for i in range(4)]
        g_sb = [sb(f"g_sb{i}", [F, N]) for i in range(2)]
        beta_ps = [pb(f"beta_ps{i}", [128, N]) for i in range(2)]
        coef_ps = pb("coef_ps", [128, N])
        g_ps = pb("g_ps", [F, N])
        op_in = [sem(f"op_in{i}") for i in range(2)]
        (sel_done, beta_f, coef_f, y_done, first_done, e_done, t_vector, t_pool, part_done, g_added, g_out, clamped,
         pool_turn) = (sem(n) for n in (
            "sel_done", "beta_f", "coef_f", "y_done", "first_done", "e_done", "t_vector", "t_pool", "part_done",
            "g_added", "g_out", "clamped", "pool_turn"))
        out_d = [sem(f"out_d{i}") for i in range(2)]
        block = ctx.enter_context(nc.Block())

        QUARTER = STEPS // 4

        def pool_count(it, s):
            return 3 * QUARTER * it + (3 * (s // 4) + s % 4)

        def exists(i, n):
            return not isinstance(i, int) or 0 <= i < n

        def run(eng, step):
            for s in range(STEPS):
                step(0, s)
            with eng.Fori(1, ITERS - 1) as it:
                for s in range(STEPS):
                    step(it, s)
            for s in range(STEPS):
                step(ITERS - 1, s)
            for s in range(5):
                step(ITERS, s)

        @block.sync
        def _(sp):
            def load(b, par, first):
                if not first:
                    sp.wait_ge(part_done, PAIRS * (b - 1))
                for name, t in (("hT", hT[par][:, :]), ("beta", beta[par][:, :].bitcast(F32)),
                                ("coef", coef[par][:, :].bitcast(F32)), ("agg", agg[par][:, :, :].rearrange("p a i -> p (a i)"))):
                    sp.dma_start(t, one(d[name][bass.ds(b, 1)] if name != "agg" else
                                        d[name][bass.ds(b, 1)].rearrange("o p a i -> o p (a i)"))).then_inc(op_in[par], 16)

            load(0, 0, True)
            load(1, 1, True)
            with sp.Fori(1, ITERS) as it:
                load(2 * it, 0, False)
                sp.wait_ge(g_out, 2 * it - 1)
                sp.dma_start(one(d["g"][bass.ds(2 * it - 2, 1)]), g_sb[0][:, :]).then_inc(out_d[0], 16)
                load(2 * it + 1, 1, False)
                sp.wait_ge(g_out, 2 * it)
                sp.dma_start(one(d["g"][bass.ds(2 * it - 1, 1)]), g_sb[1][:, :]).then_inc(out_d[1], 16)
            for par in range(2):
                sp.wait_ge(g_out, B - 1 + par)
                sp.dma_start(d["g"][B - 2 + par], g_sb[par][:, :]).then_inc(out_d[par], 16)
            for par in range(2):
                sp.wait_ge(out_d[par], 16 * (ITERS + par))

        @block.tensor
        def _(pe):
            pe.wait_ge(sel_done, 4)

            def fill_beta(n, s):
                par, i = (s // PAIRS) % 2, s % PAIRS
                wait(pe, y_done, n - 1)
                for c in range(2):
                    last = pe.matmul(beta_ps[s % 2][:, 512 * c:512 * c + 512], sel[:, i, :, :].rearrange("p a c -> p (a c)"),
                                     beta[par][:, 512 * c:512 * c + 512], start=True, stop=True)
                last.then_inc(beta_f, 1)

            pe.wait_ge(op_in[0], 64)
            fill_beta(0, 0)

            def step(it, s):
                n = STEPS * it + s
                par, i = s // PAIRS, s % PAIRS
                if exists(n + 1, ALL):
                    if i == PAIRS - 1:
                        nxt = 1 - par
                        if not (isinstance(it, int) and it == ITERS - 1 and par == 1):
                            pe.wait_ge(op_in[nxt], 64 * (it + par) + 64)
                if exists(n + 1, ALL):
                    fill_beta(n + 1, s + 1)
                if exists(n - 5, ALL):
                    j = (s - 5) % PAIRS
                    wait(pe, part_done, n - 4)
                    if j == 0:
                        wait(pe, g_out, 2 * it + (s - 5) // PAIRS)
                    for c in range(2):
                        last = pe.matmul(g_ps[:, 512 * c:512 * c + 512], k.two[:, :], part[(s - 5) % 4][:, 512 * c:512 * c + 512],
                                         start=(j == 0), stop=(j == PAIRS - 1))
                    last.then_inc(g_added, 1)
                if exists(n - 3, ALL):
                    wait(pe, part_done, n - 3)
                    i1, par1 = (s - 3) % PAIRS, ((s - 3) // PAIRS) % 2
                    for c in range(2):
                        last = pe.matmul(coef_ps[:, 512 * c:512 * c + 512], sel[:, i1, :, :].rearrange("p a c -> p (a c)"),
                                         coef[par1][:, 512 * c:512 * c + 512], start=True, stop=True)
                    last.then_inc(coef_f, 1)

            run(pe, step)

        @block.scalar
        def _(act):
            act.sem_inc(out_d[1], 16)

            def step(it, s):
                n = STEPS * it + s
                par, i = s // PAIRS, s % PAIRS
                if exists(n, ALL):
                    a = agg[par]
                    act.wait_ge(y_done, n + 1)
                    if s % 4 == 0:
                        wait(act, t_vector, QUARTER * it + s // 4)
                    else:
                        wait(act, t_pool, pool_count(it, s - 4))
                    ys, es = y[s % 8][:, :], e[s % 4][:, :]
                    if s % 4 == 2:
                        act.activation(es, ys, ACT.Exp, bias=a[:, 0, i:i + 1]).then_inc(first_done, 1)
                        act.wait_ge(first_done, n + 1)
                        act.activation(ys, ys, ACT.Relu, bias=a[:, 0, i:i + 1]).then_inc(e_done, 1)
                    else:
                        act.activation(es, ys, ACT.Relu, bias=a[:, 1, i:i + 1], scale=-1.0).then_inc(first_done, 1)
                        if s % 4:
                            act.activation(ys, ys, ACT.Relu, bias=a[:, 0, i:i + 1])
                        act.wait_ge(first_done, n + 1)
                        act.activation(es, es, ACT.Exp, scale=-1.0).then_inc(e_done, 1)
                if i == 4:
                    b = 2 * it + (s - 5) // PAIRS
                    if exists(b, B):
                        p = (par + 1) % 2
                        wait(act, out_d[p], 16 * it)
                        act.wait_ge(g_added, PAIRS * (b + 1))
                        act.activation(g_sb[p][:, :], g_ps[:, :], ACT.Copy, bias=-1.0).then_inc(g_out, 1)

            run(act, step)

        @block.gpsimd
        def _(pool):
            def step(it, s):
                n = STEPS * it + s
                if s % 4 and exists(n, ALL):
                    ys, es = y[s % 8][:, :], e[s % 4][:, :]
                    pool.wait_ge(e_done, n + 1)
                    if s % 4 == 2:
                        pool.sem_inc(pool_turn, 1)
                        pool.tensor_scalar(es, es, 1.0, None, ALU.min).then_inc(clamped, 1)
                        pool.wait_ge(clamped, QUARTER * it + s // 4 + 1)
                    pool.tensor_tensor(ys, ys, es, ALU.add).then_inc(t_pool, 1)

            run(pool, step)

        @block.vector
        def _(dve):
            for half in range(2):
                for p in (slice(0, 64), slice(64, 128)):
                    mine = k.two[p, :].rearrange("p (i two) -> p i two", two=2)[:, :, half]
                    dve.tensor_copy(sel[p, :, half, :], mine.unsqueeze(2).broadcast_to([64, PAIRS, 64])).then_inc(sel_done, 1)

            def step(it, s):
                n = STEPS * it + s
                par, i = s // PAIRS, s % PAIRS
                if exists(n, ALL):
                    if i == 0:
                        dve.wait_ge(op_in[par], 64 * it + 64)
                    wait(dve, part_done, n - 7)
                    dve.wait_ge(beta_f, n + 1)
                    dve.scalar_tensor_tensor(out=y[s % 8][:, :], in0=hT[par][:, :], scalar=agg[par][:, 0, i:i + 1],
                                             in1=beta_ps[s % 2][:, :], op0=ALU.subtract, op1=ALU.mult).then_inc(y_done, 1)
                if s % 4 == 2 and exists(n - 2, ALL):
                    yq = y[(s - 2) % 8]
                    a = agg[((s - 2) // PAIRS) % 2]
                    j = (s - 2) % PAIRS
                    dve.wait_ge(e_done, n - 1)
                    dve.scalar_tensor_tensor(out=yq[:, :], in0=yq[:, :], scalar=a[:, 2, j:j + 1], in1=e[(s - 2) % 4][:, :],
                                             op0=ALU.add, op1=ALU.max).then_inc(t_vector, 1)
                if exists(n - 4, ALL):
                    wait(dve, g_added, n - 7)
                    dve.wait_ge(coef_f, n - 3)
                    if s % 4 == 0:
                        dve.wait_ge(t_vector, QUARTER * it + s // 4)
                    else:
                        dve.wait_ge(t_pool, pool_count(it, s - 4))
                    dve.tensor_tensor(part[s % 4][:, :], y[(s - 4) % 8][:, :], coef_ps[:, :], ALU.mult).then_inc(part_done, 1)

            run(dve, step)


def mix(nc, k, w, d):
    with ExitStack() as ctx:
        sb, pb, sem = sbuf(nc, ctx, "mix"), psum(nc, ctx, "mix"), semaphores(nc, ctx, "mix")
        fcW = sb("fcW", [F, 128])
        fcb = sb("fcb", [128, 1])
        av = sb("av", [128, 1])
        av_b = sb("av_b", [128, F])
        g = [sb(f"g{i}", [F, N]) for i in range(B)]
        ind = [sb(f"ind{i}", [F, N]) for i in range(B)]
        tg = [sb(f"tg{i}", [128, N]) for i in range(2)]
        ti = [sb(f"ti{i}", [128, N]) for i in range(2)]
        c = [sb(f"c{i}", [F, N]) for i in range(2)]
        o = [sb(f"o{i}", [F, N]) for i in range(2)]
        g_ps, i_ps, d_ps = pb("g_ps", [128, N]), pb("i_ps", [128, N]), pb("d_ps", [F, N])
        r_ps = pb("r_ps", [128, NT, F])
        (w_in, wide, u_f, tg_done, ti_done, d_f, c_done, diff_done, mixed, o_done, r_f, r_done, less_done) = (sem(n) for n in (
            "w_in", "wide", "u_f", "tg_done", "ti_done", "d_f", "c_done", "diff_done", "mixed", "o_done", "r_f",
            "r_done", "less_done"))
        in_ = [sem(f"in{i}") for i in range(B)]
        block = ctx.enter_context(nc.Block())

        @block.sync
        def _(sp):
            sp.dma_start(fcW[:, :], w["fcW"]).then_inc(w_in, 16)
            sp.dma_start(fcb[:, :], w["fcb"].rearrange("(p o) -> p o", o=1)).then_inc(w_in, 16)
            sp.dma_start(av[:, :], w["av"].rearrange("(p o) -> p o", o=1)).then_inc(w_in, 16)
            for b in range(B):
                sp.dma_start(g[b][:, :], d["g"][b]).then_inc(in_[b], 16)
                sp.dma_start(ind[b][:, :], d["ind"][b]).then_inc(in_[b], 16)

        @block.tensor
        def _(pe):
            pe.wait_ge(w_in, 48)
            pe.wait_ge(wide, 1)
            for n in range(B + 2):
                b = n
                if b < B:
                    pe.wait_ge(in_[b], 32)
                    wait(pe, tg_done, b)
                    wait(pe, ti_done, b)
                    for src, ps in ((g, g_ps), (ind, i_ps)):
                        for ch in range(2):
                            s = slice(512 * ch, 512 * ch + 512)
                            last = pe.matmul(ps[:, s], fcW[:, :], src[b][:, s], start=True, stop=True)
                        last.then_inc(u_f, 1)
                b = n - 1
                if 0 <= b < B:
                    pe.wait_ge(less_done, b + 1)
                    wait(pe, c_done, b)
                    for ch in range(2):
                        s = slice(512 * ch, 512 * ch + 512)
                        last = pe.matmul(d_ps[:, s], av_b[:, :], ti[b % 2][:, s], start=True, stop=True)
                    last.then_inc(d_f, 1)
                b = n - 2
                if 0 <= b < B:
                    pe.wait_ge(o_done, b + 1)
                    wait(pe, r_done, b)
                    for t in range(NT):
                        last = pe.transpose(r_ps[:, t, :], o[b % 2][:, 128 * t:128 * t + 128], k.ident[0:64, 0:64])
                    last.then_inc(r_f, 1)

        @block.scalar
        def _(act):
            act.wait_ge(w_in, 48)
            for n in range(B + 1):
                b = n
                if b < B:
                    wait(act, d_f, b - 1)
                    act.wait_ge(u_f, 2 * b + 1)
                    act.activation(tg[b % 2][:, :], g_ps[:, :], ACT.Tanh, bias=fcb[:, 0:1]).then_inc(tg_done, 1)
                    act.wait_ge(u_f, 2 * b + 2)
                    act.activation(ti[b % 2][:, :], i_ps[:, :], ACT.Tanh, bias=fcb[:, 0:1]).then_inc(ti_done, 1)
                b = n - 1
                if 0 <= b < B:
                    act.wait_ge(d_f, b + 1)
                    wait(act, mixed, b - 1)
                    act.activation(c[b % 2][:, :], d_ps[:, :], ACT.Tanh, scale=0.5).then_inc(c_done, 1)

        @block.gpsimd
        def _(pool):
            for b in range(B):
                pool.wait_ge(tg_done, b + 1)
                pool.wait_ge(ti_done, b + 1)
                pool.tensor_tensor(ti[b % 2][:, :], ti[b % 2][:, :], tg[b % 2][:, :], ALU.subtract).then_inc(less_done, 1)

        @block.vector
        def _(dve):
            dve.wait_ge(w_in, 48)
            dve.tensor_copy(av_b[:, :], av[:, 0:1].broadcast_to([128, F])).then_inc(wide, 1)
            for n in range(B + 1):
                b = n
                if b < B:
                    p = b % 2
                    dve.wait_ge(in_[b], 32)
                    wait(dve, r_f, b - 1)
                    dve.tensor_tensor(o[p][:, :], ind[b][:, :], g[b][:, :], ALU.subtract).then_inc(diff_done, 1)
                    dve.wait_ge(diff_done, b + 1)
                    dve.wait_ge(c_done, b + 1)
                    dve.scalar_tensor_tensor(out=c[p][:, :], in0=c[p][:, :], scalar=1.0, in1=o[p][:, :], op0=ALU.add,
                                             op1=ALU.mult).then_inc(mixed, 1)
                    dve.wait_ge(mixed, b + 1)
                    dve.scalar_tensor_tensor(out=o[p][:, :], in0=c[p][:, :], scalar=0.5, in1=g[b][:, :], op0=ALU.mult,
                                             op1=ALU.add).then_inc(o_done, 1)
                b = n - 1
                if 0 <= b < B:
                    dve.wait_ge(r_f, b + 1)
                    xb = k.x[:, NT * b:NT * b + NT, :]
                    dve.tensor_tensor(xb, r_ps[:, :, :], xb, ALU.add).then_inc(r_done, 1)


def split_heads(nc, k, WhT, bhT, d):
    with ExitStack() as ctx:
        sb, pb, sem = sbuf(nc, ctx, "split_heads"), psum(nc, ctx, "split_heads"), semaphores(nc, ctx, "split_heads")
        x_cols = [sb(f"x_cols{i}", [F, 2, N], F32R) for i in range(2)]
        x_rows = [sb(f"x_rows{i}", [128, NT, 2, F], F32R) for i in range(2)]
        wT = sb("wT", [128, HEADS, 2, F])
        g_stack = sb("g_stack", [128, HEADS, 2 * F], F32R)
        bias = sb("bias", [128, HEADS])
        bias_parts = sb("bias_parts", [128, HEADS, 2])
        xT = [pb(f"xT{i}", [F, 512]) for i in range(4)]
        g_ps = pb("g_ps", [128, HEADS, 2 * F])
        w_in, x_turned, x_hi, x_lo, rows_hi, rows_lo, g_f, g_hi, g_lo, bias_done, g_out = (sem(n) for n in (
            "w_in", "x_turned", "x_hi", "x_lo", "rows_hi", "rows_lo", "g_f", "g_hi", "g_lo", "bias_done",
            "g_out"))
        cols_out = [sem(f"cols_out{i}") for i in range(2)]
        rows_out = [sem(f"rows_out{i}") for i in range(2)]
        block = ctx.enter_context(nc.Block())

        @block.sync
        def _(sp):
            for half in range(2):
                sp.dma_start(wT[:, :, half, :], WhT.rearrange("h d c -> d h c")).then_inc(w_in, 16)
            sp.dma_start(bias[:, :], bhT).then_inc(w_in, 16)
            for b in range(B):
                sp.wait_ge(rows_lo, b + 1)
                sp.dma_start(d["x_rows"][b], x_rows[b % 2][:, :, :, :].bitcast(F32)).then_inc(rows_out[b % 2], 16)
                sp.wait_ge(x_lo, 2 * b + 2)
                sp.dma_start(d["x_cols"][b], x_cols[b % 2][:, :, :].bitcast(F32)).then_inc(cols_out[b % 2], 16)
            sp.wait_ge(g_lo, 1)
            sp.dma_start(d["g_heads"].rearrange("h p c -> p h c"), g_stack[:, :, :].bitcast(F32)).then_inc(g_out, 16)
            sp.wait_ge(bias_done, 2)
            sp.dma_start(d["bias"].rearrange("h p c -> p h c"), bias_parts[:, :, :]).then_inc(g_out, 16)
            sp.wait_ge(g_out, 32)
            for p in range(2):
                sp.wait_ge(rows_out[p], 16 * (B // 2))
                sp.wait_ge(cols_out[p], 16 * (B // 2))

        @block.tensor
        def _(pe):
            for n in range(2 * B):
                wait(pe, x_lo, n - 3)
                for i in range(4):
                    last = pe.transpose(xT[n % 4][:, 128 * i:128 * i + 128], k.x[:, 4 * n + i, :], k.ident[:, :])
                last.then_inc(x_turned, 1)
            pe.wait_ge(w_in, 48)
            for h in range(HEADS):
                w = wT[:, h, :, :].rearrange("p a c -> p (a c)")
                last = pe.matmul(g_ps[:, h, :], w, w, start=True, stop=True)
            last.then_inc(g_f, 1)

        @block.scalar
        def _(act):
            for n in range(2 * B):
                b, half = n // 2, slice(512 * (n % 2), 512 * (n % 2) + 512)
                if n % 2 == 0:
                    wait(act, rows_out[b % 2], 16 * (b // 2))
                    act.activation(x_rows[b % 2][:, :, 0, :], k.x[:, NT * b:NT * b + NT, :], ACT.Copy).then_inc(rows_hi, 1)
                    wait(act, cols_out[b % 2], 16 * (b // 2))
                act.wait_ge(x_turned, n + 1)
                act.activation(x_cols[b % 2][:, 0, half], xT[n % 4][:, :], ACT.Copy).then_inc(x_hi, 1)
            act.wait_ge(g_f, 1)
            act.activation(g_stack[:, :, :], g_ps[:, :, :], ACT.Copy).then_inc(g_hi, 1)

        @block.vector
        def _(dve):
            for n in range(2 * B):
                b, half = n // 2, slice(512 * (n % 2), 512 * (n % 2) + 512)
                if n % 2 == 0:
                    dve.wait_ge(rows_hi, b + 1)
                    wait(dve, rows_out[b % 2], 16 * (b // 2))
                    dve.tensor_tensor(x_rows[b % 2][:, :, 1, :], k.x[:, NT * b:NT * b + NT, :],
                                      x_rows[b % 2][:, :, 0, :].bitcast(F32), ALU.subtract).then_inc(rows_lo, 1)
                    wait(dve, cols_out[b % 2], 16 * (b // 2))
                dve.wait_ge(x_hi, n + 1)
                dve.tensor_tensor(x_cols[b % 2][:, 1, half], xT[n % 4][:, :], x_cols[b % 2][:, 0, half].bitcast(F32),
                                  ALU.subtract).then_inc(x_lo, 1)
            dve.wait_ge(w_in, 48)
            for n, scale in enumerate((LEAK_UP, LEAK)):
                dve.tensor_scalar(bias_parts[:, :, n], bias[:, :], scale, None, ALU.mult).then_inc(bias_done, 1)
            dve.wait_ge(g_hi, 1)
            low = g_stack[64:128, :, :]
            dve.tensor_tensor(low, g_ps[64:128, :, :], low.bitcast(F32), ALU.subtract).then_inc(g_lo, 1)


def heads(nc, k, d, Wh, Wout):
    U = B * HEADS
    ITERS = U // 2
    J_ALL, C_ALL = U * 16, U * 2
    with ExitStack() as ctx:
        sb, pb, sem = sbuf(nc, ctx, "heads"), psum(nc, ctx, "heads"), semaphores(nc, ctx, "heads")
        x_cols = sb("x_cols", [128, 2 * 2 * N], F32R)
        g_st = [sb(f"g_st{i}", [128, 2 * F], F32R) for i in range(2)]
        x_rows = [sb(f"x_rows{i}", [128, NT, 2 * F], F32R) for i in range(2)]
        w_twice = [sb(f"w_twice{i}", [128, D]) for i in range(2)]
        bias = [sb(f"bias{i}", [128, 2]) for i in range(2)]
        w_out = [sb(f"w_out{i}", [128, F]) for i in range(2)]
        y_st = [sb(f"y_st{i}", [128, N], F32R) for i in range(2)]
        neg = [sb(f"neg{i}", [128, N]) for i in range(2)]
        nmax = sb("nmax", [128, 2, 1])
        P = [sb(f"P{i}", [128, 4, N]) for i in range(2)]
        den = [sb(f"den{i}", [128, 4]) for i in range(2)]
        rden = [sb(f"rden{i}", [128, 4]) for i in range(2)]
        PTh = [sb(f"PTh{i}", [128, 512], F32R) for i in range(4)]
        PTl = [sb(f"PTl{i}", [128, 512], F32R) for i in range(4)]
        rB = sb("rB", [128, 512])
        att = sb("att", [128, 512])
        pos = sb("pos", [128, 512])
        leak = sb("leak", [128, 512])
        cat = [sb(f"cat{i}", [128, 512]) for i in range(2)]
        S_ps = [pb(f"S_ps{i}", [128, N]) for i in range(2)]
        T_ps = [pb(f"T_ps{i}", [128, 512]) for i in range(2)]
        O_ps = [pb(f"O_ps{i}", [128, 512]) for i in range(2)]
        g_in = [sem(f"g_in{i}") for i in range(2)]
        late_in = [sem(f"late_in{i}") for i in range(2)]
        (x_in, s_filled, s_taken, y_hi, exp_done, turned, pt_hi, pt_lo, av_done, r_ready, rb_turned, rb_done, att_done,
         z_filled, z_done, cat_done, h2_done, acc_done, zeroed, max_turn, x_turn, load_turn) = (sem(n) for n in (
            "x_in", "s_filled", "s_taken", "y_hi", "exp_done", "turned", "pt_hi", "pt_lo", "av_done", "r_ready",
            "rb_turned", "rb_done", "att_done", "z_filled", "z_done", "cat_done", "h2_done", "acc_done", "zeroed",
            "max_turn", "x_turn", "load_turn"))
        block = ctx.enter_context(nc.Block())

        S_POS = [0, 1, 2, 3, 4, 5, 7, 8]
        Y_POS = 6

        def item(it, hp, pos):
            return 18 * it + (9 * hp + pos + 1)

        def s_bank(hp, pos):
            return S_ps[(9 * hp + pos + 1) % 2]

        def t_bank(c, j):
            return T_ps[(9 * c + j + (j > 5)) % 2]

        def recip_bank(c):
            return T_ps[(9 * c + 6) % 2]

        def s_pos(it, hp, i):
            return i if isinstance(it, int) and it == ITERS - 1 and hp == 1 else S_POS[i]

        def last_unit(it, hp):
            return isinstance(it, int) and it == ITERS - 1 and hp == 1

        def exists(i, n):
            return not isinstance(i, int) or 0 <= i < n

        def run(eng, slot):
            for s in range(16):
                slot(0, s, False)
            with eng.Fori(1, ITERS - 1) as it:
                for s in range(16):
                    slot(it, s, False)
            for s in range(16):
                slot(ITERS - 1, s, False)
            for s in range(9):
                slot(ITERS, s, True)

        @block.sync
        def _(sp):
            def load_x(b):
                wait(sp, s_filled, 72 * b - 71)
                sp.sem_inc(load_turn, 1)
                wait(sp, x_in, 32 * b)
                sp.sem_inc(load_turn, 1)
                for half in range(2):
                    sp.dma_start(x_cols[64 * half:64 * half + 64, bass.ds((b % 2) * (2 * N), 2 * N)].bitcast(F32),
                                 d["x_cols"][bass.ds(b, 1)].rearrange("o p a n -> (o p) (a n)")).then_inc(x_in, 16)

            def load_g(u, h, par):
                wait(sp, s_filled, 9 * u - 17)
                sp.sem_inc(load_turn, 1)
                sp.dma_start(g_st[par][:, :].bitcast(F32), d["g_heads"][bass.ds(h, 1)].rearrange("o p c -> (o p) c")).then_inc(g_in[par], 16)

            def load_late(u, b, h, par):
                wait(sp, h2_done, 2 * u - 2)
                sp.sem_inc(load_turn, 1)
                sp.dma_start(x_rows[par][:, :, :].rearrange("p t c -> p (t c)").bitcast(F32),
                             d["x_rows"][bass.ds(b, 1)].rearrange("o p t a c -> (o p) (t a c)")).then_inc(late_in[par], 16)
                for half in range(2):
                    sp.dma_start(w_twice[par][64 * half:64 * half + 64, :],
                                 Wh[bass.ds(h, 1)].rearrange("o c d -> (o c) d")).then_inc(late_in[par], 16)
                sp.dma_start(bias[par][:, :], d["bias"][bass.ds(h, 1)].rearrange("o p c -> (o p) c")).then_inc(late_in[par], 16)
                sp.dma_start(w_out[par][:, :], Wout[bass.ds(h, 1)].rearrange("o d f -> (o d) f")).then_inc(late_in[par], 16)

            def iteration(b, i):
                for par in range(2):
                    u, h = 8 * b + (2 * i + par), 2 * i + par
                    load_g(u, h, par)
                    load_late(u, b, h, par)

            load_g(0, 0, 0)
            load_x(0)
            load_g(1, 1, 1)
            load_late(0, 0, 0, 0)
            load_late(1, 0, 1, 1)
            load_x(1)
            for i in range(1, 4):
                iteration(0, i)
            with sp.Fori(1, B - 1) as b:
                iteration(b, 0)
                load_x(b + 1)
                for i in range(1, 4):
                    iteration(b, i)
            for i in range(4):
                iteration(B - 1, i)

        @block.tensor
        def _(pe):
            def x_part(batch, part, c):
                at = (batch % 2) * (2 * N) + (N * part + 512 * c)
                return x_cols[:, at:at + 512] if isinstance(at, int) else x_cols[:, bass.ds(at, 512)]

            def project(it, nxt, par, bank, r):
                batch = (2 * it + nxt) // 8
                pe.wait_ge(g_in[par], 16 * (it + nxt // 2) + 16)
                pe.wait_ge(x_in, 32 * batch + 32)
                wait(pe, s_taken, r - 1)
                pe.sem_inc(x_turn, 1)
                for part in range(2):
                    for c in range(2):
                        last = pe.matmul(bank[:, 512 * c:512 * c + 512], g_st[par][:, :], x_part(batch, part, c),
                                         start=(part == 0), stop=(part == 1))
                last.then_inc(s_filled, 1)

            project(0, 0, 0, S_ps[0], 0)

            def slot(it, s, tail):
                hp, i = s // 8, s % 8
                if not tail:
                    pos = s_pos(it, hp, i)
                    r = item(it, hp, pos)
                    wait(pe, s_taken, 1 if isinstance(r, int) and r == 1 else r - 1)
                    pe.sem_inc(x_turn, 1)
                    ps = s_bank(hp, pos)
                    for part in range(2):
                        for c in range(2):
                            last = pe.matmul(ps[:, 512 * c:512 * c + 512], y_st[hp][:, 128 * i:128 * i + 128],
                                             x_part(it // 4, part, c), start=(part == 0), stop=(part == 1))
                    last.then_inc(s_filled, 1)
                    if i == 5 and not last_unit(it, hp):
                        project(it, hp + 1, 1 - hp, s_bank(hp, Y_POS), item(it, hp, Y_POS))
                if s % 4 == 0:
                    c = (s - 8) // 4
                    C = 4 * it + c
                    if exists(C, C_ALL):
                        wait(pe, r_ready, C + 1)
                        wait(pe, pt_lo, 8 * C + 5)
                        for q in range(4):
                            last = pe.transpose(recip_bank(c)[:, 128 * q:128 * q + 128],
                                                rden[c % 2][:, q:q + 1].broadcast_to([128, 128]), k.ident[:, :])
                        last.then_inc(rb_turned, 1)
                if s % 4 == 0:
                    c = (s - 12) // 4
                    C = 4 * it + c
                    if exists(C, C_ALL):
                        wait(pe, cat_done, C + 1)
                        pe.matmul(O_ps[c % 2][0:F, :], w_out[(c // 2) % 2][:, :], cat[c % 2][:, :], start=True,
                                  stop=True).then_inc(h2_done, 1)
                for a in range(2):
                    n = 2 * s - 10 + a
                    J, c, j = 32 * it + n, n // 8, n % 8
                    if exists(J, J_ALL):
                        if j == 0:
                            wait(pe, exp_done, 16 * it + 4 * c + 4)
                        if j == 7:
                            wait(pe, rb_done, 4 * it + c + 1)
                        else:
                            wait(pe, pt_lo, J if j == 6 else J - 1)
                        for q in range(4):
                            last = pe.transpose(t_bank(c, j)[:, 128 * q:128 * q + 128], P[c % 2][:, q, 128 * j:128 * j + 128],
                                                k.ident[:, :])
                        last.then_inc(turned, 1)
                    n = 2 * s - 12 + a
                    V, c, v = 32 * it + n, n // 8, n % 8
                    if exists(V, J_ALL):
                        u = c // 2
                        if v == 0:
                            wait(pe, acc_done, 4 * it + c - 1)
                            pe.wait_ge(late_in[u % 2], 80 * (it + u // 2) + 80)
                        wait(pe, pt_lo, V + 1)
                        for part in (PTh, PTl):
                            last = pe.matmul(O_ps[c % 2][:, :], x_rows[u % 2][:, v, :], part[v % 4][:, :],
                                             start=(v == 0 and part is PTh), stop=(v == 7 and part is PTl))
                        last.then_inc(av_done, 1)
                if s % 4 == 2:
                    c = (s - 10) // 4
                    C = 4 * it + c
                    if exists(C, C_ALL):
                        wait(pe, att_done, C + 1)
                        pe.matmul(O_ps[c % 2][:, :], w_twice[(c // 2) % 2][:, :], att[:, :], start=True,
                                  stop=True).then_inc(z_filled, 1)

            run(pe, slot)

        @block.scalar
        def _(act):
            def take_hi(r, par, bank):
                act.wait_ge(s_filled, r + 1)
                act.activation(y_st[par][:, :], bank[:, :], ACT.Copy).then_inc(y_hi, 1)

            take_hi(0, 0, S_ps[0])

            def slot(it, s, tail):
                hp, i = s // 8, s % 8
                if s % 4 == 0:
                    c = (s - 8) // 4
                    C = 4 * it + c
                    if exists(C, C_ALL):
                        wait(act, rb_turned, C + 1)
                        wait(act, att_done, C)
                        act.activation(rB[:, :], recip_bank(c)[:, :], ACT.Copy).then_inc(rb_done, 1)
                for a in range(2):
                    n = 2 * s - 10 + a
                    J, c, j = 32 * it + n, n // 8, n % 8
                    if exists(J, J_ALL):
                        act.wait_ge(turned, J + 1)
                        wait(act, av_done, J - 3)
                        act.activation(PTh[j % 4][:, :], t_bank(c, j)[:, :], ACT.Copy).then_inc(pt_hi, 1)
                if not tail:
                    if i == 5 and not last_unit(it, hp):
                        take_hi(item(it, hp, Y_POS), 1 - hp, s_bank(hp, Y_POS))
                    r = item(it, hp, s_pos(it, hp, i))
                    c = s // 4
                    act.wait_ge(s_taken, r + 1)
                    if i % 4 == 0:
                        wait(act, turned, 32 * it + 8 * (c - 1))
                    act.activation(P[c % 2][:, i % 4, :], neg[i % 2][:, :], ACT.Exp, bias=nmax[:, i % 2, :], scale=-1.0,
                                   accum_out=den[c % 2][:, i % 4:i % 4 + 1]).then_inc(exp_done, 1)
                if s % 4 == 2:
                    c = (s - 10) // 4
                    C = 4 * it + c
                    par = (c // 2) % 2
                    if exists(C, C_ALL):
                        wait(act, z_filled, C + 1)
                        wait(act, cat_done, C)
                        act.activation(pos[:, :], O_ps[c % 2][:, :], ACT.Relu, bias=bias[par][:, 0:1], scale=LEAK_UP)
                        act.activation(leak[:, :], O_ps[c % 2][:, :], ACT.Identity, bias=bias[par][:, 1:2],
                                       scale=LEAK).then_inc(z_done, 1)

            run(act, slot)

        @block.gpsimd
        def _(pool):
            def slot(it, s, tail):
                if s % 4 == 3:
                    c = (s - 11) // 4
                    C = 4 * it + c
                    if exists(C, C_ALL):
                        pool.wait_ge(z_done, C + 1)
                        wait(pool, h2_done, C - 1)
                        pool.tensor_tensor(cat[c % 2][:, :], pos[:, :], leak[:, :], ALU.add).then_inc(cat_done, 1)

            run(pool, slot)

        @block.vector
        def _(dve):
            def take_lo(y_count, par, bank):
                dve.wait_ge(y_hi, y_count)
                low = y_st[par][64:128, :]
                dve.tensor_tensor(low, bank[64:128, :], low.bitcast(F32), ALU.subtract).then_inc(s_taken, 1)

            dve.memset(k.acc[:, :], 0.0).then_inc(zeroed, 1)
            take_lo(1, 0, S_ps[0])
            dve.wait_ge(zeroed, 1)

            def slot(it, s, tail):
                hp, i = s // 8, s % 8
                if not tail:
                    pos = s_pos(it, hp, i)
                    r = item(it, hp, pos)
                    wait(dve, exp_done, 16 * it + (s - 1))
                    dve.wait_ge(s_filled, r + 1)
                    dve.sem_inc(max_turn, 1)
                    dve.tensor_tensor_reduce(neg[i % 2][:, :], s_bank(hp, pos)[:, :], k.mask[:, i, :], -1.0, 3.0e38,
                                             ALU.add, ALU.min, nmax[:, i % 2, :]).then_inc(s_taken, 1)
                for a in range(2):
                    n = 2 * s - 10 + a
                    J, c, j = 32 * it + n, n // 8, n % 8
                    if exists(J, J_ALL):
                        dve.wait_ge(pt_hi, J + 1)
                        dve.tensor_tensor(PTl[j % 4][:, :], t_bank(c, j)[:, :], PTh[j % 4][:, :].bitcast(F32),
                                          ALU.subtract).then_inc(pt_lo, 1)
                if s % 4 == 1:
                    c = (s - 5) // 4
                    C = 4 * it + c
                    if exists(C, C_ALL):
                        wait(dve, exp_done, 4 * C + 4)
                        wait(dve, rb_turned, C - 1)
                        dve.reciprocal(rden[c % 2][:, :], den[c % 2][:, :]).then_inc(r_ready, 1)
                    c = (s - 9) // 4
                    C = 4 * it + c
                    if exists(C, C_ALL):
                        wait(dve, av_done, 8 * C + 8)
                        wait(dve, rb_done, C + 1)
                        wait(dve, z_filled, C)
                        dve.tensor_tensor(att[:, :], O_ps[c % 2][:, :], rB[:, :], ALU.mult).then_inc(att_done, 1)
                if s % 4 == 0:
                    c = (s - 12) // 4
                    C = 4 * it + c
                    if exists(C, C_ALL):
                        at = ((2 * it + c // 2) // 8) * N + 512 * (c % 2)
                        mine = k.acc[:, at:at + 512] if isinstance(at, int) else k.acc[:, bass.ds(at, 512)]
                        wait(dve, h2_done, C + 1)
                        dve.tensor_tensor(mine, O_ps[c % 2][0:F, :], mine, ALU.add).then_inc(acc_done, 1)

                if not tail and i == 5 and not last_unit(it, hp):
                    take_lo(2 * it + hp + 2, 1 - hp, s_bank(hp, Y_POS))

            run(dve, slot)


def split_output(nc, k, d):
    with ExitStack() as ctx:
        sb, pb, sem = sbuf(nc, ctx, "split_output"), psum(nc, ctx, "split_output"), semaphores(nc, ctx, "split_output")
        hi_lo = [sb(f"hi_lo{i}", [128, N], F32R) for i in range(2)]
        lo_hi = [sb(f"lo_hi{i}", [128, N], F32R) for i in range(2)]
        rows = [sb(f"rows{i}", [128, NT, 2, F], F32R) for i in range(2)]
        r_ps = [pb(f"r_ps{i}", [128, NT, F]) for i in range(2)]
        hi_done, lo_done, turned, rows_hi, rows_done = (sem(n) for n in (
            "hi_done", "lo_done", "turned", "rows_hi", "rows_done"))
        out_d = [sem(f"out_d{i}") for i in range(2)]
        block = ctx.enter_context(nc.Block())

        @block.sync
        def _(sp):
            for b in range(B):
                p = b % 2
                sp.wait_ge(rows_done, b + 1)
                sp.dma_start(d["rows"][b], rows[p][:, :, :, :].bitcast(F32)).then_inc(out_d[p], 16)
                sp.wait_ge(lo_done, b + 1)
                sp.dma_start(d["hi_lo"][b], hi_lo[p][:, :].bitcast(F32)).then_inc(out_d[p], 16)
                sp.dma_start(d["lo_hi"][b], lo_hi[p][:, :].bitcast(F32)).then_inc(out_d[p], 16)
            for p in range(2):
                sp.wait_ge(out_d[p], 48 * (B // 2))

        @block.tensor
        def _(pe):
            for b in range(B):
                wait(pe, rows_done, b - 1)
                for t in range(NT):
                    last = pe.transpose(r_ps[b % 2][:, t, :], k.acc[:, N * b + 128 * t:N * b + 128 * t + 128], k.ident[0:64, 0:64])
                last.then_inc(turned, 1)

        @block.scalar
        def _(act):
            for b in range(B):
                p = b % 2
                mine = k.acc[:, N * b:N * b + N]
                wait(act, out_d[p], 48 * (b // 2))
                act.activation(hi_lo[p][0:64, :], mine, ACT.Copy).then_inc(hi_done, 1)
                act.activation(lo_hi[p][64:128, :], mine, ACT.Copy).then_inc(hi_done, 1)
                act.wait_ge(turned, b + 1)
                act.activation(rows[p][:, :, 0, :], r_ps[p][:, :, :], ACT.Copy).then_inc(rows_hi, 1)

        @block.vector
        def _(dve):
            for b in range(B):
                p = b % 2
                mine = k.acc[:, N * b:N * b + N]
                wait(dve, out_d[p], 48 * (b // 2))
                dve.wait_ge(rows_hi, b + 1)
                dve.tensor_tensor(rows[p][:, :, 1, :], r_ps[p][:, :, :], rows[p][:, :, 0, :].bitcast(F32),
                                  ALU.subtract).then_inc(rows_done, 1)
                dve.wait_ge(hi_done, 2 * b + 2)
                hi = hi_lo[p][0:64, :].bitcast(F32)
                dve.tensor_tensor(hi_lo[p][64:128, :], mine, hi, ALU.subtract)
                dve.tensor_tensor(lo_hi[p][0:64, :], mine, hi, ALU.subtract).then_inc(lo_done, 1)


def split_scores(nc, k, a, d):
    with ExitStack() as ctx:
        sb, pb, sem = sbuf(nc, ctx, "split_scores"), psum(nc, ctx, "split_scores"), semaphores(nc, ctx, "split_scores")
        a1_b = sb("a1_b", [128, F])
        product = sb("product", [128, B * NT, F])
        a2 = sb("a2", [F, 1])
        a2_b = sb("a2_b", [F, 128])
        xT = [sb(f"xT{i}", [F, N]) for i in range(2)]
        s2 = [sb(f"s2{i}", [128, N]) for i in range(2)]
        s1 = sb("s1", [128, B, NT])
        t_ps = [pb(f"t_ps{i}", [F, N]) for i in range(2)]
        s2_ps = [pb(f"s2_ps{i}", [128, N]) for i in range(2)]
        a_in, wide, turned, xT_done, s_f, s2_done, product_done, s1_done, s1_out = (sem(n) for n in (
            "a_in", "wide", "turned", "xT_done", "s_f", "s2_done", "product_done", "s1_done", "s1_out"))
        out_d = [sem(f"out_d{i}") for i in range(2)]
        block = ctx.enter_context(nc.Block())

        @block.sync
        def _(sp):
            sp.dma_start(a1_b[:, :], a[0:F, :].rearrange("f o -> o f").broadcast_to([128, F])).then_inc(a_in, 16)
            sp.dma_start(a2[:, :], a[F:2 * F, :]).then_inc(a_in, 16)
            for b in range(B):
                sp.wait_ge(s2_done, b + 1)
                sp.dma_start(d["s2"][b], s2[b % 2][:, :]).then_inc(out_d[b % 2], 16)
            sp.wait_ge(s1_done, 1)
            sp.dma_start(d["s1"].rearrange("b p t -> p b t"), s1[:, :, :]).then_inc(s1_out, 16)
            sp.wait_ge(s1_out, 16)
            for p in range(2):
                sp.wait_ge(out_d[p], 16 * (B // 2))

        @block.tensor
        def _(pe):
            pe.wait_ge(wide, 1)
            for n in range(B + 1):
                if n < B:
                    wait(pe, xT_done, n - 1)
                    for t in range(NT):
                        last = pe.transpose(t_ps[n % 2][:, 128 * t:128 * t + 128], k.x[:, NT * n + t, :], k.ident[:, :])
                    last.then_inc(turned, 1)
                b = n - 1
                if b >= 0:
                    pe.wait_ge(xT_done, b + 1)
                    wait(pe, s2_done, b - 1)
                    for c in range(2):
                        last = pe.matmul(s2_ps[b % 2][:, 512 * c:512 * c + 512], a2_b[:, :], xT[b % 2][:, 512 * c:512 * c + 512],
                                  start=True, stop=True)
                    last.then_inc(s_f, 1)

        @block.scalar
        def _(act):
            for b in range(B):
                act.wait_ge(turned, b + 1)
                wait(act, s_f, b - 1)
                act.activation(xT[b % 2][:, :], t_ps[b % 2][:, :], ACT.Copy).then_inc(xT_done, 1)

        @block.vector
        def _(dve):
            dve.wait_ge(a_in, 32)
            dve.tensor_copy(a2_b[:, :], a2[:, 0:1].broadcast_to([F, 128])).then_inc(wide, 1)
            dve.tensor_tensor(product[:, :, :], k.x[:, :, :], a1_b[:, :].unsqueeze(1).broadcast_to([128, B * NT, F]),
                              ALU.mult).then_inc(product_done, 1)
            dve.wait_ge(product_done, 1)
            dve.reduce_sum(s1[:, :, :].rearrange("p b t -> p (b t)"), product[:, :, :], axis=AX_X).then_inc(s1_done, 1)
            for b in range(B):
                dve.wait_ge(s_f, b + 1)
                wait(dve, out_d[b % 2], 16 * (b // 2))
                dve.tensor_copy(s2[b % 2][:, :], s2_ps[b % 2][:, :]).then_inc(s2_done, 1)


def attention(nc, k, stage, products, d, b_out=None):
    ITERS = B // 2
    J_ALL, C_ALL = B * 16, B * 2
    with ExitStack() as ctx:
        sb, pb, sem = sbuf(nc, ctx, stage), psum(nc, ctx, stage), semaphores(nc, ctx, stage)
        if products:
            ops = [[sb(f"{n}{i}", [128, N], F32R) for n in ("hi_lo", "lo_hi")] for i in range(2)]
            S_ps = [pb(f"S_ps{i}", [128, N]) for i in range(2)]
            bias = sb("bias", [128, F])
        else:
            s2 = [sb(f"s2_{i}", [128, N]) for i in range(2)]
            s1 = [sb(f"s1_{i}", [128, NT]) for i in range(2)]
            z = [sb(f"z{i}", [128, N]) for i in range(2)]
            leaky = [sb(f"leaky{i}", [128, N]) for i in range(2)]
        V_COLS, V_TYPE = (2 * F, F32R) if products else (F, F32)
        rows = [sb(f"rows{i}", [128, NT, V_COLS], V_TYPE) for i in range(2)]
        neg = [sb(f"neg{i}", [128, N]) for i in range(2)]
        nmax = sb("nmax", [128, 2, 1])
        P = [sb(f"P{i}", [128, 4, N]) for i in range(2)]
        den = [sb(f"den{i}", [128, 4]) for i in range(2)]
        rden = [sb(f"rden{i}", [128, 4]) for i in range(2)]
        PT = [sb(f"PT{i}", [128, 512], V_TYPE) for i in range(4)]
        if products:
            PT_lo = [sb(f"PT_lo{i}", [128, 512], F32R) for i in range(4)]
            two = sb("two", [128, F])
        att = [sb(f"att{i}", [V_COLS, 512]) for i in range(2)]
        o1 = [sb(f"o1{i}", [128, 4, F]) for i in range(2)]
        low = sb("low", [128, 4, F])
        elow = sb("elow", [128, 4, F])
        up = sb("up", [128, 4, F])
        DEEP = 1 if products else 2
        T_ps = [pb(f"T_ps{i}", [128, 512]) for i in range(2 * DEEP)]
        O_ps = [pb(f"O_ps{i}", [V_COLS, 512]) for i in range(DEEP)]
        F_ps = pb("F_ps", [128, 4, F])
        op_in = [sem(f"op_in{i}") for i in range(2)]
        pt_done = [sem(f"pt_done{i}") for i in range(2)]
        (bias_in, s_filled, s_taken, z_done, leaky_done, exp_done, turned, av_done, att_done, f_turned, r_ready, o1_done,
         low_done, elow_done, out_step, out_turn, max_turn, f_turn, x_done, pt_hi, two_done) = (sem(n) for n in (
            "bias_in", "s_filled", "s_taken", "z_done", "leaky_done", "exp_done", "turned", "av_done", "att_done",
            "f_turned", "r_ready", "o1_done", "low_done", "elow_done", "out_step", "out_turn", "max_turn", "f_turn", "x_done", "pt_hi", "two_done"))
        block = ctx.enter_context(nc.Block())

        def exists(i, n):
            return not isinstance(i, int) or 0 <= i < n

        def t_bank(s, a):
            return T_ps[2 * (s % DEEP) + a]

        def run(eng, slot):
            for s in range(16):
                slot(0, s)
            with eng.Fori(1, ITERS - 1) as it:
                for s in range(16):
                    slot(it, s)
            for s in range(16):
                slot(ITERS - 1, s)
            for s in range(9):
                slot(ITERS, s)

        @block.sync
        def _(sp):
            def load(b, par):
                wait(sp, av_done, 16 * (b - 1))
                if products:
                    for n, name in enumerate(("hi_lo", "lo_hi")):
                        sp.dma_start(ops[par][n][:, :].bitcast(F32), one(d[name][bass.ds(b, 1)])).then_inc(op_in[par], 16)
                    sp.dma_start(rows[par][:, :, :].rearrange("p t c -> p (t c)").bitcast(F32),
                                 d["rows"][bass.ds(b, 1)].rearrange("o p t a c -> (o p) (t a c)")).then_inc(op_in[par], 16)
                else:
                    sp.dma_start(s2[par][:, :], one(d["s2"][bass.ds(b, 1)])).then_inc(op_in[par], 16)
                    sp.dma_start(s1[par][:, :], one(d["s1"][bass.ds(b, 1)])).then_inc(op_in[par], 16)
                    sp.dma_start(rows[par][:, :, :],
                                 d["x"][bass.ds(b, 1)].rearrange("o (t p) c -> (o p) t c", p=128)).then_inc(op_in[par], 16)

            if products:
                sp.dma_start(bias[:, :], b_out.rearrange("(o f) -> o f", o=1).broadcast_to([128, F])).then_inc(bias_in, 16)
            load(0, 0)
            load(1, 1)
            with sp.Fori(1, ITERS) as it:
                load(2 * it, 0)
                load(2 * it + 1, 1)

        @block.tensor
        def _(pe):
            def slot(it, s):
                G = 16 * it + s
                hp, i = s // 8, s % 8
                if exists(G, 8 * B):
                    if i == 0:
                        pe.wait_ge(op_in[hp], 48 * it + 48)
                    if products:
                        wait(pe, s_taken, G - 1)
                        tile = slice(128 * i, 128 * i + 128)
                        for n in range(2):
                            for c in range(2):
                                ch = slice(512 * c, 512 * c + 512)
                                last = pe.matmul(S_ps[i % 2][:, ch], ops[hp][0][:, tile], ops[hp][n][:, ch], start=(n == 0),
                                                 stop=(n == 1))
                        last.then_inc(s_filled, 1)
                for a in range(2):
                    J = 32 * it + (2 * s - 10 + a)
                    j = (2 * s - 10 + a) % 8
                    if exists(J, J_ALL):
                        if j == 0:
                            wait(pe, exp_done, 16 * it + 4 * ((2 * s - 10 + a) // 8) + 4)
                        wait(pe, pt_done[a], 16 * it + (s - 4 - DEEP))
                        for q in range(4):
                            last = pe.transpose(t_bank(s, a)[:, 128 * q:128 * q + 128],
                                                P[((2 * s - 10 + a) // 8) % 2][:, q, 128 * j:128 * j + 128], k.ident[:, :])
                        last.then_inc(turned, 1)
                    V = 32 * it + (2 * s - 12 + a)
                    v = (2 * s - 12 + a) % 8
                    if exists(V, J_ALL):
                        hpar = ((2 * s - 12 + a) // 16) % 2
                        wait(pe, pt_done[a], 16 * it + (2 * s - 12) // 2 + 1)
                        if v == 0:
                            wait(pe, att_done, 4 * it + (2 * s - 12) // 8 - (DEEP - 1))
                        parts = [PT, PT_lo] if products else [PT]
                        for part in parts:
                            last = pe.matmul(O_ps[((2 * s - 12) // 8) % DEEP][:, :], rows[hpar][:, v, :], part[v % 4][:, :],
                                             start=(v == 0 and part is parts[0]), stop=(v == 7 and part is parts[-1]))
                        last.then_inc(av_done, 1)
                if s % 4 == 2:
                    C = 4 * it + (s - 10) // 4
                    if exists(C, C_ALL):
                        wait(pe, att_done, C + 1)
                        wait(pe, o1_done, C)
                        pe.sem_inc(f_turn, 1)
                        for q in range(4):
                            turn = att[((s - 10) // 4) % 2][:, 128 * q:128 * q + 128]
                            if products:
                                last = pe.matmul(F_ps[:, q, :], turn, two[:, :], start=True, stop=True)
                            else:
                                last = pe.transpose(F_ps[:, q, :], turn, k.ident[0:64, 0:64])
                        last.then_inc(f_turned, 1)

            if products:
                pe.wait_ge(two_done, 2)
            run(pe, slot)

        @block.scalar
        def _(act):
            def take(it, s, a):
                J = 32 * it + (2 * s - 10 + a)
                if exists(J, J_ALL):
                    act.wait_ge(turned, J + 1)
                    wait(act, av_done, J - 3)
                    act.activation(PT[(2 * s - 10 + a) % 4][:, :], t_bank(s, a)[:, :], ACT.Copy).then_inc(
                        pt_hi if products else pt_done[a], 1)

            def scores(it, s):
                G = 16 * it + s
                hp, i = (s // 8) % 2, s % 8
                if exists(G, 8 * B):
                    if i == 0:
                        act.wait_ge(op_in[hp], 48 * (it + s // 16) + 48)
                    wait(act, leaky_done, G - 1)
                    act.activation(z[i % 2][:, :], s2[hp][:, :], ACT.Identity, bias=s1[hp][:, i:i + 1]).then_inc(z_done, 1)

            if not products:
                scores(0, 0)

            def slot(it, s):
                G = 16 * it + s
                hp, i = s // 8, s % 8
                if s % 4 == 2 and not products:
                    C = 4 * it + (s - 10) // 4
                    if exists(C, C_ALL):
                        act.wait_ge(av_done, 8 * C + 8)
                        wait(act, f_turned, C - 1)
                        act.activation(att[((s - 10) // 4) % 2][:, :], O_ps[((s - 10) // 4) % DEEP][:, :], ACT.Copy).then_inc(att_done, 1)
                take(it, s, 0)
                if products:
                    take(it, s, 1)
                else:
                    scores(it, s + 1)
                if exists(G, 8 * B):
                    act.wait_ge(s_taken, G + 1)
                    if i % 4 == 0:
                        wait(act, turned, 32 * it + 8 * (s // 4 - 1))
                    act.activation(P[(s // 4) % 2][:, i % 4, :], neg[i % 2][:, :], ACT.Exp, bias=nmax[:, i % 2, :], scale=-1.0,
                                   accum_out=den[(s // 4) % 2][:, i % 4:i % 4 + 1]).then_inc(exp_done, 1)
                if s % 4 == 0 and not products:
                    C = 4 * it + (s - 12) // 4
                    if exists(C, C_ALL):
                        act.wait_ge(low_done, C + 1)
                        act.activation(elow[:, :, :], low[:, :, :], ACT.Exp).then_inc(elow_done, 1)

            run(act, slot)

        @block.gpsimd
        def _(pool):
            if products:
                pool.wait_ge(bias_in, 16)

            def slot(it, s):
                if s % 4 == 3:
                    C = 4 * it + (s - 11) // 4
                    if exists(C, C_ALL):
                        o = o1[((s - 11) // 4) % 2]
                        xs = k.x[:, bass.ds(4 * C, 4), :]
                        pool.wait_ge(o1_done, C + 1)
                        if products:
                            pool.sem_inc(out_turn, 1)
                            pool.tensor_tensor(low[:, :, :], o[:, :, :], bias[:, :].unsqueeze(1).broadcast_to([128, 4, F]),
                                               ALU.add).then_inc(out_step, 1)
                            pool.wait_ge(out_step, 3 * C + 1)
                            pool.sem_inc(out_turn, 1)
                            pool.tensor_scalar(up[:, :, :], low[:, :, :], 0.0, 0.99, ALU.max, ALU.mult)
                            pool.tensor_scalar(elow[:, :, :], low[:, :, :], 0.01, 1.0, ALU.mult, ALU.mult).then_inc(out_step, 1)
                            pool.wait_ge(out_step, 3 * C + 2)
                        else:
                            wait(pool, elow_done, C)
                            pool.sem_inc(out_turn, 1)
                            pool.tensor_scalar(low[:, :, :], o[:, :, :], 0.0, 0.0, ALU.min, ALU.add).then_inc(low_done, 1)
                            pool.tensor_scalar(up[:, :, :], o[:, :, :], 0.0, -1.0, ALU.max, ALU.add).then_inc(out_step, 1)
                            pool.wait_ge(out_step, 2 * C + 1)
                            pool.wait_ge(elow_done, C + 1)
                        pool.sem_inc(out_turn, 1)
                        pool.tensor_tensor(up[:, :, :], up[:, :, :], elow[:, :, :], ALU.add).then_inc(out_step, 1)
                        pool.wait_ge(out_step, (3 if products else 2) * (C + 1))
                        pool.sem_inc(out_turn, 1)
                        pool.tensor_tensor(xs, xs, up[:, :, :], ALU.add).then_inc(x_done, 1)
                        pool.wait_ge(x_done, C + 1)

            run(pool, slot)

        @block.vector
        def _(dve):
            if products:
                for half in (slice(0, 64), slice(64, 128)):
                    dve.tensor_copy(two[half, :], k.ident[half, half]).then_inc(two_done, 1)

            def slot(it, s):
                G = 16 * it + s
                i = s % 8
                if exists(G, 8 * B):
                    if not products:
                        dve.wait_ge(z_done, G + 1)
                        wait(dve, s_taken, G - 1)
                        dve.scalar_tensor_tensor(out=leaky[i % 2][:, :], in0=z[i % 2][:, :], scalar=0.2, in1=z[i % 2][:, :],
                                                 op0=ALU.mult, op1=ALU.max).then_inc(leaky_done, 1)
                J = 32 * it + (2 * s - 10 + 1)
                if exists(J, J_ALL) and not products:
                    dve.wait_ge(turned, J + 1)
                    wait(dve, av_done, J - 3)
                    dve.tensor_copy(PT[(2 * s - 10 + 1) % 4][:, :], t_bank(s, 1)[:, :]).then_inc(pt_done[1], 1)
                if exists(G, 8 * B):
                    wait(dve, exp_done, G - 1)
                    dve.wait_ge(s_filled if products else leaky_done, G + 1)
                    dve.sem_inc(max_turn, 1)
                    dve.tensor_tensor_reduce(neg[i % 2][:, :], S_ps[i % 2][:, :] if products else leaky[i % 2][:, :],
                                             k.mask[:, i, :], -1.0, 3.0e38, ALU.add, ALU.min, nmax[:, i % 2, :]).then_inc(s_taken, 1)
                for a in range(2):
                    J = 32 * it + (2 * s - 10 + a)
                    n = (2 * s - 10 + a) % 4
                    if exists(J, J_ALL) and products:
                        dve.wait_ge(pt_hi, J + 1)
                        dve.tensor_tensor(PT_lo[n][:, :], t_bank(s, a)[:, :], PT[n][:, :].bitcast(F32),
                                          ALU.subtract).then_inc(pt_done[a], 1)
                if s % 4 == 1:
                    C = 4 * it + (s - 5) // 4
                    if exists(C, C_ALL):
                        wait(dve, exp_done, 4 * C + 4)
                        wait(dve, o1_done, C - 1)
                        dve.reciprocal(rden[((s - 5) // 4) % 2][:, :], den[((s - 5) // 4) % 2][:, :]).then_inc(r_ready, 1)
                    C = 4 * it + (s - 9) // 4
                    if exists(C, C_ALL) and products:
                        dve.wait_ge(av_done, 8 * C + 8)
                        wait(dve, f_turned, C - 1)
                        dve.tensor_copy(att[((s - 9) // 4) % 2][:, :], O_ps[0][:, :]).then_inc(att_done, 1)
                if s % 4 == 3:
                    C = 4 * it + (s - 11) // 4
                    if exists(C, C_ALL):
                        q = ((s - 11) // 4) % 2
                        dve.wait_ge(f_turned, C + 1)
                        dve.wait_ge(r_ready, C + 1)
                        wait(dve, x_done, C - 1)
                        dve.tensor_tensor(o1[q][:, :, :], F_ps[:, :, :], rden[q][:, :].unsqueeze(2).broadcast_to([128, 4, F]),
                                          ALU.mult).then_inc(o1_done, 1)

            run(dve, slot)


def causal(nc, k, w):
    PAIRS = B // 2
    STEPS = 3
    R = STEPS * PAIRS
    with ExitStack() as ctx:
        sb, pb, sem = sbuf(nc, ctx, "causal"), psum(nc, ctx, "causal"), semaphores(nc, ctx, "causal")
        w1v, w1e, w2 = (sb(n, [128, 128]) for n in ("w1v", "w1e", "w2"))
        b1 = sb("b1", [128, 1])
        b2 = sb("b2", [128, 1])
        b2_b = sb("b2_b", [128, 128])
        given = sb("given", [1, F])
        v = sb("v", [128, NT, B, F])
        v_hi = sb("v_hi", [128, NT, B, F], F32R)
        v_lo = sb("v_lo", [128, NT, B, F], F32R)
        vT = [sb(f"vT{p}", [128, N]) for p in range(PAIRS)]
        eff = [sb(f"eff{i}", [128, N]) for i in range(2)]
        h = [sb(f"h{i}", [128, N]) for i in range(2)]
        e_ps = [pb(f"e_ps{i}", [128, N]) for i in range(2)]
        h_ps = pb("h_ps", [128, N])
        v_ps = pb("v_ps", [128, N])
        (zeroed, w_in, given_in, v_copied, given_set, v_hi_done, v_lo_done, vT_turned, vT_taken, e_f, e_done, h_f, h_done, vT_f,
         vT_done, v_f, v_done, x_done) = (sem(n) for n in (
            "zeroed", "w_in", "given_in", "v_copied", "given_set", "v_hi_done", "v_lo_done", "vT_turned", "vT_taken", "e_f",
            "e_done", "h_f", "h_done", "vT_f", "vT_done", "v_f", "v_done", "x_done"))
        block = ctx.enter_context(nc.Block())

        def of_pair(t, p):
            return t[:, :, 2 * p:2 * p + 2, :]

        @block.sync
        def _(sp):
            sp.dma_start(given[:, :], w["intervention"]).then_inc(given_in, 16)
            for half in range(2):
                s = slice(64 * half, 64 * half + 64)
                sp.dma_start(b1[s, :], w["b1"].rearrange("(p o) -> p o", o=1)).then_inc(w_in, 16)
                sp.dma_start(b2[s, :], w["b2"].rearrange("(p o) -> p o", o=1)).then_inc(w_in, 16)
                sp.dma_start(b2_b[:, s], w["b2"].rearrange("(o f) -> o f", o=1).broadcast_to([128, F])).then_inc(w_in, 16)
            sp.wait_ge(zeroed, 3)
            for half in range(2):
                s = slice(64 * half, 64 * half + 64)
                sp.dma_start(w1v[s, s], w["W1T"][0:F, :]).then_inc(w_in, 16)
                sp.dma_start(w1e[s, s], w["W1T"][F:2 * F, :]).then_inc(w_in, 16)
                sp.dma_start(w2[s, s], w["W2T"]).then_inc(w_in, 16)

        @block.gpsimd
        def _(pool):
            for t in (w1v, w1e, w2):
                pool.memset(t[:, :], 0.0).then_inc(zeroed, 1)
            for p in range(PAIRS):
                q = R - PAIRS + p
                pool.wait_ge(v_done, q + 1)
                for b in (2 * p, 2 * p + 1):
                    xb = k.x[:, NT * b:NT * b + NT, :]
                    pool.tensor_tensor(xb, xb, v[:, :, b, :], ALU.add).then_inc(x_done, 1)

        @block.tensor
        def _(pe):
            for p in range(PAIRS):
                pe.wait_ge(given_set, 1)
                for t in range(NT):
                    last = pe.transpose((e_ps[p % 2] if p < 2 else (h_ps, v_ps)[p % 2])[:, 128 * t:128 * t + 128],
                                        of_pair(v, p)[:, t].rearrange("p b c -> p (b c)"), k.ident[:, :])
                last.then_inc(vT_turned, 1)
            pe.wait_ge(w_in, 16 * 12)
            pe.wait_ge(vT_taken, PAIRS)
            for n in range(R + 2):
                if n < R:
                    p = n % PAIRS
                    pe.wait_ge(v_hi_done, n + 1)
                    pe.wait_ge(v_lo_done, n + 1)
                    wait(pe, e_done, n - 1)
                    for t in range(NT):
                        for m, part in enumerate((v_hi, v_lo)):
                            for c in range(2):
                                last = pe.matmul(e_ps[n % 2][:, 512 * c:512 * c + 512],
                                                 of_pair(part, p)[:, t].rearrange("p b c -> p (b c)"),
                                                 k.adjT[:, t, 512 * c:512 * c + 512], start=(t == 0 and m == 0),
                                                 stop=(t == NT - 1 and m == 1))
                    last.then_inc(e_f, 1)
                q = n - 1
                if 0 <= q < R:
                    pe.wait_ge(e_done, q + 1)
                    wait(pe, h_done, q)
                    wait(pe, vT_done, q - PAIRS + 1)
                    for m in range(2):
                        for c in range(2):
                            ch = slice(512 * c, 512 * c + 512)
                            last = pe.matmul(h_ps[:, ch], (w1v, w1e)[m][:, :], (vT[q % PAIRS], eff[q % 2])[m][:, ch],
                                             start=(m == 0), stop=(m == 1))
                    last.then_inc(h_f, 1)
                q = n - 2
                if 0 <= q < R:
                    pe.wait_ge(h_done, q + 1)
                    wait(pe, v_done, q)
                    if q < R - PAIRS:
                        for c in range(2):
                            ch = slice(512 * c, 512 * c + 512)
                            last = pe.matmul(v_ps[:, ch], w2[:, :], h[q % 2][:, ch], start=True, stop=True)
                        last.then_inc(vT_f, 1)
                        pe.wait_ge(vT_done, q + 1)
                    for t in range(NT):
                        last = pe.matmul(v_ps[:, 128 * t:128 * t + 128], h[q % 2][:, 128 * t:128 * t + 128], w2[:, :],
                                         start=True, stop=True)
                    last.then_inc(v_f, 1)

        @block.scalar
        def _(act):
            act.wait_ge(given_set, 1)
            for p in range(PAIRS):
                act.activation(of_pair(v_hi, p), of_pair(v, p), ACT.Copy).then_inc(v_hi_done, 1)
            act.wait_ge(w_in, 16 * 12)
            for n in range(R + 2):
                if n < R:
                    act.wait_ge(e_f, n + 1)
                    wait(act, h_f, n - 1)
                    act.activation(eff[n % 2][:, :], e_ps[n % 2][:, :], ACT.Copy).then_inc(e_done, 1)
                q = n - 1
                if 0 <= q < R:
                    act.wait_ge(h_f, q + 1)
                    wait(act, v_f, q - 1)
                    act.activation(h[q % 2][:, :], h_ps[:, :], ACT.Relu, bias=b1[:, 0:1]).then_inc(h_done, 1)
                q = n - 2
                if 0 <= q < R - PAIRS:
                    act.wait_ge(vT_f, q + 1)
                    act.activation(vT[q % PAIRS][:, :], v_ps[:, :], ACT.Identity, bias=b2[:, 0:1]).then_inc(vT_done, 1)
                    act.wait_ge(v_done, q + 1)
                    act.activation(of_pair(v_hi, q % PAIRS), of_pair(v, q % PAIRS), ACT.Copy).then_inc(v_hi_done, 1)

        @block.vector
        def _(dve):
            dve.tensor_copy(v[:, :, :, :].rearrange("p t b c -> p b t c"),
                            k.x[:, :, :].rearrange("p (b t) c -> p b t c", b=B)).then_inc(v_copied, 1)
            dve.wait_ge(v_copied, 1)
            dve.wait_ge(given_in, 16)
            dve.tensor_copy(v[0:1, 0, :, :], given[:, :].unsqueeze(1).broadcast_to([1, B, F])).then_inc(given_set, 1)
            for p in range(PAIRS):
                dve.wait_ge(v_hi_done, p + 1)
                dve.wait_ge(given_set, 1)
                dve.tensor_tensor(of_pair(v_lo, p), of_pair(v, p), of_pair(v_hi, p).bitcast(F32), ALU.subtract).then_inc(v_lo_done, 1)
            for p in range(PAIRS):
                dve.wait_ge(vT_turned, p + 1)
                dve.tensor_copy(vT[p][:, :], (e_ps[p % 2] if p < 2 else (h_ps, v_ps)[p % 2])[:, :]).then_inc(vT_taken, 1)
            dve.wait_ge(w_in, 16 * 12)
            for q in range(R):
                dve.wait_ge(v_f, q + 1)
                dve.tensor_tensor(of_pair(v, q % PAIRS), v_ps[:, :].rearrange("p (t b c) -> p t b c", t=NT, b=2),
                                  b2_b[:, :].rearrange("p (b c) -> p b c", b=2).unsqueeze(1).broadcast_to([128, NT, 2, F]),
                                  ALU.add).then_inc(v_done, 1)
                if q < R - PAIRS:
                    dve.wait_ge(v_hi_done, PAIRS + q + 1)
                    dve.tensor_tensor(of_pair(v_lo, q % PAIRS), of_pair(v, q % PAIRS), of_pair(v_hi, q % PAIRS).bitcast(F32),
                                      ALU.subtract).then_inc(v_lo_done, 1)


def program(nc, a, out):
    with ExitStack() as ctx:
        sb = sbuf(nc, ctx, "program")
        k = Shared()
        k.ident = sb("ident", [128, 128])
        k.x = sb("x", [128, B * NT, F])
        k.mask = sb("mask", [128, NT, N], BF16)
        k.adjT = sb("adjT", [128, NT, N], F32R)

        def scratch(name, shape):
            return nc.dram_tensor(name, shape, F32, kind="Internal").ap()

        d = {"hT": scratch("hT_d", [B, 128, N]), "beta": scratch("beta_d", [B, 128, N]), "coef": scratch("coef_d", [B, 128, N]),
             "agg": scratch("agg_d", [B, 128, 3, EDGES // 2]), "g": scratch("g_d", [B, F, N]), "ind": scratch("ind_d", [B, F, N])}
        w = {"W": a["L0_gnn_W"], "a_node": a["L0_gnn_a_node"], "a_gn": a["L0_gnn_a_gn"], "a_ge": a["L0_gnn_a_ge"],
             "fcW": a["L0_gnn_fcW"], "fcb": a["L0_gnn_fcb"], "av": a["L0_gnn_av"]}
        with ExitStack() as hyper:
            sb = sbuf(nc, hyper, "hypergraph")
            k.two = sb("two", [128, 64])
            k.mask_ne = sb("mask_ne", [128, NT, EDGES], BF16)
            k.mask_en = sb("mask_en", [EDGES, N], BF16)
            setup(nc, k, a["adj"], a["L0_gnn_H"], a["HT"])
            industry(nc, k, a["x"], a["xT"], a["L0_gnn_W_ind"], d["ind"])
            hyperedges(nc, k, a["xT"], w, d)
            messages(nc, k, d)
            mix(nc, k, w, d)
        layernorm(nc, k, "norm0", None)

        with ExitStack() as graph:
            k.acc = graph.enter_context(nc.sbuf_tensor("acc", [F, B * N], F32))
            d["x_cols"], d["x_rows"] = scratch("x_cols_d", [B, F, 2, N]), scratch("x_rows_d", [B, 128, NT, 2, F])
            d["g_heads"], d["bias"] = scratch("g_heads_d", [HEADS, 128, 2 * F]), scratch("bias_d", [HEADS, 128, 2])
            d["rows"], d["hi_lo"], d["lo_hi"] = scratch("rows_d", [B, 128, NT, 2, F]), scratch("hi_lo_d", [B, 128, N]), scratch("lo_hi_d", [B, 128, N])
            split_heads(nc, k, a["WhT"], a["bhT"], d)
            heads(nc, k, d, a["L1_gnn_Wh"], a["L1_gnn_W_out"].rearrange("(h d) f -> h d f", h=HEADS))
            split_output(nc, k, d)
            attention(nc, k, "output_layer", True, d, a["L1_gnn_b_out"])
        x_d = scratch("x_d", [B, N, F])
        layernorm(nc, k, "norm1", x_d)

        d["x"], d["s2"], d["s1"] = x_d, scratch("s2_d", [B, 128, N]), scratch("s1_d", [B, 128, NT])
        split_scores(nc, k, a["L2_gnn_a"], d)
        attention(nc, k, "threshold_layer", False, d)
        layernorm(nc, k, "norm2", None)

        causal(nc, k, {"intervention": a["L3_gnn_intervention_value"], "W1T": a["W1T"], "W2T": a["W2T"],
                       "b1": a["L3_gnn_b1"], "b2": a["L3_gnn_b2"]})
        layernorm(nc, k, "norm3", out)


_INS = ['x', 'adj', 'L0_gnn_H', 'L0_gnn_W', 'L0_gnn_W_ind', 'L0_gnn_a_node', 'L0_gnn_a_gn', 'L0_gnn_a_ge', 'L0_gnn_fcW', 'L0_gnn_fcb',
        'L0_gnn_av', 'L1_gnn_Wh', 'L1_gnn_bh', 'L1_gnn_W_out', 'L1_gnn_b_out', 'L2_gnn_a', 'L3_gnn_intervention_value',
        'L3_gnn_W1', 'L3_gnn_b1', 'L3_gnn_W2', 'L3_gnn_b2']


def kernel(**inputs):
    import numpy as _np
    import concourse.bacc as _bacc
    from concourse import mybir as _mybir
    from concourse.bass_utils import run_bass_kernel_spmd as _run

    given = {name: _np.asarray(inputs[name]) for name in _INS}
    given["xT"] = given["x"].transpose(0, 2, 1)
    given["HT"] = given["L0_gnn_H"].T
    given["WhT"] = given["L1_gnn_Wh"].transpose(0, 2, 1)
    given["bhT"] = given.pop("L1_gnn_bh").T
    given["W1T"] = given.pop("L3_gnn_W1").T
    given["W2T"] = given.pop("L3_gnn_W2").T
    nc = _bacc.Bacc("TRN2", target_bir_lowering=False, num_devices=1)
    arrays, args = {}, {}
    for name, v in given.items():
        v = _np.ascontiguousarray(v)
        arrays[f"in_{name}_dram"] = v
        args[name] = nc.dram_tensor(f"in_{name}_dram", v.shape, _mybir.dt.from_np(v.dtype), kind="ExternalInput").ap()
    out = nc.dram_tensor("out_0_dram", (B, N, F), _mybir.dt.float32, kind="ExternalOutput").ap()
    program(nc, args, out)
    r = _run(nc, [arrays], core_ids=[0])
    return r.results[0]["out_0_dram"]
```
